# Optimizing a Trainium2 kernel written in Bass

```python
import numpy as np
import jax
import jax.numpy as jnp

def _softmax(x, axis=-1):
    return jax.nn.softmax(x, axis=axis)

def _gelu(x):
    return jax.nn.gelu(x, approximate=True)

def _silu(x):
    return jax.nn.silu(x)

def _sigmoid(x):
    return jax.nn.sigmoid(x)

def _layernorm(x, axis=-1, eps=1e-05):
    m = jnp.mean(x, axis=axis, keepdims=True)
    v = jnp.var(x, axis=axis, keepdims=True)
    return (x - m) / jnp.sqrt(v + eps)

def _scatter_add(tgt, idx, src, axis=0):
    return tgt.at[idx].add(src)

def _segment_sum(src, seg, n):
    return jax.ops.segment_sum(src, seg, n)
kernel_name = 'mk_recurrent_d2_jaxref_r8_7d2e1e'

def setup_inputs(seed: int=0):
    np.random.seed(seed)
    _w = jnp.asarray

    def _L0_attn_setup():
        import jax, jax.numpy as jnp
        import numpy as np
        B_, L_, DM, DS, DFF = (2, 128, 128, 16, 512)
        DI = 2 * DM
        DTR = (DM + 15) // 16
        K = 4

        def _rmsnorm(x, w, eps=1e-06):
            return x * jax.lax.rsqrt(jnp.mean(x * x, axis=-1, keepdims=True) + eps) * w

        def _causal_dw_conv(x, w, b):
            xp = jnp.pad(x, ((0, 0), (K - 1, 0), (0, 0)))
            out = jax.lax.conv_general_dilated(xp.transpose(0, 2, 1), w[:, None, :], window_strides=(1,), padding='VALID', dimension_numbers=('NCL', 'OIL', 'NCL'), feature_group_count=x.shape[-1])
            return out.transpose(0, 2, 1) + b

        def _mamba(Z, in_proj_w, conv_w, conv_b, x_proj_w, dt_proj_w, dt_proj_b, A_log, D, out_proj_w):
            xz = jnp.einsum('bld,ed->ble', Z, in_proj_w)
            x, z = jnp.split(xz, 2, axis=-1)
            x = jax.nn.silu(_causal_dw_conv(x, conv_w, conv_b))
            x_dbl = jnp.einsum('bld,ed->ble', x, x_proj_w)
            dt, Bm, Cm = jnp.split(x_dbl, [DTR, DTR + DS], axis=-1)
            dt = jax.nn.softplus(jnp.einsum('blr,dr->bld', dt, dt_proj_w) + dt_proj_b)
            A = -jnp.exp(A_log)
            deltaA = jnp.exp(dt[..., None] * A)
            deltaBx = dt[..., None] * Bm[:, :, None, :] * x[..., None]

            def step(h, xs):
                dA, dBx, C = xs
                h = dA * h + dBx
                y = jnp.einsum('bdn,bn->bd', h, C)
                return (h, y)
            h0 = jnp.zeros((Z.shape[0], DI, DS), Z.dtype)
            xs = (deltaA.transpose(1, 0, 2, 3), deltaBx.transpose(1, 0, 2, 3), Cm.transpose(1, 0, 2))
            _, ys = jax.lax.scan(step, h0, xs)
            y = ys.transpose(1, 0, 2) + x * D
            y = y * jax.nn.silu(z)
            return jnp.einsum('bld,ed->ble', y, out_proj_w)
        key = jax.random.key(seed)
        ks = jax.random.split(key, 12)
        r = lambda k, s: jax.random.normal(k, s, dtype=jnp.float32) * 0.02
        return {'Z': jax.random.normal(ks[0], (B_, L_, DM), dtype=jnp.float32), 'in_proj_w': r(ks[1], (2 * DI, DM)), 'conv_w': r(ks[2], (DI, K)), 'conv_b': jnp.zeros((DI,), jnp.float32), 'x_proj_w': r(ks[3], (DTR + 2 * DS, DI)), 'dt_proj_w': r(ks[4], (DI, DTR)), 'dt_proj_b': jax.random.uniform(ks[5], (DI,), jnp.float32, -4.0, -2.0), 'A_log': jnp.log(jnp.tile(jnp.arange(1, DS + 1, dtype=jnp.float32), (DI, 1))), 'D': jnp.ones((DI,), jnp.float32), 'out_proj_w': r(ks[6], (DM, DI)), 'mlp_w1': r(ks[7], (DFF, DM)), 'mlp_b1': jnp.zeros((DFF,), jnp.float32), 'mlp_w2': r(ks[8], (DM, DFF)), 'mlp_b2': jnp.zeros((DM,), jnp.float32), 'norm1_w': jnp.ones((DM,), jnp.float32)}
    _L0_attn_in = _L0_attn_setup()

    def _L0_ffn_setup():
        import math
        import jax, jax.numpy as jnp
        import numpy as np
        E = 24

        def layer_norm(x, w, b, eps=1e-06):
            m = x.mean(-1, keepdims=True)
            v = x.var(-1, keepdims=True)
            return (x - m) / jnp.sqrt(v + eps) * w + b

        def top2_dispatch(x, Wg, C):
            logits = x @ Wg
            gates = jax.nn.softmax(logits, axis=-1)
            idx1 = jnp.argmax(gates, axis=-1)
            m1 = jax.nn.one_hot(idx1, E, dtype=x.dtype)
            masked = jnp.where(m1 > 0, -jnp.inf, logits)
            idx2 = jnp.argmax(masked, axis=-1)
            m2 = jax.nn.one_hot(idx2, E, dtype=x.dtype)
            loc1 = jnp.cumsum(m1, axis=0) - m1
            loc2 = jnp.cumsum(m2, axis=0) - m2 + jnp.sum(m1, axis=0, keepdims=True)
            m1 = m1 * (loc1 < C)
            m2 = m2 * (loc2 < C)
            g1 = jnp.sum(gates * m1, axis=-1)
            g2 = jnp.sum(gates * m2, axis=-1)
            denom = jnp.maximum(g1 + g2, 1e-09)
            g1, g2 = (g1 / denom, g2 / denom)
            p1 = jnp.sum(loc1 * m1, axis=-1).astype(jnp.int32)
            p2 = jnp.sum(loc2 * m2, axis=-1).astype(jnp.int32)
            c1 = g1[:, None, None] * m1[:, :, None] * jax.nn.one_hot(p1, C, dtype=x.dtype)[:, None, :]
            c2 = g2[:, None, None] * m2[:, :, None] * jax.nn.one_hot(p2, C, dtype=x.dtype)[:, None, :]
            combine = c1 + c2
            dispatch = (combine > 0).astype(x.dtype)
            return (combine, dispatch)

        def moe_apply(x, combine, dispatch, W, b):
            disp = jnp.einsum('sec,sd->ecd', dispatch, x)
            h = jnp.einsum('ecd,edf->ecf', disp, W) + b[:, None, :]
            return jnp.einsum('sec,ecf->sf', combine, h)
        b, seq, d_in, d_hid = (4, 256, 128, 512)
        ks = jax.random.split(jax.random.key(seed), 6)
        s = 0.02
        return {'x': jax.random.normal(ks[0], (b, seq, d_in), dtype=jnp.float32), 'Wg': jax.random.normal(ks[1], (d_in, E), dtype=jnp.float32) * s, 'W1': jax.random.normal(ks[2], (E, d_in, d_hid), dtype=jnp.float32) * s, 'b1': jnp.zeros((E, d_hid), dtype=jnp.float32), 'W2': jax.random.normal(ks[3], (E, d_hid, d_in), dtype=jnp.float32) * s, 'b2': jnp.zeros((E, d_in), dtype=jnp.float32), 'ln_hid_w': jnp.ones((4, d_hid), dtype=jnp.float32), 'ln_hid_b': jnp.zeros((4, d_hid), dtype=jnp.float32), 'ln_out_w': jnp.ones((d_in,), dtype=jnp.float32), 'ln_out_b': jnp.zeros((d_in,), dtype=jnp.float32)}
    _L0_ffn_in = _L0_ffn_setup()

    def _L1_attn_setup():
        import jax, jax.numpy as jnp
        import numpy as np
        DIM = 128
        DIM_HEAD = 128
        HEADS = 8
        DIM_INNER = DIM_HEAD * HEADS
        key = jax.random.key(seed)
        k_x, k_qkv, k_out = jax.random.split(key, 3)
        x = jax.random.normal(k_x, (2, 256, DIM), dtype=jnp.float32)
        gamma = jnp.ones((DIM,), dtype=jnp.float32)
        w_qkv = jax.random.uniform(k_qkv, (DIM_INNER * 3, DIM), dtype=jnp.float32, minval=-1.0, maxval=1.0) / np.sqrt(DIM)
        w_out = jax.random.uniform(k_out, (DIM, DIM_INNER), dtype=jnp.float32, minval=-1.0, maxval=1.0) / np.sqrt(DIM_INNER)
        return {'x': x, 'gamma': gamma, 'w_qkv': w_qkv, 'w_out': w_out}
    _L1_attn_in = _L1_attn_setup()

    def _L1_ffn_setup():
        import jax, jax.numpy as jnp
        import numpy as np
        E = 128
        D = 128
        C = 32
        key = jax.random.key(seed)
        kx, kg, ke = jax.random.split(key, 3)
        x = jax.random.normal(kx, (4, 256, D), dtype=jnp.float32)
        wg = jax.random.normal(kg, (D, E), dtype=jnp.float32) * 0.02
        we = jax.random.normal(ke, (E, D, D), dtype=jnp.float32) * 0.02
        return {'x': x, 'wg': wg, 'we': we}
    _L1_ffn_in = _L1_ffn_setup()
    _d = {'L0_attn_Z': _L0_attn_in['Z'], 'L0_attn_in_proj_w': _L0_attn_in['in_proj_w'], 'L0_attn_conv_w': _L0_attn_in['conv_w'], 'L0_attn_conv_b': _L0_attn_in['conv_b'], 'L0_attn_x_proj_w': _L0_attn_in['x_proj_w'], 'L0_attn_dt_proj_w': _L0_attn_in['dt_proj_w'], 'L0_attn_dt_proj_b': _L0_attn_in['dt_proj_b'], 'L0_attn_A_log': _L0_attn_in['A_log'], 'L0_attn_D': _L0_attn_in['D'], 'L0_attn_out_proj_w': _L0_attn_in['out_proj_w'], 'L0_attn_mlp_w1': _L0_attn_in['mlp_w1'], 'L0_attn_mlp_b1': _L0_attn_in['mlp_b1'], 'L0_attn_mlp_w2': _L0_attn_in['mlp_w2'], 'L0_attn_mlp_b2': _L0_attn_in['mlp_b2'], 'L0_attn_norm1_w': _L0_attn_in['norm1_w'], 'L0_ffn_Wg': _L0_ffn_in['Wg'], 'L0_ffn_W1': _L0_ffn_in['W1'], 'L0_ffn_b1': _L0_ffn_in['b1'], 'L0_ffn_W2': _L0_ffn_in['W2'], 'L0_ffn_b2': _L0_ffn_in['b2'], 'L0_ffn_ln_hid_w': _L0_ffn_in['ln_hid_w'], 'L0_ffn_ln_hid_b': _L0_ffn_in['ln_hid_b'], 'L0_ffn_ln_out_w': _L0_ffn_in['ln_out_w'], 'L0_ffn_ln_out_b': _L0_ffn_in['ln_out_b'], 'L1_attn_gamma': _L1_attn_in['gamma'], 'L1_attn_w_qkv': _L1_attn_in['w_qkv'], 'L1_attn_w_out': _L1_attn_in['w_out'], 'L1_ffn_wg': _L1_ffn_in['wg'], 'L1_ffn_we': _L1_ffn_in['we']}
    _x0 = _d['L0_attn_Z']
    _d['L0_attn_Z'] = jax.random.normal(jax.random.fold_in(jax.random.key(seed), 1), (8, 512, 128), dtype=_x0.dtype)
    del _x0
    return _d

def reference(L0_attn_Z, L0_attn_in_proj_w, L0_attn_conv_w, L0_attn_conv_b, L0_attn_x_proj_w, L0_attn_dt_proj_w, L0_attn_dt_proj_b, L0_attn_A_log, L0_attn_D, L0_attn_out_proj_w, L0_attn_mlp_w1, L0_attn_mlp_b1, L0_attn_mlp_w2, L0_attn_mlp_b2, L0_attn_norm1_w, L0_ffn_Wg, L0_ffn_W1, L0_ffn_b1, L0_ffn_W2, L0_ffn_b2, L0_ffn_ln_hid_w, L0_ffn_ln_hid_b, L0_ffn_ln_out_w, L0_ffn_ln_out_b, L1_attn_gamma, L1_attn_w_qkv, L1_attn_w_out, L1_ffn_wg, L1_ffn_we):

    def _L0_attn_ref(Z, in_proj_w, conv_w, conv_b, x_proj_w, dt_proj_w, dt_proj_b, A_log, D, out_proj_w, mlp_w1, mlp_b1, mlp_w2, mlp_b2, norm1_w):
        import jax, jax.numpy as jnp
        import numpy as np
        B_, L_, DM, DS, DFF = (2, 128, 128, 16, 512)
        DI = 2 * DM
        DTR = (DM + 15) // 16
        K = 4

        def _rmsnorm(x, w, eps=1e-06):
            return x * jax.lax.rsqrt(jnp.mean(x * x, axis=-1, keepdims=True) + eps) * w

        def _causal_dw_conv(x, w, b):
            xp = jnp.pad(x, ((0, 0), (K - 1, 0), (0, 0)))
            out = jax.lax.conv_general_dilated(xp.transpose(0, 2, 1), w[:, None, :], window_strides=(1,), padding='VALID', dimension_numbers=('NCL', 'OIL', 'NCL'), feature_group_count=x.shape[-1])
            return out.transpose(0, 2, 1) + b

        def _mamba(Z, in_proj_w, conv_w, conv_b, x_proj_w, dt_proj_w, dt_proj_b, A_log, D, out_proj_w):
            xz = jnp.einsum('bld,ed->ble', Z, in_proj_w)
            x, z = jnp.split(xz, 2, axis=-1)
            x = jax.nn.silu(_causal_dw_conv(x, conv_w, conv_b))
            x_dbl = jnp.einsum('bld,ed->ble', x, x_proj_w)
            dt, Bm, Cm = jnp.split(x_dbl, [DTR, DTR + DS], axis=-1)
            dt = jax.nn.softplus(jnp.einsum('blr,dr->bld', dt, dt_proj_w) + dt_proj_b)
            A = -jnp.exp(A_log)
            deltaA = jnp.exp(dt[..., None] * A)
            deltaBx = dt[..., None] * Bm[:, :, None, :] * x[..., None]

            def step(h, xs):
                dA, dBx, C = xs
                h = dA * h + dBx
                y = jnp.einsum('bdn,bn->bd', h, C)
                return (h, y)
            h0 = jnp.zeros((Z.shape[0], DI, DS), Z.dtype)
            xs = (deltaA.transpose(1, 0, 2, 3), deltaBx.transpose(1, 0, 2, 3), Cm.transpose(1, 0, 2))
            _, ys = jax.lax.scan(step, h0, xs)
            y = ys.transpose(1, 0, 2) + x * D
            y = y * jax.nn.silu(z)
            return jnp.einsum('bld,ed->ble', y, out_proj_w)
        y = _mamba(Z, in_proj_w, conv_w, conv_b, x_proj_w, dt_proj_w, dt_proj_b, A_log, D, out_proj_w)
        Z_mam = _rmsnorm(y + Z, norm1_w)
        h = jax.nn.gelu(jnp.einsum('bld,fd->blf', Z_mam, mlp_w1) + mlp_b1, approximate=False)
        mlp = jnp.einsum('blf,df->bld', h, mlp_w2) + mlp_b2
        return _rmsnorm(mlp + Z_mam, norm1_w)

    def _L0_ffn_ref(x, Wg, W1, b1, W2, b2, ln_hid_w, ln_hid_b, ln_out_w, ln_out_b):
        import math
        import jax, jax.numpy as jnp
        import numpy as np
        E = 24

        def layer_norm(x, w, b, eps=1e-06):
            m = x.mean(-1, keepdims=True)
            v = x.var(-1, keepdims=True)
            return (x - m) / jnp.sqrt(v + eps) * w + b

        def top2_dispatch(x, Wg, C):
            logits = x @ Wg
            gates = jax.nn.softmax(logits, axis=-1)
            idx1 = jnp.argmax(gates, axis=-1)
            m1 = jax.nn.one_hot(idx1, E, dtype=x.dtype)
            masked = jnp.where(m1 > 0, -jnp.inf, logits)
            idx2 = jnp.argmax(masked, axis=-1)
            m2 = jax.nn.one_hot(idx2, E, dtype=x.dtype)
            loc1 = jnp.cumsum(m1, axis=0) - m1
            loc2 = jnp.cumsum(m2, axis=0) - m2 + jnp.sum(m1, axis=0, keepdims=True)
            m1 = m1 * (loc1 < C)
            m2 = m2 * (loc2 < C)
            g1 = jnp.sum(gates * m1, axis=-1)
            g2 = jnp.sum(gates * m2, axis=-1)
            denom = jnp.maximum(g1 + g2, 1e-09)
            g1, g2 = (g1 / denom, g2 / denom)
            p1 = jnp.sum(loc1 * m1, axis=-1).astype(jnp.int32)
            p2 = jnp.sum(loc2 * m2, axis=-1).astype(jnp.int32)
            c1 = g1[:, None, None] * m1[:, :, None] * jax.nn.one_hot(p1, C, dtype=x.dtype)[:, None, :]
            c2 = g2[:, None, None] * m2[:, :, None] * jax.nn.one_hot(p2, C, dtype=x.dtype)[:, None, :]
            combine = c1 + c2
            dispatch = (combine > 0).astype(x.dtype)
            return (combine, dispatch)

        def moe_apply(x, combine, dispatch, W, b):
            disp = jnp.einsum('sec,sd->ecd', dispatch, x)
            h = jnp.einsum('ecd,edf->ecf', disp, W) + b[:, None, :]
            return jnp.einsum('sec,ecf->sf', combine, h)
        bsz, seq, d = x.shape
        H = 4
        n = seq // H
        S = bsz * n
        C = math.ceil(2 * S / E)
        xg = x.reshape(bsz, H, n, d).transpose(1, 0, 2, 3).reshape(H, S, d)

        def per_group(xf, lw, lb):
            combine, dispatch = top2_dispatch(xf, Wg, C)
            h = moe_apply(xf, combine, dispatch, W1, b1)
            h = layer_norm(h, lw, lb)
            h = jax.nn.relu(h)
            return moe_apply(h, combine, dispatch, W2, b2)
        out = jax.vmap(per_group)(xg, ln_hid_w, ln_hid_b)
        out = out.reshape(H, bsz, n, d).transpose(1, 0, 2, 3).reshape(bsz, seq, d)
        return layer_norm(out + x, ln_out_w, ln_out_b)

    def _L1_attn_ref(x, gamma, w_qkv, w_out):
        import jax, jax.numpy as jnp
        import numpy as np
        DIM = 128
        DIM_HEAD = 128
        HEADS = 8
        DIM_INNER = DIM_HEAD * HEADS
        scale_norm = DIM ** 0.5
        scale_attn = DIM_HEAD ** (-0.5)
        l2 = jnp.sqrt(jnp.sum(x * x, axis=-1, keepdims=True))
        xn = x / jnp.maximum(l2, 1e-12) * scale_norm * gamma
        qkv = jnp.einsum('bnc,fc->bnf', xn, w_qkv)
        b, n, _ = qkv.shape
        qkv = qkv.reshape(b, n, 3, HEADS, DIM_HEAD)
        q, k, v = (qkv[:, :, 0], qkv[:, :, 1], qkv[:, :, 2])
        q = q * scale_attn
        sim = jnp.einsum('bihd,bjhd->bhij', q, k)
        causal_mask = jnp.triu(jnp.ones((n, n), dtype=bool), k=1)
        neg = -jnp.finfo(sim.dtype).max
        sim = jnp.where(causal_mask, neg, sim)
        attn = jax.nn.softmax(sim, axis=-1)
        out = jnp.einsum('bhij,bjhd->bihd', attn, v)
        out = out.reshape(b, n, DIM_INNER)
        return jnp.einsum('bnf,cf->bnc', out, w_out)

    def _L1_ffn_ref(x, wg, we):
        import jax, jax.numpy as jnp
        import numpy as np
        E = 128
        D = 128
        C = 32
        B, S, d = x.shape
        xt = x.reshape(-1, d)
        T = xt.shape[0]
        logits = xt @ wg
        gates = jax.nn.softmax(logits, axis=-1)
        e1 = jnp.argmax(gates, axis=-1)
        mask1 = jax.nn.one_hot(e1, E, dtype=logits.dtype)
        logits2 = jnp.where(mask1 > 0, -jnp.inf, logits)
        e2 = jnp.argmax(logits2, axis=-1)
        mask2 = jax.nn.one_hot(e2, E, dtype=logits.dtype)
        g1 = jnp.take_along_axis(gates, e1[:, None], 1)[:, 0]
        g2 = jnp.take_along_axis(gates, e2[:, None], 1)[:, 0]
        denom = jnp.maximum(g1 + g2, jnp.finfo(gates.dtype).eps)
        g1, g2 = (g1 / denom, g2 / denom)
        loc1 = jnp.take_along_axis(jnp.cumsum(mask1, axis=0), e1[:, None], 1)[:, 0].astype(jnp.int32) - 1
        counts1 = mask1.sum(axis=0)
        loc2 = (jnp.take_along_axis(jnp.cumsum(mask2, axis=0), e2[:, None], 1)[:, 0] + counts1[e2]).astype(jnp.int32) - 1
        v1 = (loc1 < C).astype(xt.dtype)
        v2 = (loc2 < C).astype(xt.dtype)
        idx1 = e1.astype(jnp.int32) * C + jnp.minimum(loc1, C - 1)
        idx2 = e2.astype(jnp.int32) * C + jnp.minimum(loc2, C - 1)
        buf = jnp.zeros((E * C, d), dtype=xt.dtype)
        buf = buf.at[idx1].add(xt * v1[:, None])
        buf = buf.at[idx2].add(xt * v2[:, None])
        yb = jnp.einsum('ecd,edf->ecf', buf.reshape(E, C, d), we).reshape(E * C, d)
        y = (g1 * v1)[:, None] * yb[idx1] + (g2 * v2)[:, None] * yb[idx2]
        return y.reshape(B, S, d)
    x = L0_attn_Z
    xn = _layernorm(x, axis=-1)
    s = _L0_attn_ref(xn, L0_attn_in_proj_w, L0_attn_conv_w, L0_attn_conv_b, L0_attn_x_proj_w, L0_attn_dt_proj_w, L0_attn_dt_proj_b, L0_attn_A_log, L0_attn_D, L0_attn_out_proj_w, L0_attn_mlp_w1, L0_attn_mlp_b1, L0_attn_mlp_w2, L0_attn_mlp_b2, L0_attn_norm1_w)
    g = _silu(_L0_ffn_ref(xn, L0_ffn_Wg, L0_ffn_W1, L0_ffn_b1, L0_ffn_W2, L0_ffn_b2, L0_ffn_ln_hid_w, L0_ffn_ln_hid_b, L0_ffn_ln_out_w, L0_ffn_ln_out_b))
    x = x + s * g
    xn = _layernorm(x, axis=-1)
    s = _L1_attn_ref(xn, L1_attn_gamma, L1_attn_w_qkv, L1_attn_w_out)
    g = _silu(_L1_ffn_ref(xn, L1_ffn_wg, L1_ffn_we))
    x = x + s * g
    return x

_drawn_inputs = setup_inputs


def setup_inputs(seed=0):
    import zlib

    import numpy as np

    out = dict(_drawn_inputs(seed))
    spreads = {'L0_attn_conv_b': (0.0, 0.8),
     'L0_attn_D': (1.0, 0.6),
     'L0_attn_mlp_b1': (0.0, 0.8),
     'L0_attn_mlp_b2': (0.0, 0.1),
     'L0_attn_norm1_w': (1.0, 0.2),
     'L0_ffn_b1': (0.0, 0.1),
     'L0_ffn_b2': (0.0, 0.1),
     'L0_ffn_ln_hid_w': (1.0, 0.6),
     'L0_ffn_ln_hid_b': (0.0, 0.8),
     'L0_ffn_ln_out_w': (1.0, 0.2),
     'L0_ffn_ln_out_b': (0.0, 0.1),
     'L1_attn_gamma': (1.0, 0.6)}
    factors = {'L0_attn_in_proj_w': 8.0,
     'L0_attn_conv_w': 8.0,
     'L0_attn_x_proj_w': 8.0,
     'L0_attn_dt_proj_w': 8.0,
     'L0_attn_dt_proj_b': 8.0,
     'L0_attn_A_log': 8.0,
     'L0_attn_out_proj_w': 8.0,
     'L0_attn_mlp_w1': 3.16,
     'L0_attn_mlp_w2': 2.918,
     'L1_attn_w_qkv': 8.0,
     'L1_attn_w_out': 8.0,
     'L1_ffn_wg': 8.0,
     'L1_ffn_we': 8.0}
    for name, (base, spread) in spreads.items():
        noise = np.random.default_rng([zlib.crc32(name.encode()), seed]).standard_normal(out[name].shape)
        drawn = base * np.exp(spread * noise) if base else spread * noise
        out[name] = jnp.asarray(drawn.astype(out[name].dtype))
    for name, factor in factors.items():
        out[name] = (out[name] * factor).astype(out[name].dtype)
    return out
```

```python
from contextlib import ExitStack

import numpy as np
import concourse.bass as bass
from concourse import mybir

F32 = mybir.dt.float32
BF16 = mybir.dt.bfloat16
U32 = mybir.dt.uint32
ALU = mybir.AluOpType
ACT = mybir.ActivationFunctionType
AX_X = mybir.AxisListType.X

P = 128
B, L, D = 8, 512, 128
N_TOK = B * L
NT = N_TOK // P
TB = L // P
DI, DS, DTR, KC = 256, 16, 8, 4
HALF = DI // P
DFF = 512
FC = DFF // P
PAD = L + KC - 1

HG, E0, C0, HID = 4, 24, 86, 512
E1, C1 = 128, 32


class Chain:

    def __init__(self, eng, sem):
        self.eng, self.sem, self.n = eng, sem, 0

    def __call__(self, ins):
        self.n += 1
        ins.then_inc(self.sem, 1)
        self.eng.wait_ge(self.sem, self.n)
        return ins


class Scope:

    def __init__(self, nc, ctx, tag):
        self.nc, self.ctx, self.tag = nc, ctx, tag

    def sb(self, name, shape, dt=F32):
        return self.ctx.enter_context(self.nc.sbuf_tensor(f"{self.tag}_{name}", shape, dt))

    def ps(self, name, shape, dt=F32):
        return self.ctx.enter_context(self.nc.psum_tensor(f"{self.tag}_{name}", shape, dt))

    def sem(self, name):
        return self.ctx.enter_context(self.nc.semaphore(f"{self.tag}_{name}"))


def bcast(ap, n):
    return ap.unsqueeze(2).broadcast_to([ap.shape[0], ap.shape[1], n])


def layernorm_stage(nc, src_dram, xn_dram, x_rows, xn_rows, xnT, ident, tag, loads):
    G = 4
    steps = NT // G
    with ExitStack() as ctx:
        s = Scope(nc, ctx, tag)
        sums = s.sb("sums", [P, NT])
        nmean = s.sb("nmean", [P, NT])
        sq = s.sb("sq", [P, G, D])
        var = s.sb("var", [P, NT])
        rstd = s.sb("rstd", [P, NT])
        pt = s.ps("pt", [P, 4, L])
        x_in = s.sem("x_in")
        x_in2 = s.sem("x_in2")
        consts_in = s.sem("consts_in")
        chain = s.sem("chain")
        var_ready = s.sem("var_ready")
        rstd_ready = s.sem("rstd_ready")
        normed = s.sem("normed")
        turned = s.sem("turned")
        evacuated = s.sem("evacuated")
        stored = s.sem("stored")
        block = ctx.enter_context(nc.Block())

        @block.sync
        def _(sp):
            if src_dram is not None:
                for h in range(2):
                    sp.dma_start(x_rows[:, h * 16:(h + 1) * 16, :],
                                 src_dram[:, h * 16:(h + 1) * 16, :]).then_inc(x_in if h == 0 else x_in2, 16)
            for dst, src in loads:
                sp.dma_start(dst, src).then_inc(consts_in, 16)
            for g in range(steps):
                sp.wait_ge(normed, g + 1)
                sp.dma_start(xn_dram[:, g * G:(g + 1) * G, :], xn_rows[:, g * G:(g + 1) * G, :]).then_inc(stored, 16)
            sp.wait_ge(stored, 16 * steps)
            if loads:
                sp.wait_ge(consts_in, 16 * len(loads))

        @block.vector
        def _(dve):
            link = Chain(dve, chain)
            link(nc.vector.memset(xnT[:, :, 0:KC - 1], 0.0))
            for g in range(steps):
                t = slice(g * G, (g + 1) * G)
                if src_dram is not None and g == 0:
                    dve.wait_ge(x_in, 16)
                if src_dram is not None and g == steps // 2:
                    dve.wait_ge(x_in2, 16)
                link(nc.vector.tensor_reduce(sums[:, t], x_rows[:, t, :], AX_X, ALU.add))
                link(nc.vector.tensor_scalar(nmean[:, t], sums[:, t], -1.0 / D, None, ALU.mult))
                link(nc.vector.tensor_tensor(xn_rows[:, t, :], x_rows[:, t, :], bcast(nmean[:, t], D), ALU.add))
                link(nc.vector.tensor_tensor(sq[:, :, :], xn_rows[:, t, :], xn_rows[:, t, :], ALU.mult))
                link(nc.vector.tensor_reduce(var[:, t], sq[:, :, :], AX_X, ALU.add))
                nc.vector.tensor_scalar(var[:, t], var[:, t], 1.0 / D, 1e-5, ALU.mult, ALU.add).then_inc(var_ready, 1)
                dve.wait_ge(rstd_ready, g + 1)
                link(nc.vector.reciprocal(rstd[:, t], rstd[:, t]))
                nc.vector.tensor_tensor(xn_rows[:, t, :], xn_rows[:, t, :], bcast(rstd[:, t], D),
                                        ALU.mult).then_inc(normed, 1)

        @block.tensor
        def _(pe):
            if loads:
                pe.wait_ge(consts_in, 16 * len(loads))
            for g in range(steps):
                pe.wait_ge(normed, g + 1)
                if g >= 4:
                    pe.wait_ge(evacuated, g - 3)
                for j in range(G):
                    last = nc.tensor.transpose(pt[:, g % 4, j * P:(j + 1) * P], xn_rows[:, g * G + j, :], ident)
                last.then_inc(turned, 1)

        @block.scalar
        def _(act):
            for g in range(steps + 1):
                if g < steps:
                    t = slice(g * G, (g + 1) * G)
                    act.wait_ge(var_ready, g + 1)
                    nc.scalar.activation(rstd[:, t], var[:, t], ACT.Sqrt).then_inc(rstd_ready, 1)
                if g:
                    act.wait_ge(turned, g)
                    nc.scalar.activation(xnT[:, g - 1, KC - 1:PAD], pt[:, (g - 1) % 4, :],
                                         ACT.Copy).then_inc(evacuated, 1)


def mamba_input_stage(nc, w, xnT, xT, zT):
    with ExitStack() as ctx:
        s = Scope(nc, ctx, "mi")
        taps = s.sb("taps", [P, KC, DI])
        pj = s.ps("pj", [P, 8, L])
        chain = s.sem("chain")
        folded = s.sem("folded")
        product = s.sem("product")
        activated = s.sem("activated")
        block = ctx.enter_context(nc.Block())

        @block.vector
        def _(dve):
            for k in range(KC):
                nc.vector.tensor_tensor(taps[:, k, :], w["in_T"][:, 0:DI], w["conv_rows"][:, k, :],
                                        ALU.mult).then_inc(folded, 1)

        @block.tensor
        def _(pe):
            pe.wait_ge(folded, KC)
            for n in range(B * 4):
                b, e = divmod(n, 4)
                if n >= 8:
                    pe.wait_ge(activated, n - 7)
                if e < HALF:
                    for k in range(KC):
                        last = nc.tensor.matmul(pj[:, n % 8, :], taps[:, k, e * P:(e + 1) * P],
                                                xnT[:, b, k:k + L], start=(k == 0), stop=(k == KC - 1))
                else:
                    last = nc.tensor.matmul(pj[:, n % 8, :], w["in_T"][:, e * P:(e + 1) * P],
                                            xnT[:, b, KC - 1:PAD], start=True, stop=True)
                last.then_inc(product, 1)

        @block.scalar
        def _(act):
            for n in range(B * 4):
                b, e = divmod(n, 4)
                act.wait_ge(product, n + 1)
                if e < HALF:
                    nc.scalar.activation(xT[:, e, b * L:(b + 1) * L], pj[:, n % 8, :], ACT.Silu,
                                         bias=w["conv_b"][:, e:e + 1]).then_inc(activated, 1)
                else:
                    nc.scalar.activation(zT[:, e - HALF, b * L:(b + 1) * L], pj[:, n % 8, :],
                                         ACT.Silu).then_inc(activated, 1)


def scan_stage(nc, w, xT, zT):
    PAIRS = DS // 2
    with ExitStack() as ctx:
        s = Scope(nc, ctx, "sc")
        negA = s.sb("negA", [P, 2, DS])
        bc3 = s.sb("bc3", [96, 2, L], BF16)
        rest = s.sb("rest", [96, L])
        mid = s.sb("mid", [96, L], BF16)
        dtr = s.sb("dtr", [DTR, 2, L])
        dt = s.sb("dt", [P, 2, 2, L])
        u = s.sb("u", [P, 2, 2, L])
        mag = s.sb("mag", [P, L])
        em = s.sb("em", [P, L])
        ln1 = s.sb("ln1", [P, L])
        lost = s.sb("lost", [P, L])
        relu = s.sb("relu", [P, L])
        dA = s.sb("dA", [P, 4, 2, L])
        st = s.sb("st", [P, 4, 2, L])
        yg = s.sb("yg", [P, 2, L])
        p_b = s.ps("p_b", [P, 2, L])
        p_c = s.ps("p_c", [P, 2, L])
        p_y = s.ps("p_y", [P, 2, L])
        p_x = s.ps("p_x", [P, L])
        p_dt = s.ps("p_dt", [P, L])
        chain = s.sem("chain")
        a_chain = s.sem("a_chain")
        exp_A = s.sem("exp_A")
        neg_A = s.sem("neg_A")
        cleared = s.sem("cleared")
        xp_ready = s.sem("xp_ready")
        dr_copied = s.sem("dr_copied")
        bc_read = s.sem("bc_read")
        bc_done = s.sem("bc_done")
        dt_product = s.sem("dt_product")
        mag_read = s.sem("mag_read")
        relu_read = s.sem("relu_read")
        ln_ready = s.sem("ln_ready")
        dt_done = s.sem("dt_done")
        b_ready = s.sem("b_ready")
        b_used = s.sem("b_used")
        c_ready = s.sem("c_ready")
        hc_ready = s.sem("hc_ready")
        hc_used = s.sem("hc_used")
        decay_ready = s.sem("decay_ready")
        scanned = s.sem("scanned")
        y_used = s.sem("y_used")
        block = ctx.enter_context(nc.Block())

        @block.scalar
        def _(act):
            link = Chain(act, a_chain)

            def copy_dt_rank(b):
                act.wait_ge(xp_ready, b + 1)
                if b >= 2:
                    act.wait_ge(dt_product, 2 * (b - 1))
                nc.scalar.activation(dtr[:, b % 2, :], p_x[96:96 + DTR, :], ACT.Copy).then_inc(dr_copied, 1)

            def softplus_logs(b, h):
                n = 2 * b + h
                act.wait_ge(dt_product, n + 1)
                nc.scalar.activation(mag[:, :], p_dt[:, :], ACT.Abs, bias=w["dt_b"][:, h:h + 1]).then_inc(mag_read, 1)
                act.wait_ge(mag_read, n + 1)
                if n:
                    act.wait_ge(dt_done, n)
                link(nc.scalar.activation(em[:, :], mag[:, :], ACT.Exp, scale=-1.0))
                nc.scalar.activation(ln1[:, :], em[:, :], ACT.Ln, bias=1.0).then_inc(ln_ready, 1)

            nc.scalar.activation(negA[:, :, :], w["A_log"][:, :, :], ACT.Exp).then_inc(exp_A, 1)
            copy_dt_rank(0)
            softplus_logs(0, 0)
            softplus_logs(0, 1)
            act.wait_ge(cleared, 1)
            act.wait_ge(neg_A, 1)
            for i in range(B * PAIRS):
                b, q = divmod(i, PAIRS)
                if q == 0:
                    act.wait_ge(dt_done, 2 * b + 2)
                for h in range(HALF):
                    m = 2 * i + h
                    if m >= 4:
                        act.wait_ge(scanned, m - 3)
                    for j in range(2):
                        ins = nc.scalar.activation(dA[:, m % 4, j, 1:L], dt[:, b % 2, h, 1:L], ACT.Exp,
                                                   scale=negA[:, h, 2 * q + j:2 * q + j + 1])
                    ins.then_inc(decay_ready, 1)
                if b + 1 < B:
                    if q == 1:
                        copy_dt_rank(b + 1)
                    if q == 3:
                        softplus_logs(b + 1, 0)
                    if q == 5:
                        softplus_logs(b + 1, 1)

        @block.tensor
        def _(pe):
            def x_project(b):
                if b:
                    pe.wait_ge(dr_copied, b)
                    pe.wait_ge(bc_read, b)
                for h in range(HALF):
                    ins = nc.tensor.matmul(p_x[0:96 + DTR, :], w["xproj_T"][:, h, :], xT[:, h, b * L:(b + 1) * L],
                                           start=(h == 0), stop=(h == 1))
                ins.then_inc(xp_ready, 1)

            def dt_project(b, h):
                n = 2 * b + h
                pe.wait_ge(dr_copied, b + 1)
                if n:
                    pe.wait_ge(mag_read, n)
                    pe.wait_ge(relu_read, n)
                nc.tensor.matmul(p_dt[:, :], w["dt_T"][:, h * P:(h + 1) * P], dtr[:, b % 2, :],
                                 start=True, stop=True).then_inc(dt_product, 1)

            def sum_states(i):
                b, q = divmod(i, PAIRS)
                for h in range(HALF):
                    m = 2 * i + h
                    if q == 0 and b and h == 0:
                        pe.wait_ge(y_used, b)
                    pe.wait_ge(hc_ready, m + 1)
                    for j in range(2):
                        ins = nc.tensor.matmul(p_y[:, h, :], w["ident"], st[:, m % 4, j, :],
                                               start=(q == 0 and j == 0), stop=(q == PAIRS - 1 and j == 1))
                    ins.then_inc(hc_used, 1)

            x_project(0)
            dt_project(0, 0)
            dt_project(0, 1)
            for i in range(B * PAIRS):
                b, q = divmod(i, PAIRS)
                if q == 0:
                    pe.wait_ge(bc_done, b + 1)
                if i:
                    pe.wait_ge(b_used, i)
                for j in range(2):
                    ins = nc.tensor.matmul(p_b[:, j, :], w["sel"][:, (2 * q + j) * P:(2 * q + j + 1) * P],
                                           bc3[:, b % 2, :], start=True, stop=True)
                ins.then_inc(b_ready, 1)
                if i:
                    pe.wait_ge(hc_ready, 2 * i)
                for j in range(2):
                    n = DS + 2 * q + j
                    ins = nc.tensor.matmul(p_c[:, j, :], w["sel"][:, n * P:(n + 1) * P],
                                           bc3[:, b % 2, :], start=True, stop=True)
                ins.then_inc(c_ready, 1)
                if i:
                    sum_states(i - 1)
                if b + 1 < B:
                    if q == 1:
                        x_project(b + 1)
                    if q == 2:
                        dt_project(b + 1, 0)
                    if q == 4:
                        dt_project(b + 1, 1)
            sum_states(B * PAIRS - 1)

        @block.vector
        def _(dve):
            link = Chain(dve, chain)
            dve.wait_ge(exp_A, 1)
            nc.vector.tensor_scalar(negA[:, :, :], negA[:, :, :], -1.0, None, ALU.mult).then_inc(neg_A, 1)
            nc.vector.memset(dA[:, :, :, 0:1], 0.0).then_inc(cleared, 1)

            def split_bc(b):
                dve.wait_ge(dr_copied, b + 1)
                hi = bc3[:, b % 2, :]
                link(nc.vector.tensor_copy(hi, p_x[0:96, :]))
                nc.vector.tensor_tensor(rest[:, :], p_x[0:96, :], hi, ALU.subtract).then_inc(bc_read, 1)
                dve.wait_ge(bc_read, b + 1)
                link(nc.vector.tensor_copy(mid[:, :], rest[:, :]))
                nc.vector.tensor_copy(bc3[32:64, b % 2, :], mid[32:64, :])
                nc.vector.tensor_tensor(bc3[64:96, b % 2, :], rest[64:96, :], mid[64:96, :],
                                        ALU.subtract).then_inc(bc_done, 1)
                dve.wait_ge(bc_done, b + 1)

            def softplus(b, h):
                n = 2 * b + h
                dve.wait_ge(mag_read, n + 1)
                nc.vector.tensor_scalar(relu[:, :], p_dt[:, :], w["dt_b"][:, h:h + 1], 0.0,
                                        ALU.add, ALU.max).then_inc(relu_read, 1)
                dve.wait_ge(ln_ready, n + 1)
                link(nc.vector.tensor_scalar(lost[:, :], em[:, :], 1.0, 1.0, ALU.add, ALU.subtract))
                link(nc.vector.tensor_tensor(lost[:, :], em[:, :], lost[:, :], ALU.subtract))
                link(nc.vector.tensor_tensor(lost[:, :], lost[:, :], ln1[:, :], ALU.add))
                nc.vector.tensor_tensor(dt[:, b % 2, h, :], relu[:, :], lost[:, :], ALU.add).then_inc(dt_done, 1)
                dve.wait_ge(dt_done, n + 1)
                link(nc.vector.tensor_tensor(u[:, b % 2, h, :], dt[:, b % 2, h, :], xT[:, h, b * L:(b + 1) * L],
                                             ALU.mult))

            def gate(b):
                cols = slice(b * L, (b + 1) * L)
                dve.wait_ge(hc_used, 2 * PAIRS * (b + 1))
                for h in range(HALF):
                    ins = nc.vector.scalar_tensor_tensor(out=yg[:, h, :], in0=xT[:, h, cols], scalar=w["D"][:, h:h + 1],
                                                         in1=p_y[:, h, :], op0=ALU.mult, op1=ALU.add)
                ins.then_inc(y_used, 1)
                dve.wait_ge(y_used, b + 1)
                for h in range(HALF):
                    ins = nc.vector.tensor_tensor(zT[:, h, cols], yg[:, h, :], zT[:, h, cols], ALU.mult)
                link(ins)

            split_bc(0)
            softplus(0, 0)
            softplus(0, 1)
            for i in range(B * PAIRS):
                b, q = divmod(i, PAIRS)
                dve.wait_ge(b_ready, i + 1)
                for h in range(HALF):
                    m = 2 * i + h
                    if m >= 4:
                        dve.wait_ge(hc_used, m - 3)
                    ins = nc.vector.tensor_tensor(st[:, m % 4, :, :], p_b[:, :, :],
                                                  u[:, b % 2, h, :].unsqueeze(1).broadcast_to([P, 2, L]), ALU.mult)
                ins.then_inc(b_used, 1)
                dve.wait_ge(b_used, i + 1)
                for h in range(HALF):
                    m = 2 * i + h
                    dve.wait_ge(decay_ready, m + 1)
                    nc.vector.tensor_tensor_scan(st[:, m % 4, :, :].rearrange("p a b -> p (a b)"),
                                                 dA[:, m % 4, :, :].rearrange("p a b -> p (a b)"),
                                                 st[:, m % 4, :, :].rearrange("p a b -> p (a b)"),
                                                 0.0, ALU.mult, ALU.add).then_inc(scanned, 1)
                dve.wait_ge(c_ready, i + 1)
                for h in range(HALF):
                    m = 2 * i + h
                    dve.wait_ge(scanned, m + 1)
                    nc.vector.tensor_tensor(st[:, m % 4, :, :], st[:, m % 4, :, :], p_c[:, :, :],
                                            ALU.mult).then_inc(hc_ready, 1)
                if q == 0 and b:
                    gate(b - 1)
                dve.wait_ge(hc_ready, 2 * i + 2)
                if b + 1 < B:
                    if q == 2:
                        split_bc(b + 1)
                    if q == 4:
                        softplus(b + 1, 0)
                    if q == 6:
                        softplus(b + 1, 1)
            gate(B - 1)


def mamba_output_stage(nc, w, yT, xn_rows, s_rows):
    with ExitStack() as ctx:
        s = Scope(nc, ctx, "mo")
        z = s.sb("z", [P, NT, D])
        zT = s.sb("zT", [P, 2, L])
        hT = s.sb("hT", [P, 2, FC, L])
        sq = s.sb("sq", [P, TB, D])
        acc = s.sb("acc", [P, NT])
        root = s.sb("root", [P, NT])
        p_o = s.ps("p_o", [P, L])
        p_t = s.ps("p_t", [P, 2, L])
        p_h = s.ps("p_h", [P, 4, L])
        p_m = s.ps("p_m", [P, L])
        chain = s.sem("chain")
        projected = s.sem("projected")
        o_used = s.sem("o_used")
        mean_ready = s.sem("mean_ready")
        root_ready = s.sem("root_ready")
        z_ready = s.sem("z_ready")
        z_turned = s.sem("z_turned")
        zT_ready = s.sem("zT_ready")
        h_product = s.sem("h_product")
        h_ready = s.sem("h_ready")
        m_product = s.sem("m_product")
        m_used = s.sem("m_used")
        block = ctx.enter_context(nc.Block())

        @block.tensor
        def _(pe):
            for b in range(B):
                if b:
                    pe.wait_ge(o_used, b)
                for j in range(TB):
                    for h in range(HALF):
                        ins = nc.tensor.matmul(p_o[:, j * D:(j + 1) * D], yT[:, h, b * L + j * P:b * L + (j + 1) * P],
                                               w["out_T"][:, h, :], start=(h == 0), stop=(h == 1))
                ins.then_inc(projected, 1)

            def hidden(b):
                pe.wait_ge(z_ready, b + 1)
                if b >= 2:
                    pe.wait_ge(zT_ready, b - 1)
                for j in range(TB):
                    ins = nc.tensor.transpose(p_t[:, b % 2, j * P:(j + 1) * P], z[:, b * TB + j, :], w["ident"])
                ins.then_inc(z_turned, 1)
                pe.wait_ge(zT_ready, b + 1)
                for f in range(FC):
                    n = FC * b + f
                    if n >= 4:
                        pe.wait_ge(h_ready, n - 3)
                    nc.tensor.matmul(p_h[:, n % 4, :], w["w1_T"][:, f * P:(f + 1) * P], zT[:, b % 2, :],
                                     start=True, stop=True).then_inc(h_product, 1)

            hidden(0)
            for b in range(B):
                if b + 1 < B:
                    hidden(b + 1)
                pe.wait_ge(h_ready, FC * (b + 1))
                if b:
                    pe.wait_ge(m_used, b)
                for j in range(TB):
                    for f in range(FC):
                        ins = nc.tensor.matmul(p_m[:, j * D:(j + 1) * D], hT[:, b % 2, f, j * P:(j + 1) * P],
                                               w["w2_T"][:, f, :], start=(f == 0), stop=(f == FC - 1))
                ins.then_inc(m_product, 1)

        @block.scalar
        def _(act):
            for b in range(B):
                act.wait_ge(mean_ready, b + 1)
                t = slice(b * TB, (b + 1) * TB)
                nc.scalar.activation(root[:, t], acc[:, t], ACT.Sqrt).then_inc(root_ready, 1)
            for b in range(B):
                act.wait_ge(z_turned, b + 1)
                if b >= 2:
                    act.wait_ge(h_product, FC * (b - 1))
                nc.scalar.activation(zT[:, b % 2, :], p_t[:, b % 2, :], ACT.Copy).then_inc(zT_ready, 1)
                for f in range(FC):
                    n = FC * b + f
                    act.wait_ge(h_product, n + 1)
                    if b >= 2 and f == 0:
                        act.wait_ge(m_product, b - 1)
                    nc.scalar.activation(hT[:, b % 2, f, :], p_h[:, n % 4, :], ACT.Gelu,
                                         bias=w["b1"][:, f:f + 1]).then_inc(h_ready, 1)
            act.wait_ge(mean_ready, B + 1)
            nc.scalar.activation(root[:, :], acc[:, :], ACT.Sqrt).then_inc(root_ready, 1)

        @block.vector
        def _(dve):
            link = Chain(dve, chain)

            def rows(p):
                return p[:, :].rearrange("p (a d) -> p a d", d=D)

            def squares(v, t):
                link(nc.vector.tensor_tensor(sq[:, :, :], v, v, ALU.mult))
                link(nc.vector.tensor_reduce(acc[:, t], sq[:, :, :], AX_X, ALU.add))

            def scale(v, t, signal):
                n = t.stop - t.start
                link(nc.vector.reciprocal(root[:, t], root[:, t]))
                link(nc.vector.tensor_tensor(v, v, bcast(root[:, t], D), ALU.mult))
                ins = nc.vector.tensor_tensor(v, v, w["norm1"][:, :].unsqueeze(1).broadcast_to([P, n, D]), ALU.mult)
                if signal is None:
                    link(ins)
                else:
                    ins.then_inc(signal, 1)

            for b in range(B + 1):
                if b < B:
                    t = slice(b * TB, (b + 1) * TB)
                    dve.wait_ge(projected, b + 1)
                    nc.vector.tensor_tensor(z[:, t, :], rows(p_o), xn_rows[:, t, :], ALU.add).then_inc(o_used, 1)
                    dve.wait_ge(o_used, b + 1)
                    squares(z[:, t, :], t)
                    nc.vector.tensor_scalar(acc[:, t], acc[:, t], 1.0 / D, 1e-6, ALU.mult,
                                            ALU.add).then_inc(mean_ready, 1)
                if b:
                    dve.wait_ge(root_ready, b)
                    t = slice((b - 1) * TB, b * TB)
                    scale(z[:, t, :], t, z_ready)
            dve.wait_ge(z_ready, B)
            for b in range(B):
                t = slice(b * TB, (b + 1) * TB)
                link(nc.vector.tensor_tensor(s_rows[:, t, :], z[:, t, :],
                                             w["b2"][:, :].unsqueeze(1).broadcast_to([P, TB, D]), ALU.add))
                dve.wait_ge(m_product, b + 1)
                nc.vector.tensor_tensor(s_rows[:, t, :], rows(p_m), s_rows[:, t, :], ALU.add).then_inc(m_used, 1)
                dve.wait_ge(m_used, b + 1)
                squares(s_rows[:, t, :], t)
            nc.vector.tensor_scalar(acc[:, :], acc[:, :], 1.0 / D, 1e-6, ALU.mult, ALU.add).then_inc(mean_ready, 1)
            dve.wait_ge(root_ready, B + 1)
            scale(s_rows[:, :, :], slice(0, NT), None)


class Routing:
    pass


def routing_stage(nc, w, r, xnT, wg, cfg, tag):
    E, C, groups, LO, HI, masked_first, floor = (cfg[x] for x in ("E", "C", "groups", "LO", "HI", "masked", "floor"))
    steps = NT // groups
    width = groups * E
    TC = 16 if E < 32 else 4
    NCH = NT // TC
    split = HI < E
    with ExitStack() as ctx:
        s = Scope(nc, ctx, tag)
        lg = s.sb("lg", [P, NT, E])
        ex = s.sb("ex", [P, NT, E])
        mx = s.sb("mx", [P, NT, 8])
        ix = s.sb("ix", [P, NT, 8], U32)
        idx = s.sb("idx", [P, 2, NT])
        lo_e = s.sb("lo_e", [P, 2, NT])
        hi_e = s.sb("hi_e", [P, 2, NT])
        bits = s.sb("bits", [P, 2, NT], U32)
        m = [s.sb(f"m{k}", [P, NT, E], BF16) for k in range(2)]
        acc = [s.sb(f"acc{k}", [P, steps + 1, width], BF16) for k in range(2)]
        mh = s.sb("mh", [P, NT, HI], BF16)
        loc = s.sb("loc", [P, 2, NT])
        valid = s.sb("valid", [P, 2, NT])
        lo = s.sb("lo", [P, 2, NT])
        A = [s.sb(f"A{k}", [P, NT, LO], BF16) for k in range(2)]
        R = [s.sb(f"R{k}", [P, NT, 2, HI], BF16) for k in range(2)]
        S = s.sb("S", [P, NT])
        d21 = s.sb("d21", [P, NT])
        g = s.sb("g", [P, 2, NT])
        den = s.sb("den", [P, NT])
        rows = s.sb("rows", [P, 2, NT])
        tabf = s.sb("tabf", [LO, groups, HI])
        p_l = s.ps("p_l", [P, 4, 512])
        p_n = s.ps("p_n", [P, 2, 512])
        p_t = s.ps("p_t", [LO, 512])
        chain = s.sem("chain")
        logits = s.sem("logits")
        logits_used = s.sem("logits_used")
        masks = s.sem("masks")
        counted = s.sem("counted")
        count_used = s.sem("count_used")
        shifted = s.sem("shifted")
        exps = s.sem("exps")
        onehots = s.sem("onehots")
        table = s.sem("table")
        back_ready = s.sem("back_ready")
        g_ready = s.sem("g_ready")
        g_turned = s.sem("g_turned")
        g_copied = s.sem("g_copied")
        block = ctx.enter_context(nc.Block())

        @block.tensor
        def _(pe):
            for t in range(NT):
                c, j = divmod(t, TC)
                b, q = divmod(t, TB)
                if j == 0 and c >= 4:
                    pe.wait_ge(logits_used, c - 3)
                ins = nc.tensor.matmul(p_l[:, c % 4, j * E:(j + 1) * E],
                                       xnT[:, b, KC - 1 + q * P:KC - 1 + (q + 1) * P], wg, start=True, stop=True)
                if j == TC - 1:
                    ins.then_inc(logits, 1)
            pe.wait_ge(masks, 1)
            for k in range(2):
                for c in range(NCH):
                    n = k * NCH + c
                    if n >= 2:
                        pe.wait_ge(count_used, n - 1)
                    cols = TC * E
                    steps_c = TC // groups
                    out = p_n[:, n % 2, 0:cols]
                    nc.tensor.matmul(out, w["tri"], m[k][:, c * TC:(c + 1) * TC, :].rearrange("p a b -> p (a b)"),
                                     start=True, stop=False)
                    last = k == 0
                    ins = nc.tensor.matmul(out, w["ones"],
                                           acc[k][:, c * steps_c:(c + 1) * steps_c, :].rearrange("p a b -> p (a b)"),
                                           start=False, stop=last)
                    if k:
                        total = acc[0][:, steps:steps + 1, :].broadcast_to([P, steps_c, width])
                        ins = nc.tensor.matmul(out, w["ones"], total, start=False, stop=True)
                    ins.then_inc(counted, 1)
            pe.wait_ge(onehots, 1)
            for h in range(groups):
                for i in range(steps):
                    t = i * groups + h
                    for k in range(2):
                        ins = nc.tensor.matmul(p_t[:, h * 2 * HI:(h + 1) * 2 * HI], A[k][:, t, :],
                                               R[k][:, t, :, :].rearrange("p a b -> p (a b)"),
                                               start=(i == 0 and k == 0), stop=(i == steps - 1 and k == 1))
            ins.then_inc(table, 1)
            if r.GT is not None:
                pe.wait_ge(g_ready, 1)
                for b in range(B):
                    if b >= 2:
                        pe.wait_ge(g_copied, b - 1)
                    for j in range(TB):
                        ins = nc.tensor.transpose(p_l[0:E, b % 2, j * P:(j + 1) * P], ex[:, b * TB + j, :], w["ident"])
                    ins.then_inc(g_turned, 1)

        @block.scalar
        def _(act):
            act.wait_ge(shifted, 1)
            nc.scalar.activation(lg[:, :, :], ex[:, :, :], ACT.Exp).then_inc(exps, 1)
            nc.scalar.activation(d21[:, :], d21[:, :], ACT.Exp).then_inc(exps, 1)
            if r.GT is not None:
                for b in range(B):
                    act.wait_ge(g_turned, b + 1)
                    nc.scalar.activation(r.GT[:, b * L:(b + 1) * L], p_l[0:E, b % 2, :], ACT.Copy).then_inc(g_copied, 1)

        @block.vector
        def _(dve):
            link = Chain(dve, chain)
            v = nc.vector
            for c in range(NCH):
                dve.wait_ge(logits, c + 1)
                v.tensor_copy(lg[:, c * TC:(c + 1) * TC, :],
                              p_l[:, c % 4, 0:TC * E].rearrange("p (a b) -> p a b", b=E)).then_inc(logits_used, 1)
            dve.wait_ge(logits_used, NCH)
            for t in range(NT):
                ins = v.max(mx[:, t, :], lg[:, t, :])
            link(ins)
            for t in range(NT):
                ins = v.max_index(ix[:, t, :], mx[:, t, :], lg[:, t, :])
            link(ins)
            v.tensor_tensor(d21[:, :], mx[:, :, 1], mx[:, :, 0], ALU.subtract)
            v.tensor_tensor(ex[:, :, :], lg[:, :, :], bcast(mx[:, :, 0], E), ALU.subtract).then_inc(shifted, 1)
            for k in range(2):
                link(v.tensor_copy(idx[:, k, :], ix[:, :, k]))
            for k in range(2):
                v.tensor_tensor(m[k][:, :, :], w["iota"][:, 0:E].unsqueeze(1).broadcast_to([P, NT, E]),
                                bcast(idx[:, k, :], E), ALU.is_equal)
                link(v.memset(acc[k][:, 0, :], 0.0))
            for i in range(steps):
                for k in range(2):
                    ins = v.tensor_tensor(acc[k][:, i + 1, :], acc[k][:, i, :],
                                          m[k][:, i * groups:(i + 1) * groups, :].rearrange("p a b -> p (a b)"), ALU.add)
                link(ins)
            v.memset(den[:, :], 0.0).then_inc(masks, 1)
            if split:
                for k in range(2):
                    link(v.tensor_single_scalar(bits[:, k, :], ix[:, :, k], 2, ALU.logical_shift_right))
                    link(v.tensor_copy(hi_e[:, k, :], bits[:, k, :]))
                    link(v.tensor_single_scalar(bits[:, k, :], ix[:, :, k], 3, ALU.bitwise_and))
                    link(v.tensor_copy(lo_e[:, k, :], bits[:, k, :]))
            dve.wait_ge(exps, 2)
            link(v.tensor_reduce(S[:, :], lg[:, :, :], AX_X, ALU.add))
            link(v.reciprocal(g[:, 0, :], S[:, :]))
            link(v.tensor_tensor(g[:, 1, :], d21[:, :], g[:, 0, :], ALU.mult))
            for k in range(2):
                for c in range(NCH):
                    n = k * NCH + c
                    dve.wait_ge(counted, n + 1)
                    t = slice(c * TC, (c + 1) * TC)
                    v.tensor_tensor(ex[:, t, :], p_n[:, n % 2, 0:TC * E].rearrange("p (a b) -> p a b", b=E),
                                    m[k][:, t, :], ALU.mult).then_inc(count_used, 1)
                dve.wait_ge(count_used, (k + 1) * NCH)
                link(v.tensor_reduce(loc[:, k, :], ex[:, :, :], AX_X, ALU.add))
            link(v.tensor_scalar(valid[:, :, :], loc[:, :, :], float(C), None, ALU.is_lt))
            if split:
                link(v.scalar_tensor_tensor(out=lo[:, :, :], in0=lo_e[:, :, :], scalar=float(C), in1=loc[:, :, :],
                                            op0=ALU.mult, op1=ALU.add))
                link(v.tensor_tensor(lo[:, :, :], lo[:, :, :], valid[:, :, :], ALU.mult))
                link(v.tensor_scalar(rows[:, :, :], valid[:, :, :], -1000.0, 1000.0, ALU.mult, ALU.add))
                link(v.tensor_tensor(lo[:, :, :], lo[:, :, :], rows[:, :, :], ALU.add))
            low, high = (lo, hi_e) if split else (loc, idx)
            for k in range(2):
                link(v.tensor_tensor(A[k][:, :, :], w["iota"][:, 0:LO].unsqueeze(1).broadcast_to([P, NT, LO]),
                                     bcast(low[:, k, :], LO), ALU.is_equal))
                if split:
                    link(v.tensor_tensor(mh[:, :, :], w["iota"][:, 0:HI].unsqueeze(1).broadcast_to([P, NT, HI]),
                                         bcast(high[:, k, :], HI), ALU.is_equal))
                pick = mh if split else m[k]
                v.tensor_scalar(R[k][:, :, 0, :], pick[:, :, :], w["pcol"], None, ALU.mult)
                link(v.tensor_tensor(R[k][:, :, 1, :], pick[:, :, :], bcast(w["iota"][:, 0:NT], HI), ALU.mult))
            v.memset(S[:, :], 0.0).then_inc(onehots, 1)
            link(v.scalar_tensor_tensor(out=rows[:, :, :], in0=idx[:, :, :], scalar=float(C), in1=loc[:, :, :],
                                        op0=ALU.mult, op1=ALU.add))
            link(v.tensor_tensor(rows[:, :, :], rows[:, :, :], valid[:, :, :], ALU.mult))
            if groups > 1:
                for k in range(2):
                    ins = v.tensor_tensor(rows[:, k, :].rearrange("p (a b) -> p a b", b=groups),
                                          rows[:, k, :].rearrange("p (a b) -> p a b", b=groups),
                                          w["group_base"][:, 0:groups].unsqueeze(1).broadcast_to([P, steps, groups]),
                                          ALU.add)
                link(ins)
            link(v.tensor_copy(r.back[:, :, :], rows[:, :, :]))
            if masked_first:
                link(v.tensor_tensor(g[:, :, :], g[:, :, :], valid[:, :, :], ALU.mult))
            link(v.tensor_tensor(den[:, :], g[:, 0, :], g[:, 1, :], ALU.add))
            link(v.tensor_scalar(den[:, :], den[:, :], floor, None, ALU.max))
            link(v.reciprocal(den[:, :], den[:, :]))
            for k in range(2):
                link(v.tensor_tensor(r.wk[:, k, :], g[:, k, :], den[:, :], ALU.mult))
            if not masked_first:
                link(v.tensor_tensor(r.wk[:, :, :], r.wk[:, :, :], valid[:, :, :], ALU.mult))
            dve.wait_ge(table, 1)
            pt = p_t[:, 0:groups * 2 * HI].rearrange("p (h a c) -> p h a c", h=groups, a=2)
            link(v.tensor_scalar(tabf[:, :, :], pt[:, :, 0, :], float(NT), None, ALU.mult))
            link(v.tensor_tensor(tabf[:, :, :], tabf[:, :, :], pt[:, :, 1, :], ALU.add))
            if groups > 1:
                pass
            link(v.tensor_copy(r.tab[:, :, :], tabf[:, :, :]))
            if r.GT is not None:
                link(v.tensor_tensor(ex[:, :, :], m[0][:, :, :], bcast(r.wk[:, 0, :], E), ALU.mult))
                link(v.tensor_tensor(lg[:, :, :], m[1][:, :, :], bcast(r.wk[:, 1, :], E), ALU.mult))
                v.tensor_tensor(ex[:, :, :], ex[:, :, :], lg[:, :, :], ALU.add).then_inc(g_ready, 1)


def moe0_first_stage(nc, w, r, xn_dram, W1, y1_dram):
    RING = 4
    with ExitStack() as ctx:
        s = Scope(nc, ctx, "e1")
        w1 = s.sb("w1", [P, 3, HID])
        xg = s.sb("xg", [C0, RING, HG, D])
        xgT = s.sb("xgT", [P, 2, HG * C0])
        out = s.sb("out", [C0, 2, HG, HID])
        p_x = s.ps("p_x", [P, 2, 512])
        p_o = s.ps("p_o", [C0, 4, HID])
        w_in = [s.sem(f"w_in{i}") for i in range(3)]
        gathered = [s.sem(f"gathered{i}") for i in range(RING)]
        stored = [s.sem(f"stored{i}") for i in range(2)]
        turned = s.sem("turned")
        xT_ready = s.sem("xT_ready")
        product = s.sem("product")
        a_out = s.sem("a_out")
        v_out = s.sem("v_out")
        block = ctx.enter_context(nc.Block())

        @block.sync
        def _(sp):
            for e in range(E0 + 1):
                if e < E0:
                    if e >= 3:
                        sp.wait_ge(product, HG * (e - 2))
                    sp.dma_start(w1[:, e % 3, :], W1[e]).then_inc(w_in[e % 3], 16)
                if e:
                    f = e - 1
                    sp.wait_ge(a_out, 2 * (f + 1))
                    sp.wait_ge(v_out, 2 * (f + 1))
                    sp.dma_start(y1_dram[:, f, :, :].rearrange("h c n -> c h n"),
                                 out[:, f % 2, :, :]).then_inc(stored[f % 2], 16)
            for i in range(2):
                sp.wait_ge(stored[i], 16 * (E0 // 2))

        @block.gpsimd
        def _(pool):
            for e in range(E0):
                if e >= RING:
                    pool.wait_ge(turned, e - RING + 1)
                for h in range(HG):
                    nc.gpsimd.indirect_dma_start(
                        out=xg[:, e % RING, h, :], out_offset=None, in_=xn_dram,
                        in_offset=bass.IndirectOffsetOnAxis(ap=r.tab[:, h, e:e + 1], axis=0),
                    ).then_inc(gathered[e % RING], 16)

        @block.tensor
        def _(pe):
            def turn(e):
                pe.wait_ge(gathered[e % RING], 16 * HG * (e // RING + 1))
                if e >= 2:
                    pe.wait_ge(xT_ready, e - 1)
                for h in range(HG):
                    ins = nc.tensor.transpose(p_x[:, e % 2, h * C0:(h + 1) * C0], xg[:, e % RING, h, :],
                                              w["ident"][0:C0, 0:C0])
                ins.then_inc(turned, 1)

            turn(0)
            for e in range(E0):
                if e + 1 < E0:
                    turn(e + 1)
                pe.wait_ge(xT_ready, e + 1)
                pe.wait_ge(w_in[e % 3], 16 * (e // 3 + 1))
                for h in range(HG):
                    if e:
                        pe.wait_ge(a_out if h % 2 == 0 else v_out, 2 * (e - 1) + h // 2 + 1)
                    nc.tensor.matmul(p_o[:, h, :], xgT[:, e % 2, h * C0:(h + 1) * C0], w1[:, e % 3, :],
                                     start=True, stop=True).then_inc(product, 1)

        @block.scalar
        def _(act):
            def evacuate_x(e):
                act.wait_ge(turned, e + 1)
                if e >= 2:
                    act.wait_ge(product, HG * (e - 1))
                nc.scalar.activation(xgT[:, e % 2, :], p_x[:, e % 2, 0:HG * C0], ACT.Copy).then_inc(xT_ready, 1)

            evacuate_x(0)
            for e in range(E0):
                if e + 1 < E0:
                    evacuate_x(e + 1)
                if e >= 2:
                    act.wait_ge(stored[e % 2], 16 * (e // 2))
                for h in (0, 2):
                    act.wait_ge(product, HG * e + h + 1)
                    nc.scalar.activation(out[:, e % 2, h, :], p_o[:, h, :], ACT.Copy).then_inc(a_out, 1)

        @block.vector
        def _(dve):
            for e in range(E0):
                if e >= 2:
                    dve.wait_ge(stored[e % 2], 16 * (e // 2))
                for h in (1, 3):
                    dve.wait_ge(product, HG * e + h + 1)
                    nc.vector.tensor_copy(out[:, e % 2, h, :], p_o[:, h, :]).then_inc(v_out, 1)


def moe0_middle_stage(nc, w, r, y1_rows, r_dram):
    RING = 4
    with ExitStack() as ctx:
        s = Scope(nc, ctx, "e2")
        yk = s.sb("yk", [P, RING, 2, HID])
        hb = s.sb("hb", [P, RING, HID])
        ro = s.sb("ro", [P, RING, HID])
        stats = s.sb("stats", [P, NT, 6])
        mv = s.sb("mv", [P, NT, 2])
        rstd = s.sb("rstd", [P, NT])
        nm = s.sb("nm", [P, NT])
        p_b = s.ps("p_b", [P, 4, HID])
        gathered = [s.sem(f"gathered{i}") for i in range(RING)]
        stored = [s.sem(f"stored{i}") for i in range(RING)]
        chain = s.sem("chain")
        biased = s.sem("biased")
        combined = s.sem("combined")
        var_ready = s.sem("var_ready")
        root_ready = s.sem("root_ready")
        scale_ready = s.sem("scale_ready")
        centred = s.sem("centred")
        weighted = s.sem("weighted")
        r_ready = s.sem("r_ready")
        block = ctx.enter_context(nc.Block())

        @block.gpsimd
        def _(pool):
            for t in range(NT):
                if t >= RING:
                    pool.wait_ge(combined, t - RING + 1)
                for k in range(2):
                    nc.gpsimd.indirect_dma_start(
                        out=yk[:, t % RING, k, :], out_offset=None, in_=y1_rows,
                        in_offset=bass.IndirectOffsetOnAxis(ap=r.back[:, k, t:t + 1], axis=0),
                    ).then_inc(gathered[t % RING], 16)

        @block.tensor
        def _(pe):
            for t in range(NT):
                if t >= 4:
                    pe.wait_ge(combined, t - 3)
                nc.tensor.matmul(p_b[:, t % 4, :], r.GT[:, t * P:(t + 1) * P], w["b1_experts"], start=True,
                                 stop=True).then_inc(biased, 1)

        @block.vector
        def _(dve):
            link = Chain(dve, chain)
            v = nc.vector

            def combine(t):
                dve.wait_ge(gathered[t % RING], 32 * (t // RING + 1))
                dve.wait_ge(biased, t + 1)
                if t >= RING:
                    dve.wait_ge(centred, t - RING + 1)
                link(v.scalar_tensor_tensor(out=hb[:, t % RING, :], in0=yk[:, t % RING, 0, :],
                                            scalar=r.wk[:, 0, t:t + 1], in1=p_b[:, t % 4, :],
                                            op0=ALU.mult, op1=ALU.add))
                v.scalar_tensor_tensor(out=hb[:, t % RING, :], in0=yk[:, t % RING, 1, :], scalar=r.wk[:, 1, t:t + 1],
                                       in1=hb[:, t % RING, :], op0=ALU.mult, op1=ALU.add).then_inc(combined, 1)
                dve.wait_ge(combined, t + 1)
                link(v.bn_stats(stats[:, t, :], hb[:, t % RING, :]))
                link(v.bn_aggr(mv[:, t, :], stats[:, t, :]))
                v.tensor_scalar(nm[:, t:t + 1], mv[:, t, 1:2], 1e-6, None, ALU.add).then_inc(var_ready, 1)

            def scales(t):
                dve.wait_ge(root_ready, t + 1)
                link(v.reciprocal(rstd[:, t:t + 1], rstd[:, t:t + 1]))
                v.tensor_scalar(nm[:, t:t + 1], mv[:, t, 0:1], rstd[:, t:t + 1], -1.0, ALU.mult,
                                ALU.mult).then_inc(scale_ready, 1)

            def weigh(t):
                dve.wait_ge(centred, t + 1)
                ro_t = ro[:, t % RING, :]
                link(v.tensor_tensor(ro_t, ro_t, w["ln_w"][:, t % HG, :], ALU.mult))
                v.tensor_tensor(ro_t, ro_t, w["ln_b"][:, t % HG, :], ALU.add).then_inc(weighted, 1)

            for t in range(NT + 2):
                if t < NT:
                    combine(t)
                if 1 <= t <= NT:
                    scales(t - 1)
                if t >= 2:
                    weigh(t - 2)

        @block.scalar
        def _(act):
            for t in range(NT + 3):
                if t < NT:
                    act.wait_ge(var_ready, t + 1)
                    nc.scalar.activation(rstd[:, t:t + 1], nm[:, t:t + 1], ACT.Sqrt).then_inc(root_ready, 1)
                if 1 <= t <= NT:
                    n = t - 1
                    act.wait_ge(scale_ready, n + 1)
                    if n >= RING:
                        act.wait_ge(stored[n % RING], 16 * (n // RING))
                    nc.scalar.activation(ro[:, n % RING, :], hb[:, n % RING, :], ACT.Identity, scale=rstd[:, n:n + 1],
                                         bias=nm[:, n:n + 1]).then_inc(centred, 1)
                if t >= 3:
                    n = t - 3
                    act.wait_ge(weighted, n + 1)
                    nc.scalar.activation(ro[:, n % RING, :], ro[:, n % RING, :], ACT.Relu).then_inc(r_ready, 1)

        @block.sync
        def _(sp):
            for t in range(NT):
                sp.wait_ge(r_ready, t + 1)
                sp.dma_start(r_dram[:, t, :], ro[:, t % RING, :]).then_inc(stored[t % RING], 16)
            for i in range(RING):
                sp.wait_ge(stored[i], 16 * (NT // RING))


def moe0_second_stage(nc, w, r, r_rows, W2, y2_dram):
    RING = 3
    N = E0 * HG
    with ExitStack() as ctx:
        s = Scope(nc, ctx, "e3")
        w2 = s.sb("w2", [P, 3, FC, D])
        rg = s.sb("rg", [C0, RING, HG, HID])
        rT = s.sb("rT", [P, 3, FC * C0])
        out = s.sb("out", [C0, 2, HG, D])
        p_x = s.ps("p_x", [P, 3, 512])
        p_o = s.ps("p_o", [C0, 2, HG * D])
        w_in = [s.sem(f"w_in{i}") for i in range(3)]
        gathered = [s.sem(f"gathered{i}") for i in range(RING)]
        stored = [s.sem(f"stored{i}") for i in range(2)]
        turned = s.sem("turned")
        rT_ready = s.sem("rT_ready")
        product = s.sem("product")
        copied = s.sem("copied")
        block = ctx.enter_context(nc.Block())

        @block.sync
        def _(sp):
            for e in range(E0 + 1):
                if e < E0:
                    if e >= 3:
                        sp.wait_ge(product, HG * (e - 2))
                    sp.dma_start(w2[:, e % 3, :, :], W2[e].rearrange("(f p) d -> p f d", p=P)).then_inc(w_in[e % 3], 16)
                if e:
                    f = e - 1
                    sp.wait_ge(copied, f + 1)
                    sp.dma_start(y2_dram[:, f, :, :].rearrange("h c n -> c h n"),
                                 out[:, f % 2, :, :]).then_inc(stored[f % 2], 16)
            for i in range(2):
                sp.wait_ge(stored[i], 16 * (E0 // 2))

        @block.gpsimd
        def _(pool):
            for e in range(E0):
                if e >= RING:
                    pool.wait_ge(turned, HG * (e - RING + 1))
                for h in range(HG):
                    nc.gpsimd.indirect_dma_start(
                        out=rg[:, e % RING, h, :], out_offset=None, in_=r_rows,
                        in_offset=bass.IndirectOffsetOnAxis(ap=r.tab[:, h, e:e + 1], axis=0),
                    ).then_inc(gathered[e % RING], 16)

        @block.tensor
        def _(pe):
            def turn(n):
                e, h = divmod(n, HG)
                if h == 0:
                    pe.wait_ge(gathered[e % RING], 16 * HG * (e // RING + 1))
                if n >= 3:
                    pe.wait_ge(rT_ready, n - 2)
                for f in range(FC):
                    ins = nc.tensor.transpose(p_x[:, n % 3, f * C0:(f + 1) * C0], rg[:, e % RING, h, f * P:(f + 1) * P],
                                              w["ident"][0:C0, 0:C0])
                ins.then_inc(turned, 1)

            turn(0)
            turn(1)
            for n in range(N):
                e, h = divmod(n, HG)
                if n + 2 < N:
                    turn(n + 2)
                pe.wait_ge(rT_ready, n + 1)
                if h == 0:
                    pe.wait_ge(w_in[e % 3], 16 * (e // 3 + 1))
                    if e >= 2:
                        pe.wait_ge(copied, e - 1)
                for f in range(FC):
                    ins = nc.tensor.matmul(p_o[:, e % 2, h * D:(h + 1) * D], rT[:, n % 3, f * C0:(f + 1) * C0],
                                           w2[:, e % 3, f, :], start=(f == 0), stop=(f == FC - 1))
                ins.then_inc(product, 1)

        @block.scalar
        def _(act):
            for n in range(N):
                act.wait_ge(turned, n + 1)
                if n >= 3:
                    act.wait_ge(product, n - 2)
                nc.scalar.activation(rT[:, n % 3, :], p_x[:, n % 3, 0:FC * C0], ACT.Copy).then_inc(rT_ready, 1)

        @block.vector
        def _(dve):
            for e in range(E0):
                dve.wait_ge(product, HG * (e + 1))
                if e >= 2:
                    dve.wait_ge(stored[e % 2], 16 * (e // 2))
                nc.vector.tensor_copy(out[:, e % 2, :, :].rearrange("p a b -> p (a b)"),
                                      p_o[:, e % 2, :]).then_inc(copied, 1)


def moe0_output_stage(nc, w, r, y2_rows, xn_rows, s_rows, x_dram, x_rows):
    RING = 4
    with ExitStack() as ctx:
        s = Scope(nc, ctx, "e4")
        yk = s.sb("yk", [P, RING, 2, D])
        o = s.sb("o", [P, NT, D])
        sq = s.sb("sq", [P, 8, D])
        acc = s.sb("acc", [P, NT])
        var = s.sb("var", [P, NT])
        p_b = s.ps("p_b", [P, 4, D * TB])
        gathered = [s.sem(f"gathered{i}") for i in range(RING)]
        chain = s.sem("chain")
        x_in = s.sem("x_in")
        biased = s.sem("biased")
        combined = s.sem("combined")
        var_ready = s.sem("var_ready")
        root_ready = s.sem("root_ready")
        o_ready = s.sem("o_ready")
        g_ready = s.sem("g_ready")
        block = ctx.enter_context(nc.Block())

        @block.sync
        def _(sp):
            sp.dma_start(x_rows[:, :, :], x_dram).then_inc(x_in, 16)
            sp.wait_ge(x_in, 16)

        @block.gpsimd
        def _(pool):
            for t in range(NT):
                if t >= RING:
                    pool.wait_ge(combined, t - RING + 1)
                for k in range(2):
                    nc.gpsimd.indirect_dma_start(
                        out=yk[:, t % RING, k, :], out_offset=None, in_=y2_rows,
                        in_offset=bass.IndirectOffsetOnAxis(ap=r.back[:, k, t:t + 1], axis=0),
                    ).then_inc(gathered[t % RING], 16)

        @block.tensor
        def _(pe):
            for b in range(B):
                if b >= 4:
                    pe.wait_ge(combined, TB * (b - 3))
                for j in range(TB):
                    t = b * TB + j
                    ins = nc.tensor.matmul(p_b[:, b % 4, j * D:(j + 1) * D], r.GT[:, t * P:(t + 1) * P],
                                           w["b2_experts"], start=True, stop=True)
                ins.then_inc(biased, 1)

        @block.vector
        def _(dve):
            link = Chain(dve, chain)
            v = nc.vector
            for t in range(NT):
                b, j = divmod(t, TB)
                dve.wait_ge(gathered[t % RING], 32 * (t // RING + 1))
                dve.wait_ge(biased, b + 1)
                link(v.scalar_tensor_tensor(out=o[:, t, :], in0=yk[:, t % RING, 0, :], scalar=r.wk[:, 0, t:t + 1],
                                            in1=p_b[:, b % 4, j * D:(j + 1) * D], op0=ALU.mult, op1=ALU.add))
                v.scalar_tensor_tensor(out=o[:, t, :], in0=yk[:, t % RING, 1, :], scalar=r.wk[:, 1, t:t + 1],
                                       in1=o[:, t, :], op0=ALU.mult, op1=ALU.add).then_inc(combined, 1)
            dve.wait_ge(combined, NT)
            row_norm(nc, dve, link, o, xn_rows, sq, acc, var, 1e-6, var_ready, root_ready)
            for c in range(4):
                t = slice(c * 8, (c + 1) * 8)
                link(v.tensor_tensor(o[:, t, :], o[:, t, :], w["ln_out_w"][:, :].unsqueeze(1).broadcast_to([P, 8, D]),
                                     ALU.mult))
                v.tensor_tensor(o[:, t, :], o[:, t, :], w["ln_out_b"][:, :].unsqueeze(1).broadcast_to([P, 8, D]),
                                ALU.add).then_inc(o_ready, 1)
            dve.wait_ge(x_in, 16)
            for c in range(4):
                t = slice(c * 8, (c + 1) * 8)
                dve.wait_ge(g_ready, c + 1)
                link(v.tensor_tensor(o[:, t, :], o[:, t, :], s_rows[:, t, :], ALU.mult))
                link(v.tensor_tensor(x_rows[:, t, :], x_rows[:, t, :], o[:, t, :], ALU.add))

        @block.scalar
        def _(act):
            act.wait_ge(var_ready, 1)
            nc.scalar.activation(var[:, :], var[:, :], ACT.Sqrt).then_inc(root_ready, 1)
            for c in range(4):
                act.wait_ge(o_ready, c + 1)
                nc.scalar.activation(o[:, c * 8:(c + 1) * 8, :], o[:, c * 8:(c + 1) * 8, :], ACT.Silu).then_inc(g_ready, 1)


def row_norm(nc, dve, link, o, add, sq, acc, var, eps, var_ready, root_ready):
    v = nc.vector
    for c in range(4):
        t = slice(c * 8, (c + 1) * 8)
        link(v.tensor_tensor(o[:, t, :], o[:, t, :], add[:, t, :], ALU.add))
        link(v.tensor_reduce(acc[:, t], o[:, t, :], AX_X, ALU.add))
        link(v.tensor_scalar(acc[:, t], acc[:, t], -1.0 / D, None, ALU.mult))
        link(v.tensor_tensor(o[:, t, :], o[:, t, :], bcast(acc[:, t], D), ALU.add))
        link(v.tensor_tensor(sq[:, :, :], o[:, t, :], o[:, t, :], ALU.mult))
        link(v.tensor_reduce(var[:, t], sq[:, :, :], AX_X, ALU.add))
    v.tensor_scalar(var[:, :], var[:, :], 1.0 / D, eps, ALU.mult, ALU.add).then_inc(var_ready, 1)
    dve.wait_ge(root_ready, 1)
    link(v.reciprocal(var[:, :], var[:, :]))
    for c in range(4):
        t = slice(c * 8, (c + 1) * 8)
        link(v.tensor_tensor(o[:, t, :], o[:, t, :], bcast(var[:, t], D), ALU.mult))


NH = 8
SCALE = float(D) ** -0.5
SIM_AT = [(1, 384), (2, 0), (1, 0), (0, 0)]
PT_AT = [(0, 0), (1, 0), (2, 0), (1, 384)]


def attention_fold_stage(nc, w, xn_rows, xaT, M, N):
    with ExitStack() as ctx:
        s = Scope(nc, ctx, "af")
        sq = s.sb("sq", [P, 8, D])
        l2 = s.sb("l2", [P, NT])
        xa = s.sb("xa", [P, NT, D])
        qkv = s.sb("qkv", [P, 3 * NH, D])
        wo = s.sb("wo", [P, NH, D])
        p_w = s.ps("p_w", [P, 4, 512])
        p_x = s.ps("p_x", [P, 4, 512])
        w_in = s.sem("w_in")
        chain = s.sem("chain")
        summed = s.sem("summed")
        root_ready = s.sem("root_ready")
        xa_ready = s.sem("xa_ready")
        folded = s.sem("folded")
        fold_copied = s.sem("fold_copied")
        turned = s.sem("turned")
        xaT_ready = s.sem("xaT_ready")
        block = ctx.enter_context(nc.Block())

        @block.sync
        def _(sp):
            sp.dma_start(qkv[:, :, :], w["qkv_dram"]).then_inc(w_in, 16)
            sp.dma_start(wo[:, :, :], w["wo_dram"]).then_inc(w_in, 16)
            sp.wait_ge(w_in, 32)

        @block.tensor
        def _(pe):
            pe.wait_ge(w_in, 32)
            for n in range(4):
                for j in range(4):
                    h = (n % 2) * 4 + j
                    if n < 2:
                        ins = nc.tensor.matmul(p_w[:, n, j * D:(j + 1) * D], qkv[:, h, :], qkv[:, NH + h, :],
                                               start=True, stop=True)
                    else:
                        ins = nc.tensor.matmul(p_w[:, n, j * D:(j + 1) * D], qkv[:, 2 * NH + h, :], wo[:, h, :],
                                               start=True, stop=True)
                ins.then_inc(folded, 1)
            for b in range(B):
                pe.wait_ge(xa_ready, b // 2 + 1)
                if b >= 4:
                    pe.wait_ge(xaT_ready, b - 3)
                for j in range(TB):
                    ins = nc.tensor.transpose(p_x[:, b % 4, j * P:(j + 1) * P], xa[:, b * TB + j, :], w["ident"])
                ins.then_inc(turned, 1)

        @block.scalar
        def _(act):
            act.wait_ge(summed, 1)
            nc.scalar.activation(l2[:, :], l2[:, :], ACT.Sqrt).then_inc(root_ready, 1)
            for n in range(4):
                act.wait_ge(folded, n + 1)
                dst = (M if n < 2 else N)[:, (n % 2) * 512:(n % 2 + 1) * 512]
                nc.scalar.activation(dst, p_w[:, n, :], ACT.Copy, scale=SCALE if n < 2 else 1.0).then_inc(fold_copied, 1)
            for b in range(B):
                act.wait_ge(turned, b + 1)
                nc.scalar.activation(xaT[:, b, :], p_x[:, b % 4, :], ACT.Copy, scale=w["gamma"]).then_inc(xaT_ready, 1)

        @block.vector
        def _(dve):
            link = Chain(dve, chain)
            v = nc.vector
            for c in range(4):
                t = slice(c * 8, (c + 1) * 8)
                link(v.tensor_tensor(sq[:, :, :], xn_rows[:, t, :], xn_rows[:, t, :], ALU.mult))
                link(v.tensor_reduce(l2[:, t], sq[:, :, :], AX_X, ALU.add))
            v.memset(sq[:, 0, 0:1], 0.0).then_inc(summed, 1)
            dve.wait_ge(root_ready, 1)
            link(v.tensor_scalar(l2[:, :], l2[:, :], 1e-12, None, ALU.max))
            link(v.reciprocal(l2[:, :], l2[:, :]))
            link(v.tensor_scalar(l2[:, :], l2[:, :], float(D) ** 0.5, None, ALU.mult))
            for c in range(4):
                t = slice(c * 8, (c + 1) * 8)
                v.tensor_tensor(xa[:, t, :], xn_rows[:, t, :], bcast(l2[:, t], D), ALU.mult).then_inc(xa_ready, 1)


def attention_stage(nc, w, xaT, M, N, s_rows):
    NI = B * NH
    BANKS = [(3,), (2, 0), (1,)]
    with ExitStack() as ctx:
        s = Scope(nc, ctx, "at")
        qT = s.sb("qT", [P, 3, L])
        V = s.sb("V", [P, 2, TB, NH * D])
        pr = s.sb("pr", [P, 2, 3, 512])
        pT = s.sb("pT", [P, 2, 3, 512])
        mx = s.sb("mx", [P, 2, 4])
        nmx = s.sb("nmx", [P, 2, 4])
        sums = s.sb("sums", [P, 3, 4])
        p_s = s.ps("p_s", [P, 3, 512])
        p_t = s.ps("p_t", [P, 3, 512])
        p_o = s.ps("p_o", [P, 4, D])
        p_q = s.ps("p_q", [P, 512])
        chain = s.sem("chain")
        q_product = s.sem("q_product")
        q_copied = s.sem("q_copied")
        v_product = s.sem("v_product")
        v_copied = s.sem("v_copied")
        scores = s.sem("scores")
        maxed = s.sem("maxed")
        exped = s.sem("exped")
        turned = s.sem("turned")
        pT_ready = s.sem("pT_ready")
        out_ready = s.sem("out_ready")
        out_used = s.sem("out_used")
        block = ctx.enter_context(nc.Block())


        @block.tensor
        def _(pe):
            def query(n):
                b, h = divmod(n, NH)
                pe.wait_ge(v_copied, min(NH * B, NH + max(n - 2, 0)))
                if n:
                    pe.wait_ge(q_copied, n)
                nc.tensor.matmul(p_q[:, :], M[:, h * D:(h + 1) * D], xaT[:, b, :], start=True,
                                 stop=True).then_inc(q_product, 1)

            def value(k):
                b, i = divmod(k, NH)
                t, half = divmod(i, 2)
                if k:
                    pe.wait_ge(v_copied, k)
                if k >= NH:
                    pe.wait_ge(q_copied, min(NI, k - NH + 3))
                nc.tensor.matmul(p_q[:, :], xaT[:, b, t * P:(t + 1) * P], N[:, half * 512:(half + 1) * 512],
                                 start=True, stop=True).then_inc(v_product, 1)

            def score(n):
                b, h = divmod(n, NH)
                pe.wait_ge(q_copied, n + 1)
                for k, tiles in enumerate(BANKS):
                    if n:
                        pe.wait_ge(exped, 3 * (n - 1) + k + 1)
                    for i in tiles:
                        bank, c = SIM_AT[i]
                        K = (i + 1) * P
                        nc.tensor.matmul(p_s[:, bank, c:c + K], qT[:, n % 3, i * P:(i + 1) * P], xaT[:, b, 0:K],
                                         start=True, stop=False)
                        ins = nc.tensor.matmul(p_s[:, bank, c + i * P:c + K], w["ident_bf"], w["mask_bf"],
                                               start=False, stop=True)
                    ins.then_inc(scores, 1)

            def turn(n):
                pe.wait_ge(exped, 3 * (n + 1))
                for bank, keys in enumerate(((0,), (1, 3), (2,))):
                    if n:
                        pe.wait_ge(pT_ready, 3 * (n - 1) + bank + 1)
                    for j in keys:
                        c = PT_AT[j][1]
                        for i in range(j, TB):
                            sbank, sc = SIM_AT[i]
                            ins = nc.tensor.transpose(p_t[:, bank, c + (i - j) * P:c + (i - j + 1) * P],
                                                      pr[:, n % 2, sbank, sc + j * P:sc + (j + 1) * P], w["ident"])
                    ins.then_inc(turned, 1)

            def weigh(n):
                b, h = divmod(n, NH)
                pe.wait_ge(v_copied, NH * (b + 1))
                if n:
                    pe.wait_ge(out_used, n)
                pe.wait_ge(pT_ready, 3 * (n + 1))
                for i in range(TB):
                    for j in range(i + 1):
                        bank, c = PT_AT[j]
                        ins = nc.tensor.matmul(p_o[:, i, :], pT[:, n % 2, bank, c + (i - j) * P:c + (i - j + 1) * P],
                                               V[:, b % 2, j, h * D:(h + 1) * D], start=(j == 0), stop=(j == i))
                ins.then_inc(out_ready, 1)

            for k in range(NH):
                value(k)
            query(0)
            query(1)
            score(0)
            for n in range(NI):
                turn(n)
                if n + 2 < NI:
                    query(n + 2)
                if n + 1 < NI:
                    score(n + 1)
                if n + NH < NI:
                    value(n + NH)
                weigh(n)

        @block.scalar
        def _(act):
            def copy_query(n):
                act.wait_ge(q_product, n + 1)
                if n >= 3:
                    act.wait_ge(scores, 3 * (n - 2))
                nc.scalar.activation(qT[:, n % 3, :], p_q[:, :], ACT.Copy).then_inc(q_copied, 1)

            def copy_value(k):
                b, i = divmod(k, NH)
                t, half = divmod(i, 2)
                act.wait_ge(v_product, k + 1)
                if b >= 2:
                    act.wait_ge(out_ready, NH * (b - 1))
                nc.scalar.activation(V[:, b % 2, t, half * 512:(half + 1) * 512], p_q[:, :],
                                     ACT.Copy).then_inc(v_copied, 1)

            def exps(n):
                if n >= 2:
                    act.wait_ge(turned, 3 * (n - 1))
                if n >= 3:
                    act.wait_ge(out_used, n - 2)
                for k, tiles in enumerate(BANKS):
                    act.wait_ge(maxed, 3 * n + k + 1)
                    for i in tiles:
                        bank, c = SIM_AT[i]
                        K = (i + 1) * P
                        ins = nc.scalar.activation(pr[:, n % 2, bank, c:c + K], p_s[:, bank, c:c + K], ACT.Exp,
                                                   bias=nmx[:, n % 2, i:i + 1], accum_out=sums[:, n % 3, i:i + 1])
                    ins.then_inc(exped, 1)

            for k in range(NH):
                copy_value(k)
            copy_query(0)
            copy_query(1)
            for n in range(NI):
                exps(n)
                if n and n - 1 + NH < NI:
                    copy_value(n - 1 + NH)
                if n + 2 < NI:
                    copy_query(n + 2)

        @block.vector
        def _(dve):
            link = Chain(dve, chain)
            v = nc.vector

            def maxima(n):
                for k, tiles in enumerate(BANKS):
                    dve.wait_ge(scores, 3 * n + k + 1)
                    for i in tiles:
                        bank, c = SIM_AT[i]
                        link(v.tensor_reduce(mx[:, n % 2, i:i + 1], p_s[:, bank, c:c + (i + 1) * P], AX_X, ALU.max))
                        ins = v.tensor_scalar(nmx[:, n % 2, i:i + 1], mx[:, n % 2, i:i + 1], -1.0, None, ALU.mult)
                    ins.then_inc(maxed, 1)

            def add_head(n):
                b, h = divmod(n, NH)
                link(v.reciprocal(sums[:, n % 3, :], sums[:, n % 3, :]))
                dve.wait_ge(out_ready, n + 1)
                for i in range(TB):
                    o = s_rows[:, b * TB + i, :]
                    if h == 0:
                        ins = v.tensor_scalar(o, p_o[:, i, :], sums[:, n % 3, i:i + 1], None, ALU.mult)
                    else:
                        ins = v.scalar_tensor_tensor(out=o, in0=p_o[:, i, :], scalar=sums[:, n % 3, i:i + 1], in1=o,
                                                     op0=ALU.mult, op1=ALU.add)
                ins.then_inc(out_used, 1)

            maxima(0)
            for n in range(NI):
                for bank in range(3):
                    dve.wait_ge(turned, 3 * n + bank + 1)
                    cols = 512 if bank < 2 else 256
                    v.tensor_copy(pT[:, n % 2, bank, 0:cols], p_t[:, bank, 0:cols]).then_inc(pT_ready, 1)
                if n > 1:
                    dve.wait_ge(out_used, n - 1)
                if n:
                    add_head(n - 1)
                if n + 1 < NI:
                    maxima(n + 1)
            dve.wait_ge(out_used, NI - 1)
            add_head(NI - 1)


def moe1_expert_stage(nc, w, r, xn_dram, we_dram, y_dram):
    EG = 4
    NG = E1 // EG
    WG = 4
    RING = 4
    with ExitStack() as ctx:
        s = Scope(nc, ctx, "f1")
        we = s.sb("we", [P, 3, WG * EG, D])
        xg = s.sb("xg", [P, RING, D])
        xgT = s.sb("xgT", [P, 3, P])
        out = s.sb("out", [C1, RING, EG, D])
        p_x = s.ps("p_x", [P, 4, 512])
        p_o = s.ps("p_o", [C1, 4, EG * D])
        w_in = [s.sem(f"w_in{i}") for i in range(3)]
        gathered = [s.sem(f"gathered{i}") for i in range(RING)]
        stored = [s.sem(f"stored{i}") for i in range(RING)]
        turned = s.sem("turned")
        xT_ready = s.sem("xT_ready")
        product = s.sem("product")
        copied = s.sem("copied")
        block = ctx.enter_context(nc.Block())

        @block.sync
        def _(sp):
            def load(c):
                if c >= 3:
                    sp.wait_ge(product, WG * (c - 2))
                sp.dma_start(we[:, c % 3, :, :],
                             we_dram[c * WG * EG:(c + 1) * WG * EG].rearrange("e d f -> d e f")).then_inc(w_in[c % 3], 16)

            for g in range(NG):
                if g % WG == 0:
                    if g == 0:
                        load(0)
                        load(1)
                    if g // WG + 2 < NG // WG:
                        load(g // WG + 2)
                sp.wait_ge(copied, g + 1)
                sp.dma_start(y_dram[g * EG:(g + 1) * EG].rearrange("e c f -> c e f"),
                             out[:, g % RING, :, :]).then_inc(stored[g % RING], 16)
            for i in range(RING):
                sp.wait_ge(stored[i], 16 * (NG // RING))

        @block.gpsimd
        def _(pool):
            for g in range(NG):
                if g >= RING:
                    pool.wait_ge(turned, g - RING + 1)
                nc.gpsimd.indirect_dma_start(
                    out=xg[:, g % RING, :], out_offset=None, in_=xn_dram,
                    in_offset=bass.IndirectOffsetOnAxis(ap=r.tab[:, 0, g:g + 1], axis=0),
                ).then_inc(gathered[g % RING], 16)

        @block.tensor
        def _(pe):
            def turn(g):
                pe.wait_ge(gathered[g % RING], 16 * (g // RING + 1))
                if g >= 4:
                    pe.wait_ge(xT_ready, g - 3)
                nc.tensor.transpose(p_x[:, g % 4, 0:P], xg[:, g % RING, :], w["ident"]).then_inc(turned, 1)

            turn(0)
            turn(1)
            for g in range(NG):
                if g + 2 < NG:
                    turn(g + 2)
                pe.wait_ge(xT_ready, g + 1)
                pe.wait_ge(w_in[(g // WG) % 3], 16 * (g // WG // 3 + 1))
                if g >= 4:
                    pe.wait_ge(copied, g - 3)
                for j in range(EG):
                    ins = nc.tensor.matmul(p_o[:, g % 4, j * D:(j + 1) * D], xgT[:, g % 3, j * C1:(j + 1) * C1],
                                           we[:, (g // WG) % 3, (g % WG) * EG + j, :], start=True, stop=True)
                ins.then_inc(product, 1)

        @block.scalar
        def _(act):
            for g in range(NG):
                act.wait_ge(turned, g + 1)
                if g >= 3:
                    act.wait_ge(product, g - 2)
                nc.scalar.activation(xgT[:, g % 3, :], p_x[:, g % 4, 0:P], ACT.Copy).then_inc(xT_ready, 1)

        @block.vector
        def _(dve):
            for g in range(NG):
                dve.wait_ge(product, g + 1)
                if g >= RING:
                    dve.wait_ge(stored[g % RING], 16 * (g // RING))
                nc.vector.tensor_copy(out[:, g % RING, :, :].rearrange("p a b -> p (a b)"),
                                      p_o[:, g % 4, :]).then_inc(copied, 1)


def moe1_output_stage(nc, w, r, y_rows, s_rows, x_rows, out_dram, stored):
    RING = 4
    with ExitStack() as ctx:
        s = Scope(nc, ctx, "f2")
        yk = s.sb("yk", [P, RING, 2, D])
        o = s.sb("o", [P, NT, D])
        gathered = [s.sem(f"gathered{i}") for i in range(RING)]
        chain = s.sem("chain")
        scaled = s.sem("scaled")
        combined = s.sem("combined")
        g_ready = s.sem("g_ready")
        x_ready = s.sem("x_ready")
        block = ctx.enter_context(nc.Block())

        @block.gpsimd
        def _(pool):
            for t in range(NT):
                if t >= RING:
                    pool.wait_ge(combined, t - RING + 1)
                for k in range(2):
                    nc.gpsimd.indirect_dma_start(
                        out=yk[:, t % RING, k, :], out_offset=None, in_=y_rows,
                        in_offset=bass.IndirectOffsetOnAxis(ap=r.back[:, k, t:t + 1], axis=0),
                    ).then_inc(gathered[t % RING], 16)

        @block.vector
        def _(dve):
            link = Chain(dve, chain)
            v = nc.vector

            def update(c):
                t = slice(c * 8, (c + 1) * 8)
                dve.wait_ge(g_ready, c + 1)
                link(v.tensor_tensor(o[:, t, :], o[:, t, :], s_rows[:, t, :], ALU.mult))
                v.tensor_tensor(x_rows[:, t, :], x_rows[:, t, :], o[:, t, :], ALU.add).then_inc(x_ready, 1)

            for t in range(NT):
                dve.wait_ge(scaled, t + 1)
                v.scalar_tensor_tensor(out=o[:, t, :], in0=yk[:, t % RING, 1, :], scalar=r.wk[:, 1, t:t + 1],
                                       in1=o[:, t, :], op0=ALU.mult, op1=ALU.add).then_inc(combined, 1)
                if t % 8 == 4 and t > 8:
                    update(t // 8 - 1)
            update(3)

        @block.scalar
        def _(act):
            def gate(c):
                act.wait_ge(combined, 8 * (c + 1))
                nc.scalar.activation(o[:, c * 8:(c + 1) * 8, :], o[:, c * 8:(c + 1) * 8, :], ACT.Silu).then_inc(g_ready, 1)

            for t in range(NT):
                act.wait_ge(gathered[t % RING], 32 * (t // RING + 1))
                nc.scalar.activation(o[:, t, :], yk[:, t % RING, 0, :], ACT.Copy,
                                     scale=r.wk[:, 0, t:t + 1]).then_inc(scaled, 1)
                if t % 8 == 1 and t > 8:
                    gate(t // 8 - 1)
            gate(3)

        @block.sync
        def _(sp):
            for c in range(4):
                sp.wait_ge(x_ready, c + 1)
                sp.dma_start(out_dram[:, c * 8:(c + 1) * 8, :], x_rows[:, c * 8:(c + 1) * 8, :]).then_inc(stored, 16)
            sp.wait_ge(stored, 64)


def load_stage(nc, tag, pairs):
    with ExitStack() as ctx:
        s = Scope(nc, ctx, tag)
        loaded = s.sem("loaded")
        block = ctx.enter_context(nc.Block())

        @block.sync
        def _(sp):
            for dst, src in pairs:
                sp.dma_start(dst, src).then_inc(loaded, 16)
            sp.wait_ge(loaded, 16 * len(pairs))


def clear_semaphores(nc):
    released = sorted(int(n) for n in nc.released_uncleared_semaphores)
    with nc.Block() as block:
        @block.gpsimd
        def _(pool):
            first = released[0]
            for n, following in zip(released, released[1:] + [None]):
                if following != n + 1:
                    pool.sem_clear(range(first, n + 1))
                    first = following


def program(nc, a, out):
    with ExitStack() as top:
        G = Scope(nc, top, "g")

        def dram(name, shape):
            return nc.dram_tensor(name, shape, F32, kind="Internal").ap()

        xn_dram = dram("xn_scratch", [P, NT, D])
        y1_dram = dram("y1_scratch", [HG, E0, C0, HID])
        r_dram = dram("r_scratch", [P, NT, HID])
        y2_dram = dram("y2_scratch", [HG, E0, C0, D])
        xn1_dram = dram("xn1_scratch", [P, NT, D])
        y3_dram = dram("y3_scratch", [E1, C1, D])

        outputs_stored = G.sem("outputs_stored")
        w = {}

        def resident(scope, names):
            pairs = []
            for n in names:
                src = a[n]
                shape = list(src.shape)
                buf = scope.sb(n, [P] + shape[1:] if shape[0] == 1 else shape, src.dtype)
                whole = buf[tuple(slice(None) for _ in shape)]
                w[n] = whole
                flat = whole
                if shape[0] == 1:
                    if len(shape) == 3:
                        flat = whole.rearrange("p a b -> p (a b)")
                        src = src.rearrange("o a b -> o (a b)")
                    src = src.broadcast_to([P, src.shape[1]])
                pairs.append((flat, src))
            return pairs

        consts = resident(G, ["ident", "tri", "ones", "ident_bf", "mask_bf", "iota", "pcol", "group_base"])
        xn_rows = G.sb("xn_rows", [P, NT, D])
        s_rows = G.sb("s_rows", [P, NT, D])

        with ExitStack() as mamba:
            H = Scope(nc, mamba, "mamba")
            mw = resident(H, ["xproj_T", "dt_T", "dt_b", "A_log", "D", "sel", "out_T", "w1_T", "b1", "w2_T", "b2",
                              "norm1"])
            zT = H.sb("zT", [P, 2, N_TOK])
            with ExitStack() as scan:
                xT = Scope(nc, scan, "scan").sb("xT", [P, 2, N_TOK])
                with ExitStack() as inp:
                    I = Scope(nc, inp, "inp")
                    iw = resident(I, ["in_T", "conv_rows", "conv_b"])
                    xnT = I.sb("xnT", [P, B, PAD])
                    x_rows = I.sb("x_rows", [P, NT, D])
                    layernorm_stage(nc, a["x"], xn_dram, x_rows, xn_rows, xnT, w["ident"], "ln0", consts + iw + mw)
                    mamba_input_stage(nc, w, xnT, xT, zT)
                scan_stage(nc, w, xT, zT)
            mamba_output_stage(nc, w, zT, xn_rows, s_rows)

        rows = G.sb("rows", [P, NT, D])
        with ExitStack() as moe:
            F = Scope(nc, moe, "moe")
            r = Routing()
            r.tab = F.sb("tab", [C0, HG, E0], U32)
            r.back = F.sb("back", [P, 2, NT], U32)
            r.wk = F.sb("wk", [P, 2, NT])
            r.GT = F.sb("GT", [E0, N_TOK])
            fw = resident(F, ["wg0", "b1_experts", "b2_experts", "ln_w", "ln_b", "ln_out_w", "ln_out_b"])
            load_stage(nc, "fl", fw)
            with ExitStack() as rt:
                xnT = Scope(nc, rt, "rt").sb("xnT", [P, B, PAD])
                transpose_stage(nc, w, xn_rows, xnT)
                routing_stage(nc, w, r, xnT, w["wg0"],
                              dict(E=E0, C=C0, groups=HG, LO=C0, HI=E0, masked=True, floor=1e-9), "r0")
            moe0_first_stage(nc, w, r, xn_dram.rearrange("p t d -> (p t) d"), a["W1"], y1_dram)
            moe0_middle_stage(nc, w, r, y1_dram.rearrange("h e c n -> (h e c) n"), r_dram)
            moe0_second_stage(nc, w, r, r_dram.rearrange("p t n -> (p t) n"), a["W2"], y2_dram)
            moe0_output_stage(nc, w, r, y2_dram.rearrange("h e c n -> (h e c) n"), xn_rows, s_rows, a["x"], rows)

        clear_semaphores(nc)
        with ExitStack() as l1:
            H = Scope(nc, l1, "l1")
            r = Routing()
            r.tab = H.sb("tab", [P, 1, E1 // 4], U32)
            r.back = H.sb("back", [P, 2, NT], U32)
            r.wk = H.sb("wk", [P, 2, NT])
            r.GT = None
            l1w = resident(H, ["wg1", "gamma"])
            with ExitStack() as rt:
                xnT = Scope(nc, rt, "rt1").sb("xnT", [P, B, PAD])
                layernorm_stage(nc, None, xn1_dram, rows, xn_rows, xnT, w["ident"], "ln1", l1w)
                routing_stage(nc, w, r, xnT, w["wg1"],
                              dict(E=E1, C=C1, groups=1, LO=P, HI=E1 // 4, masked=False,
                                   floor=float(np.finfo(np.float32).eps)), "r1")
            w["qkv_dram"], w["wo_dram"] = a["qkv"], a["wo"]
            with ExitStack() as att:
                A_ = Scope(nc, att, "att")
                xaT = A_.sb("xaT", [P, B, L])
                M = A_.sb("M", [P, NH * D])
                N = A_.sb("N", [P, NH * D])
                attention_fold_stage(nc, w, xn_rows, xaT, M, N)
                attention_stage(nc, w, xaT, M, N, s_rows)
            moe1_expert_stage(nc, w, r, xn1_dram.rearrange("p t d -> (p t) d"), a["we"], y3_dram)
            moe1_output_stage(nc, w, r, y3_dram.rearrange("e c n -> (e c) n"), s_rows, rows, out, outputs_stored)


def transpose_stage(nc, w, xn_rows, xnT):
    with ExitStack() as ctx:
        s = Scope(nc, ctx, "tr")
        pt = s.ps("pt", [P, 4, L])
        turned = s.sem("turned")
        copied = s.sem("copied")
        block = ctx.enter_context(nc.Block())

        @block.tensor
        def _(pe):
            for b in range(B):
                if b >= 4:
                    pe.wait_ge(copied, b - 3)
                for j in range(TB):
                    ins = nc.tensor.transpose(pt[:, b % 4, j * P:(j + 1) * P], xn_rows[:, b * TB + j, :], w["ident"])
                ins.then_inc(turned, 1)

        @block.scalar
        def _(act):
            for b in range(B):
                act.wait_ge(turned, b + 1)
                nc.scalar.activation(xnT[:, b, KC - 1:PAD], pt[:, b % 4, :], ACT.Copy).then_inc(copied, 1)


def laid_out(i):

    c = np.ascontiguousarray
    bf16 = np.dtype("bfloat16")
    xp = i["L0_attn_x_proj_w"].T.reshape(HALF, P, DTR + 2 * DS).transpose(1, 0, 2)
    sel = np.zeros((96, 2 * DS, P), bf16)
    for row in range(96):
        sel[row, row % (2 * DS)] = 1
    qkv = i["L1_attn_w_qkv"].reshape(3 * NH, D, D).transpose(1, 0, 2)
    return {
        "x": c(i["L0_attn_Z"].reshape(NT, P, D).transpose(1, 0, 2)),
        "in_T": c(i["L0_attn_in_proj_w"].T),
        "conv_rows": c(i["L0_attn_conv_w"].T[None]),
        "conv_b": c(i["L0_attn_conv_b"].reshape(HALF, P).T),
        "xproj_T": c(np.concatenate([xp[:, :, DTR:]] * 3 + [xp[:, :, :DTR]], axis=2)),
        "dt_T": c(i["L0_attn_dt_proj_w"].T),
        "dt_b": c(i["L0_attn_dt_proj_b"].reshape(HALF, P).T),
        "A_log": c(i["L0_attn_A_log"].reshape(HALF, P, DS).transpose(1, 0, 2)),
        "D": c(i["L0_attn_D"].reshape(HALF, P).T),
        "out_T": c(i["L0_attn_out_proj_w"].T.reshape(HALF, P, D).transpose(1, 0, 2)),
        "w1_T": c(i["L0_attn_mlp_w1"].T),
        "b1": c(i["L0_attn_mlp_b1"].reshape(FC, P).T),
        "w2_T": c(i["L0_attn_mlp_w2"].T.reshape(FC, P, D).transpose(1, 0, 2)),
        "b2": c(i["L0_attn_mlp_b2"][None]),
        "norm1": c(i["L0_attn_norm1_w"][None]),
        "wg0": c(i["L0_ffn_Wg"]),
        "W1": c(i["L0_ffn_W1"]),
        "W2": c(i["L0_ffn_W2"]),
        "b1_experts": c(i["L0_ffn_b1"]),
        "b2_experts": c(i["L0_ffn_b2"]),
        "ln_w": c(i["L0_ffn_ln_hid_w"][None]),
        "ln_b": c(i["L0_ffn_ln_hid_b"][None]),
        "ln_out_w": c(i["L0_ffn_ln_out_w"][None]),
        "ln_out_b": c(i["L0_ffn_ln_out_b"][None]),
        "gamma": c(i["L1_attn_gamma"][:, None]),
        "qkv": c(qkv),
        "wo": c(i["L1_attn_w_out"].T.reshape(NH, D, D).transpose(1, 0, 2)),
        "wg1": c(i["L1_ffn_wg"]),
        "we": c(i["L1_ffn_we"]),
        "ident": np.eye(P, dtype=np.float32),
        "ident_bf": np.eye(P, dtype=np.float32).astype(bf16),
        "mask_bf": (np.triu(np.ones((P, P), np.float32), 1) * np.float32(-1e30)).astype(bf16),
        "tri": np.triu(np.ones((P, P), np.float32), 1).astype(bf16),
        "ones": np.ones((P, P), bf16),
        "iota": np.tile(np.arange(P, dtype=np.float32), (P, 1)),
        "pcol": np.arange(P, dtype=np.float32)[:, None].copy(),
        "group_base": np.tile(np.arange(HG, dtype=np.float32) * (E0 * C0), (P, 1)),
        "sel": c(sel.reshape(96, 2 * DS * P)),
    }


def kernel(**inputs):
    import concourse.bacc as bacc
    from concourse.bass_utils import run_bass_kernel_spmd

    nc = bacc.Bacc("TRN2", target_bir_lowering=False, num_devices=1)
    arrays = laid_out({n: np.asarray(v) for n, v in inputs.items()})
    a = {n: nc.dram_tensor(n, v.shape, mybir.dt.from_np(v.dtype), kind="ExternalInput").ap() for n, v in arrays.items()}
    out = nc.dram_tensor("out", (P, NT, D), F32, kind="ExternalOutput").ap()
    program(nc, a, out)
    r = run_bass_kernel_spmd(nc, [arrays], core_ids=[0])
    got = r.results[0]["out"]
    return np.ascontiguousarray(got.transpose(1, 0, 2)).reshape(B, L, D)
```

```python
from contextlib import ExitStack

import numpy as np
import concourse.bass as bass
from concourse import mybir

F32 = mybir.dt.float32
BF16 = mybir.dt.bfloat16
U32 = mybir.dt.uint32
ALU = mybir.AluOpType
ACT = mybir.ActivationFunctionType
AX_X = mybir.AxisListType.X

P = 128
B, L, D = 8, 512, 128
N_TOK = B * L
NT = N_TOK // P
TB = L // P
DI, DS, DTR, KC = 256, 16, 8, 4
HALF = DI // P
DFF = 512
FC = DFF // P
PAD = L + KC - 1

HG, E0, C0, HID = 4, 24, 86, 512
E1, C1 = 128, 32


class Chain:

    def __init__(self, eng, sem):
        self.eng, self.sem, self.n = eng, sem, 0

    def __call__(self, ins):
        self.n += 1
        ins.then_inc(self.sem, 1)
        self.eng.wait_ge(self.sem, self.n)
        return ins


class Scope:

    def __init__(self, nc, ctx, tag):
        self.nc, self.ctx, self.tag = nc, ctx, tag

    def sb(self, name, shape, dt=F32):
        return self.ctx.enter_context(self.nc.sbuf_tensor(f"{self.tag}_{name}", shape, dt))

    def ps(self, name, shape, dt=F32):
        return self.ctx.enter_context(self.nc.psum_tensor(f"{self.tag}_{name}", shape, dt))

    def sem(self, name):
        return self.ctx.enter_context(self.nc.semaphore(f"{self.tag}_{name}"))


class Arena:

    def __init__(self, buf):
        self.buf, self.used = buf, 0

    def sb(self, name, shape, dt=F32):
        per_row = int(np.prod(shape[1:]))
        words = -(-per_row * mybir.dt.size(dt) // 4)
        part = self.buf[0:shape[0], self.used:self.used + words]
        self.used += words
        assert self.used <= self.buf.shape[1], name
        if dt is not F32:
            part = part.bitcast(dt)[:, 0:per_row]
        dims = "abcd"[:len(shape) - 1]
        return part.rearrange(f"p ({' '.join(dims)}) -> p {' '.join(dims)}", **dict(zip(dims, shape[1:])))


def bcast(ap, n):
    return ap.unsqueeze(2).broadcast_to([ap.shape[0], ap.shape[1], n])


def layernorm_stage(nc, src_dram, xn_dram, x_rows, xn_rows, xnT, ident, tag, loads):
    G = 4
    steps = NT // G
    with ExitStack() as ctx:
        s = Scope(nc, ctx, tag)
        sums = s.sb("sums", [P, NT])
        nmean = s.sb("nmean", [P, NT])
        sq = s.sb("sq", [P, G, D])
        var = s.sb("var", [P, NT])
        rstd = s.sb("rstd", [P, NT])
        pt = s.ps("pt", [P, 4, L])
        x_in = s.sem("x_in")
        x_in2 = s.sem("x_in2")
        consts_in = s.sem("consts_in")
        chain = s.sem("chain")
        var_ready = s.sem("var_ready")
        rstd_ready = s.sem("rstd_ready")
        normed = s.sem("normed")
        turned = s.sem("turned")
        evacuated = s.sem("evacuated")
        stored = s.sem("stored")
        block = ctx.enter_context(nc.Block())

        @block.sync
        def _(sp):
            if src_dram is not None:
                for h in range(2):
                    sp.dma_start(x_rows[:, h * 16:(h + 1) * 16, :],
                                 src_dram[:, h * 16:(h + 1) * 16, :]).then_inc(x_in if h == 0 else x_in2, 16)
            for dst, src in loads:
                sp.dma_start(dst, src).then_inc(consts_in, 16)
            for g in range(steps):
                sp.wait_ge(normed, g + 1)
                sp.dma_start(xn_dram[:, g * G:(g + 1) * G, :], xn_rows[:, g * G:(g + 1) * G, :]).then_inc(stored, 16)
            sp.wait_ge(stored, 16 * steps)
            if loads:
                sp.wait_ge(consts_in, 16 * len(loads))

        @block.vector
        def _(dve):
            link = Chain(dve, chain)
            link(nc.vector.memset(xnT[:, :, 0:KC - 1], 0.0))
            for g in range(steps):
                t = slice(g * G, (g + 1) * G)
                if src_dram is not None and g == 0:
                    dve.wait_ge(x_in, 16)
                if src_dram is not None and g == steps // 2:
                    dve.wait_ge(x_in2, 16)
                link(nc.vector.tensor_reduce(sums[:, t], x_rows[:, t, :], AX_X, ALU.add))
                link(nc.vector.tensor_scalar(nmean[:, t], sums[:, t], -1.0 / D, None, ALU.mult))
                link(nc.vector.tensor_tensor(xn_rows[:, t, :], x_rows[:, t, :], bcast(nmean[:, t], D), ALU.add))
                link(nc.vector.tensor_tensor(sq[:, :, :], xn_rows[:, t, :], xn_rows[:, t, :], ALU.mult))
                link(nc.vector.tensor_reduce(var[:, t], sq[:, :, :], AX_X, ALU.add))
                nc.vector.tensor_scalar(var[:, t], var[:, t], 1.0 / D, 1e-5, ALU.mult, ALU.add).then_inc(var_ready, 1)
                dve.wait_ge(rstd_ready, g + 1)
                link(nc.vector.reciprocal(rstd[:, t], rstd[:, t]))
                nc.vector.tensor_tensor(xn_rows[:, t, :], xn_rows[:, t, :], bcast(rstd[:, t], D),
                                        ALU.mult).then_inc(normed, 1)

        @block.tensor
        def _(pe):
            if loads:
                pe.wait_ge(consts_in, 16 * len(loads))
            for g in range(steps):
                pe.wait_ge(normed, g + 1)
                if g >= 4:
                    pe.wait_ge(evacuated, g - 3)
                for j in range(G):
                    last = nc.tensor.transpose(pt[:, g % 4, j * P:(j + 1) * P], xn_rows[:, g * G + j, :], ident)
                last.then_inc(turned, 1)

        @block.scalar
        def _(act):
            for g in range(steps + 1):
                if g < steps:
                    t = slice(g * G, (g + 1) * G)
                    act.wait_ge(var_ready, g + 1)
                    nc.scalar.activation(rstd[:, t], var[:, t], ACT.Sqrt).then_inc(rstd_ready, 1)
                if g:
                    act.wait_ge(turned, g)
                    nc.scalar.activation(xnT[:, g - 1, KC - 1:PAD], pt[:, (g - 1) % 4, :],
                                         ACT.Copy).then_inc(evacuated, 1)


def mamba_input_stage(nc, w, xnT, xT, zT):
    with ExitStack() as ctx:
        s = Scope(nc, ctx, "mi")
        taps = s.sb("taps", [P, KC, DI])
        pj = s.ps("pj", [P, 8, L])
        chain = s.sem("chain")
        folded = s.sem("folded")
        product = s.sem("product")
        activated = s.sem("activated")
        block = ctx.enter_context(nc.Block())

        @block.vector
        def _(dve):
            for k in range(KC):
                nc.vector.tensor_tensor(taps[:, k, :], w["in_T"][:, 0:DI], w["conv_rows"][:, k, :],
                                        ALU.mult).then_inc(folded, 1)

        @block.tensor
        def _(pe):
            pe.wait_ge(folded, KC)
            for n in range(B * 4):
                b, e = divmod(n, 4)
                if n >= 8:
                    pe.wait_ge(activated, n - 7)
                if e < HALF:
                    for k in range(KC):
                        last = nc.tensor.matmul(pj[:, n % 8, :], taps[:, k, e * P:(e + 1) * P],
                                                xnT[:, b, k:k + L], start=(k == 0), stop=(k == KC - 1))
                else:
                    last = nc.tensor.matmul(pj[:, n % 8, :], w["in_T"][:, e * P:(e + 1) * P],
                                            xnT[:, b, KC - 1:PAD], start=True, stop=True)
                last.then_inc(product, 1)

        @block.scalar
        def _(act):
            for n in range(B * 4):
                b, e = divmod(n, 4)
                act.wait_ge(product, n + 1)
                if e < HALF:
                    nc.scalar.activation(xT[:, e, b * L:(b + 1) * L], pj[:, n % 8, :], ACT.Silu,
                                         bias=w["conv_b"][:, e:e + 1]).then_inc(activated, 1)
                else:
                    nc.scalar.activation(zT[:, e - HALF, b * L:(b + 1) * L], pj[:, n % 8, :],
                                         ACT.Silu).then_inc(activated, 1)


def side_by_side(main, beside):
    for _ in main:
        next(beside, None)
    for _ in beside:
        pass


PE_SLOTS, ACT_SLOTS = 4, 2


def scan_stage(nc, w, xT, zT, spare, beside):
    PAIRS = DS // 2
    STEPS = B * PAIRS
    with ExitStack() as ctx:
        s = Scope(nc, ctx, "sc")
        negA = s.sb("negA", [P, 2, DS])
        bc3 = s.sb("bc3", [96, 2, L], BF16)
        rest = spare.sb("rest", [96, L])
        mid = spare.sb("mid", [96, L], BF16)
        dtr = s.sb("dtr", [DTR, L])
        dt = s.sb("dt", [P, 2, 2, L])
        u = s.sb("u", [P, 2, 2, L])
        lost = spare.sb("lost", [P, L])
        logs = s.sb("logs", [P, 2, L])
        dA = s.sb("dA", [P, 4, 2, L])
        st = s.sb("st", [P, 4, 2, L])
        p_b = s.ps("p_b", [P, L])
        p_c = s.ps("p_c", [P, 2, L])
        p_y = s.ps("p_y", [P, 2, L])
        p_x = s.ps("p_x", [P, L])
        chain = s.sem("chain")
        a_chain = s.sem("a_chain")
        exp_A = s.sem("exp_A")
        neg_A = s.sem("neg_A")
        cleared = s.sem("cleared")
        xp_ready = s.sem("xp_ready")
        dr_copied = s.sem("dr_copied")
        bc_read = s.sem("bc_read")
        bc_done = s.sem("bc_done")
        dt_product = s.sem("dt_product")
        mag_read = s.sem("mag_read")
        relu_read = s.sem("relu_read")
        ln_ready = s.sem("ln_ready")
        dt_done = s.sem("dt_done")
        b_ready = s.sem("b_ready")
        b_used = s.sem("b_used")
        c_ready = s.sem("c_ready")
        hc_ready = s.sem("hc_ready")
        pair_added = s.sem("pair_added")
        hc_used = s.sem("hc_used")
        decay_ready = s.sem("decay_ready")
        scanned = s.sem("scanned")
        y_used = s.sem("y_used")
        gated = s.sem("gated")
        block = ctx.enter_context(nc.Block())

        def scalar_steps(act):
            link = Chain(act, a_chain)

            def copy_dt_rank(b):
                act.wait_ge(xp_ready, b + 1)
                if b:
                    act.wait_ge(dt_product, 2 * b)
                nc.scalar.activation(dtr[:, :], p_x[96:96 + DTR, :], ACT.Copy).then_inc(dr_copied, 1)

            def softplus_logs(b, h):
                n = 2 * b + h
                act.wait_ge(dt_product, n + 1)
                if n:
                    act.wait_ge(dt_done, n)
                if h == 0 and b >= 2:
                    act.wait_ge(gated, b - 1)
                nc.scalar.activation(lost[:, :], p_x[:, :], ACT.Abs, bias=w["dt_b"][:, h:h + 1]).then_inc(mag_read, 1)
                act.wait_ge(mag_read, n + 1)
                link(nc.scalar.activation(logs[:, 0, :], lost[:, :], ACT.Exp, scale=-1.0))
                nc.scalar.activation(logs[:, 1, :], logs[:, 0, :], ACT.Ln, bias=1.0).then_inc(ln_ready, 1)

            nc.scalar.activation(negA[:, :, :], w["A_log"][:, :, :], ACT.Exp).then_inc(exp_A, 1)
            copy_dt_rank(0)
            softplus_logs(0, 0)
            softplus_logs(0, 1)
            act.wait_ge(cleared, 1)
            act.wait_ge(neg_A, 1)

            def decays(i, h):
                b, q = divmod(i, PAIRS)
                m = 2 * i + h
                if q == 0:
                    act.wait_ge(dt_done, 2 * b + h + 1)
                if m >= 4:
                    act.wait_ge(scanned, m - 3)
                for j in range(2):
                    ins = nc.scalar.activation(dA[:, m % 4, j, 1:L], dt[:, b % 2, h, 1:L], ACT.Exp,
                                               scale=negA[:, h, 2 * q + j:2 * q + j + 1])
                ins.then_inc(decay_ready, 1)

            decays(0, 0)
            decays(0, 1)
            copy_dt_rank(1)
            for i in range(STEPS):
                b, q = divmod(i, PAIRS)
                if i + 1 < STEPS:
                    decays(i + 1, 0)
                yield
                if i + 1 < STEPS:
                    decays(i + 1, 1)
                yield
                if b + 1 < B:
                    if q == 1:
                        softplus_logs(b + 1, 0)
                    if q == 4:
                        softplus_logs(b + 1, 1)
                if b + 2 < B and q == 7:
                    copy_dt_rank(b + 2)

        def tensor_steps(pe):
            def x_project(b):
                if b:
                    pe.wait_ge(relu_read, 2 * b)
                for h in range(HALF):
                    ins = nc.tensor.matmul(p_x[0:96 + DTR, :], w["xproj_T"][:, h, :], xT[:, h, b * L:(b + 1) * L],
                                           start=(h == 0), stop=(h == 1))
                ins.then_inc(xp_ready, 1)

            def dt_project(b, h):
                n = 2 * b + h
                pe.wait_ge(dr_copied, b + 1)
                if h == 0:
                    pe.wait_ge(bc_read, b + 1)
                else:
                    pe.wait_ge(relu_read, n)
                nc.tensor.matmul(p_x[:, :], w["dt_T"][:, h * P:(h + 1) * P], dtr[:, :],
                                 start=True, stop=True).then_inc(dt_product, 1)

            def broadcast_b(i, j):
                b, q = divmod(i, PAIRS)
                if q == 0 and j == 0:
                    pe.wait_ge(bc_done, b + 1)
                if i or j:
                    pe.wait_ge(b_used, 2 * i + j)
                n = 2 * q + j
                nc.tensor.matmul(p_b[:, :], w["sel"][:, n * P:(n + 1) * P], bc3[:, b % 2, :], start=True,
                                 stop=True).then_inc(b_ready, 1)

            def broadcast_c(i):
                b, q = divmod(i, PAIRS)
                if i:
                    pe.wait_ge(hc_ready, 2 * i)
                for j in range(2):
                    n = DS + 2 * q + j
                    ins = nc.tensor.matmul(p_c[:, j, :], w["sel"][:, n * P:(n + 1) * P], bc3[:, b % 2, :],
                                           start=True, stop=True)
                ins.then_inc(c_ready, 1)

            def sum_states(i, h):
                b, q = divmod(i, PAIRS)
                if q == 0 and b and h == 0:
                    pe.wait_ge(y_used, b)
                pe.wait_ge(pair_added, 2 * i + h + 1)
                nc.tensor.matmul(p_y[:, h, :], w["ident"], st[:, (2 * i + h) % 4, 0, :],
                                 start=(q == 0), stop=(q == PAIRS - 1)).then_inc(hc_used, 1)

            x_project(0)
            dt_project(0, 0)
            dt_project(0, 1)
            x_project(1)
            broadcast_b(0, 0)
            for i in range(STEPS):
                b, q = divmod(i, PAIRS)
                broadcast_b(i, 1)
                yield
                if i + 1 < STEPS:
                    broadcast_b(i + 1, 0)
                if i:
                    sum_states(i - 1, 0)
                broadcast_c(i)
                yield
                if i:
                    sum_states(i - 1, 1)
                yield
                if b + 1 < B:
                    if q == 1:
                        dt_project(b + 1, 0)
                    if q == 3:
                        dt_project(b + 1, 1)
                if b + 2 < B and q == 7:
                    x_project(b + 2)
                yield
            sum_states(STEPS - 1, 0)
            sum_states(STEPS - 1, 1)

        def pool_steps(pool):
            def add_pair(i):
                for h in range(HALF):
                    m = 2 * i + h
                    pool.wait_ge(hc_ready, m + 1)
                    nc.gpsimd.tensor_tensor(st[:, m % 4, 0, :], st[:, m % 4, 0, :], st[:, m % 4, 1, :],
                                            ALU.add).then_inc(pair_added, 1)

            for i in range(STEPS):
                if i:
                    add_pair(i - 1)
                yield
            add_pair(STEPS - 1)

        def vector_steps(dve):
            link = Chain(dve, chain)
            dve.wait_ge(exp_A, 1)
            nc.vector.tensor_scalar(negA[:, :, :], negA[:, :, :], -1.0, None, ALU.mult).then_inc(neg_A, 1)
            nc.vector.memset(dA[:, :, :, 0:1], 0.0).then_inc(cleared, 1)

            def split_bc(b):
                dve.wait_ge(dr_copied, b + 1)
                hi = bc3[:, b % 2, :]
                link(nc.vector.tensor_copy(hi, p_x[0:96, :]))
                nc.vector.tensor_tensor(rest[:, :], p_x[0:96, :], hi, ALU.subtract).then_inc(bc_read, 1)
                dve.wait_ge(bc_read, b + 1)
                link(nc.vector.tensor_copy(mid[:, :], rest[:, :]))
                nc.vector.tensor_copy(bc3[32:64, b % 2, :], mid[32:64, :])
                nc.vector.tensor_tensor(bc3[64:96, b % 2, :], rest[64:96, :], mid[64:96, :],
                                        ALU.subtract).then_inc(bc_done, 1)
                dve.wait_ge(bc_done, b + 1)

            def relu(b, h):
                n = 2 * b + h
                dve.wait_ge(mag_read, n + 1)
                nc.vector.tensor_scalar(dt[:, b % 2, h, :], p_x[:, :], w["dt_b"][:, h:h + 1], 0.0,
                                        ALU.add, ALU.max).then_inc(relu_read, 1)

            def softplus(b, h):
                n = 2 * b + h
                em = logs[:, 0, :]
                dve.wait_ge(relu_read, n + 1)
                dve.wait_ge(ln_ready, n + 1)
                link(nc.vector.tensor_scalar(lost[:, :], em, 1.0, 1.0, ALU.add, ALU.subtract))
                link(nc.vector.tensor_tensor(lost[:, :], em, lost[:, :], ALU.subtract))
                link(nc.vector.tensor_tensor(lost[:, :], lost[:, :], logs[:, 1, :], ALU.add))
                nc.vector.tensor_tensor(dt[:, b % 2, h, :], dt[:, b % 2, h, :], lost[:, :], ALU.add).then_inc(dt_done, 1)
                dve.wait_ge(dt_done, n + 1)
                link(nc.vector.tensor_tensor(u[:, b % 2, h, :], dt[:, b % 2, h, :], xT[:, h, b * L:(b + 1) * L],
                                             ALU.mult))

            def gate(b):
                cols = slice(b * L, (b + 1) * L)
                dve.wait_ge(hc_used, 2 * PAIRS * (b + 1))
                for h in range(HALF):
                    ins = nc.vector.scalar_tensor_tensor(out=logs[:, h, :], in0=xT[:, h, cols],
                                                         scalar=w["D"][:, h:h + 1], in1=p_y[:, h, :],
                                                         op0=ALU.mult, op1=ALU.add)
                ins.then_inc(y_used, 1)
                dve.wait_ge(y_used, b + 1)
                for h in range(HALF):
                    ins = nc.vector.tensor_tensor(zT[:, h, cols], logs[:, h, :], zT[:, h, cols], ALU.mult)
                ins.then_inc(gated, 1)

            def times_b(i, j):
                b, q = divmod(i, PAIRS)
                dve.wait_ge(b_ready, 2 * i + j + 1)
                for h in range(HALF):
                    m = 2 * i + h
                    if m >= 4 and j == 0:
                        dve.wait_ge(hc_used, m - 3)
                    ins = nc.vector.tensor_tensor(st[:, m % 4, j, :], p_b[:, :], u[:, b % 2, h, :], ALU.mult)
                ins.then_inc(b_used, 1)

            def times_c(i, h):
                m = 2 * i + h
                dve.wait_ge(c_ready, i + 1)
                dve.wait_ge(scanned, m + 1)
                nc.vector.tensor_tensor(st[:, m % 4, :, :], st[:, m % 4, :, :], p_c[:, :, :],
                                        ALU.mult).then_inc(hc_ready, 1)

            split_bc(0)
            for h in range(HALF):
                relu(0, h)
                softplus(0, h)
            for i in range(STEPS):
                b, q = divmod(i, PAIRS)
                if q == 1 and b:
                    gate(b - 1)
                times_b(i, 0)
                if i:
                    times_c(i - 1, 0)
                times_b(i, 1)
                if i:
                    times_c(i - 1, 1)
                dve.wait_ge(b_used, 2 * i + 2)
                for h in range(HALF):
                    m = 2 * i + h
                    dve.wait_ge(decay_ready, m + 1)
                    nc.vector.tensor_tensor_scan(st[:, m % 4, :, :].rearrange("p a b -> p (a b)"),
                                                 dA[:, m % 4, :, :].rearrange("p a b -> p (a b)"),
                                                 st[:, m % 4, :, :].rearrange("p a b -> p (a b)"),
                                                 0.0, ALU.mult, ALU.add).then_inc(scanned, 1)
                if b + 1 < B:
                    if q == 0:
                        split_bc(b + 1)
                    if q in (2, 5):
                        relu(b + 1, (q - 2) // 3)
                    if q in (3, 6):
                        softplus(b + 1, (q - 3) // 3)
                yield
            times_c(STEPS - 1, 0)
            times_c(STEPS - 1, 1)
            gate(B - 1)

        @block.scalar
        def _(act):
            side_by_side(scalar_steps(act), beside.scalar(act))

        @block.tensor
        def _(pe):
            side_by_side(tensor_steps(pe), beside.tensor(pe))

        @block.gpsimd
        def _(pool):
            side_by_side(pool_steps(pool), beside.pool(pool))

        @block.vector
        def _(dve):
            side_by_side(vector_steps(dve), beside.vector(dve))

        @block.sync
        def _(sp):
            beside.sync(sp)


def mamba_output_stage(nc, w, yT, xn_rows, s_rows):
    with ExitStack() as ctx:
        s = Scope(nc, ctx, "mo")
        z = s.sb("z", [P, NT, D])
        zT = s.sb("zT", [P, 2, L])
        hT = s.sb("hT", [P, 2, FC, L])
        sq = s.sb("sq", [P, TB, D])
        acc = s.sb("acc", [P, NT])
        root = s.sb("root", [P, NT])
        p_o = s.ps("p_o", [P, L])
        p_t = s.ps("p_t", [P, 2, L])
        p_h = s.ps("p_h", [P, 4, L])
        p_m = s.ps("p_m", [P, L])
        chain = s.sem("chain")
        projected = s.sem("projected")
        o_used = s.sem("o_used")
        mean_ready = s.sem("mean_ready")
        root_ready = s.sem("root_ready")
        z_ready = s.sem("z_ready")
        z_turned = s.sem("z_turned")
        zT_ready = s.sem("zT_ready")
        h_product = s.sem("h_product")
        h_ready = s.sem("h_ready")
        m_product = s.sem("m_product")
        m_used = s.sem("m_used")
        block = ctx.enter_context(nc.Block())

        @block.tensor
        def _(pe):
            for b in range(B):
                if b:
                    pe.wait_ge(o_used, b)
                for j in range(TB):
                    for h in range(HALF):
                        ins = nc.tensor.matmul(p_o[:, j * D:(j + 1) * D], yT[:, h, b * L + j * P:b * L + (j + 1) * P],
                                               w["out_T"][:, h, :], start=(h == 0), stop=(h == 1))
                ins.then_inc(projected, 1)

            def hidden(b):
                pe.wait_ge(z_ready, b + 1)
                if b >= 2:
                    pe.wait_ge(zT_ready, b - 1)
                for j in range(TB):
                    ins = nc.tensor.transpose(p_t[:, b % 2, j * P:(j + 1) * P], z[:, b * TB + j, :], w["ident"])
                ins.then_inc(z_turned, 1)
                pe.wait_ge(zT_ready, b + 1)
                for f in range(FC):
                    n = FC * b + f
                    if n >= 4:
                        pe.wait_ge(h_ready, n - 3)
                    nc.tensor.matmul(p_h[:, n % 4, :], w["w1_T"][:, f * P:(f + 1) * P], zT[:, b % 2, :],
                                     start=True, stop=True).then_inc(h_product, 1)

            hidden(0)
            for b in range(B):
                if b + 1 < B:
                    hidden(b + 1)
                pe.wait_ge(h_ready, FC * (b + 1))
                if b:
                    pe.wait_ge(m_used, b)
                for j in range(TB):
                    for f in range(FC):
                        ins = nc.tensor.matmul(p_m[:, j * D:(j + 1) * D], hT[:, b % 2, f, j * P:(j + 1) * P],
                                               w["w2_T"][:, f, :], start=(f == 0), stop=(f == FC - 1))
                ins.then_inc(m_product, 1)

        @block.scalar
        def _(act):
            for b in range(B):
                act.wait_ge(mean_ready, b + 1)
                t = slice(b * TB, (b + 1) * TB)
                nc.scalar.activation(root[:, t], acc[:, t], ACT.Sqrt).then_inc(root_ready, 1)
            for b in range(B):
                act.wait_ge(z_turned, b + 1)
                if b >= 2:
                    act.wait_ge(h_product, FC * (b - 1))
                nc.scalar.activation(zT[:, b % 2, :], p_t[:, b % 2, :], ACT.Copy).then_inc(zT_ready, 1)
                for f in range(FC):
                    n = FC * b + f
                    act.wait_ge(h_product, n + 1)
                    if b >= 2 and f == 0:
                        act.wait_ge(m_product, b - 1)
                    nc.scalar.activation(hT[:, b % 2, f, :], p_h[:, n % 4, :], ACT.Gelu,
                                         bias=w["b1"][:, f:f + 1]).then_inc(h_ready, 1)
            act.wait_ge(mean_ready, B + 1)
            nc.scalar.activation(root[:, :], acc[:, :], ACT.Sqrt).then_inc(root_ready, 1)

        @block.vector
        def _(dve):
            link = Chain(dve, chain)

            def rows(p):
                return p[:, :].rearrange("p (a d) -> p a d", d=D)

            def squares(v, t):
                link(nc.vector.tensor_tensor(sq[:, :, :], v, v, ALU.mult))
                link(nc.vector.tensor_reduce(acc[:, t], sq[:, :, :], AX_X, ALU.add))

            def scale(v, t, signal):
                n = t.stop - t.start
                link(nc.vector.reciprocal(root[:, t], root[:, t]))
                link(nc.vector.tensor_tensor(v, v, bcast(root[:, t], D), ALU.mult))
                ins = nc.vector.tensor_tensor(v, v, w["norm1"][:, :].unsqueeze(1).broadcast_to([P, n, D]), ALU.mult)
                if signal is None:
                    link(ins)
                else:
                    ins.then_inc(signal, 1)

            for b in range(B + 1):
                if b < B:
                    t = slice(b * TB, (b + 1) * TB)
                    dve.wait_ge(projected, b + 1)
                    nc.vector.tensor_tensor(z[:, t, :], rows(p_o), xn_rows[:, t, :], ALU.add).then_inc(o_used, 1)
                    dve.wait_ge(o_used, b + 1)
                    squares(z[:, t, :], t)
                    nc.vector.tensor_scalar(acc[:, t], acc[:, t], 1.0 / D, 1e-6, ALU.mult,
                                            ALU.add).then_inc(mean_ready, 1)
                if b:
                    dve.wait_ge(root_ready, b)
                    t = slice((b - 1) * TB, b * TB)
                    scale(z[:, t, :], t, z_ready)
            dve.wait_ge(z_ready, B)
            for b in range(B):
                t = slice(b * TB, (b + 1) * TB)
                link(nc.vector.tensor_tensor(s_rows[:, t, :], z[:, t, :],
                                             w["b2"][:, :].unsqueeze(1).broadcast_to([P, TB, D]), ALU.add))
                dve.wait_ge(m_product, b + 1)
                nc.vector.tensor_tensor(s_rows[:, t, :], rows(p_m), s_rows[:, t, :], ALU.add).then_inc(m_used, 1)
                dve.wait_ge(m_used, b + 1)
                squares(s_rows[:, t, :], t)
            nc.vector.tensor_scalar(acc[:, :], acc[:, :], 1.0 / D, 1e-6, ALU.mult, ALU.add).then_inc(mean_ready, 1)
            dve.wait_ge(root_ready, B + 1)
            scale(s_rows[:, :, :], slice(0, NT), None)


class Routing:
    pass


GT_BATCHES = 3


def gate_rows(GT, t, n=1):
    stripe, at = divmod(t, GT_BATCHES * TB)
    return GT[32 * stripe:32 * stripe + E0, at * P:(at + n) * P]


def expert_biases(b, t):
    stripe = t // (GT_BATCHES * TB)
    return b[32 * stripe:32 * stripe + E0, :]


def routing_stage(nc, w, r, xnT, wg, cfg, tag, scratch):
    E, C, groups, LO, HI, masked_first, floor = (cfg[x] for x in ("E", "C", "groups", "LO", "HI", "masked", "floor"))
    steps = NT // groups
    width = groups * E
    TC = 16 if E < 32 else 4
    NCH = NT // TC
    split = HI < E
    with ExitStack() as ctx:
        s = Scope(nc, ctx, tag)
        lg = scratch.sb("lg", [P, NT, E])
        ex = scratch.sb("ex", [P, NT, E])
        mx = scratch.sb("mx", [P, NT, 8])
        ix = scratch.sb("ix", [P, NT, 8], U32)
        idx = scratch.sb("idx", [P, 2, NT])
        lo_e = scratch.sb("lo_e", [P, 2, NT])
        hi_e = scratch.sb("hi_e", [P, 2, NT])
        bits = scratch.sb("bits", [P, 2, NT], U32)
        m = [scratch.sb(f"m{k}", [P, NT, E], BF16) for k in range(2)]
        acc = [scratch.sb(f"acc{k}", [P, steps + 1, width], BF16) for k in range(2)]
        mh = scratch.sb("mh", [P, NT, HI], BF16)
        loc = scratch.sb("loc", [P, 2, NT])
        valid = scratch.sb("valid", [P, 2, NT])
        lo = scratch.sb("lo", [P, 2, NT])
        A = [scratch.sb(f"A{k}", [P, NT, LO], BF16) for k in range(2)]
        R = [scratch.sb(f"R{k}", [P, NT, 2, HI], BF16) for k in range(2)]
        S = scratch.sb("S", [P, NT])
        d21 = scratch.sb("d21", [P, NT])
        g = scratch.sb("g", [P, 2, NT])
        den = scratch.sb("den", [P, NT])
        rows = scratch.sb("rows", [P, 2, NT])
        tabf = scratch.sb("tabf", [LO, groups, HI])
        p_l = s.ps("p_l", [P, 4, 512])
        p_n = s.ps("p_n", [P, 2, 512])
        p_t = s.ps("p_t", [LO, 512])
        chain = s.sem("chain")
        logits = s.sem("logits")
        logits_used = s.sem("logits_used")
        masks = s.sem("masks")
        counted = s.sem("counted")
        count_used = s.sem("count_used")
        shifted = s.sem("shifted")
        exps = s.sem("exps")
        onehots = s.sem("onehots")
        table = s.sem("table")
        back_ready = s.sem("back_ready")
        g_ready = s.sem("g_ready")
        g_turned = s.sem("g_turned")
        g_copied = s.sem("g_copied")
        block = ctx.enter_context(nc.Block())

        @block.tensor
        def _(pe):
            for t in range(NT):
                c, j = divmod(t, TC)
                b, q = divmod(t, TB)
                if j == 0 and c >= 4:
                    pe.wait_ge(logits_used, c - 3)
                ins = nc.tensor.matmul(p_l[:, c % 4, j * E:(j + 1) * E],
                                       xnT[:, b, KC - 1 + q * P:KC - 1 + (q + 1) * P], wg, start=True, stop=True)
                if j == TC - 1:
                    ins.then_inc(logits, 1)
            pe.wait_ge(masks, 1)
            for k in range(2):
                for c in range(NCH):
                    n = k * NCH + c
                    if n >= 2:
                        pe.wait_ge(count_used, n - 1)
                    cols = TC * E
                    steps_c = TC // groups
                    out = p_n[:, n % 2, 0:cols]
                    nc.tensor.matmul(out, w["tri"], m[k][:, c * TC:(c + 1) * TC, :].rearrange("p a b -> p (a b)"),
                                     start=True, stop=False)
                    last = k == 0
                    ins = nc.tensor.matmul(out, w["ones"],
                                           acc[k][:, c * steps_c:(c + 1) * steps_c, :].rearrange("p a b -> p (a b)"),
                                           start=False, stop=last)
                    if k:
                        total = acc[0][:, steps:steps + 1, :].broadcast_to([P, steps_c, width])
                        ins = nc.tensor.matmul(out, w["ones"], total, start=False, stop=True)
                    ins.then_inc(counted, 1)
            pe.wait_ge(onehots, 1)
            for h in range(groups):
                for i in range(steps):
                    t = i * groups + h
                    for k in range(2):
                        ins = nc.tensor.matmul(p_t[:, h * 2 * HI:(h + 1) * 2 * HI], A[k][:, t, :],
                                               R[k][:, t, :, :].rearrange("p a b -> p (a b)"),
                                               start=(i == 0 and k == 0), stop=(i == steps - 1 and k == 1))
            ins.then_inc(table, 1)
            if r.GT is not None:
                pe.wait_ge(g_ready, 1)
                for b in range(B):
                    if b >= 2:
                        pe.wait_ge(g_copied, b - 1)
                    for j in range(TB):
                        ins = nc.tensor.transpose(p_l[0:E, b % 2, j * P:(j + 1) * P], ex[:, b * TB + j, :], w["ident"])
                    ins.then_inc(g_turned, 1)

        @block.scalar
        def _(act):
            act.wait_ge(shifted, 1)
            nc.scalar.activation(lg[:, :, :], ex[:, :, :], ACT.Exp).then_inc(exps, 1)
            nc.scalar.activation(d21[:, :], d21[:, :], ACT.Exp).then_inc(exps, 1)
            if r.GT is not None:
                for b in range(B):
                    act.wait_ge(g_turned, b + 1)
                    nc.scalar.activation(gate_rows(r.GT, b * TB, TB), p_l[0:E, b % 2, :], ACT.Copy).then_inc(g_copied, 1)

        @block.vector
        def _(dve):
            link = Chain(dve, chain)
            v = nc.vector
            for c in range(NCH):
                dve.wait_ge(logits, c + 1)
                v.tensor_copy(lg[:, c * TC:(c + 1) * TC, :],
                              p_l[:, c % 4, 0:TC * E].rearrange("p (a b) -> p a b", b=E)).then_inc(logits_used, 1)
            dve.wait_ge(logits_used, NCH)
            for t in range(NT):
                ins = v.max(mx[:, t, :], lg[:, t, :])
            link(ins)
            for t in range(NT):
                ins = v.max_index(ix[:, t, :], mx[:, t, :], lg[:, t, :])
            link(ins)
            v.tensor_tensor(d21[:, :], mx[:, :, 1], mx[:, :, 0], ALU.subtract)
            v.tensor_tensor(ex[:, :, :], lg[:, :, :], bcast(mx[:, :, 0], E), ALU.subtract).then_inc(shifted, 1)
            for k in range(2):
                link(v.tensor_copy(idx[:, k, :], ix[:, :, k]))
            for k in range(2):
                v.tensor_tensor(m[k][:, :, :], w["iota"][:, 0:E].unsqueeze(1).broadcast_to([P, NT, E]),
                                bcast(idx[:, k, :], E), ALU.is_equal)
                link(v.memset(acc[k][:, 0, :], 0.0))
            for i in range(steps):
                for k in range(2):
                    ins = v.tensor_tensor(acc[k][:, i + 1, :], acc[k][:, i, :],
                                          m[k][:, i * groups:(i + 1) * groups, :].rearrange("p a b -> p (a b)"), ALU.add)
                link(ins)
            v.memset(den[:, :], 0.0).then_inc(masks, 1)
            if split:
                for k in range(2):
                    link(v.tensor_single_scalar(bits[:, k, :], ix[:, :, k], 2, ALU.logical_shift_right))
                    link(v.tensor_copy(hi_e[:, k, :], bits[:, k, :]))
                    link(v.tensor_single_scalar(bits[:, k, :], ix[:, :, k], 3, ALU.bitwise_and))
                    link(v.tensor_copy(lo_e[:, k, :], bits[:, k, :]))
            dve.wait_ge(exps, 2)
            link(v.tensor_reduce(S[:, :], lg[:, :, :], AX_X, ALU.add))
            link(v.reciprocal(g[:, 0, :], S[:, :]))
            link(v.tensor_tensor(g[:, 1, :], d21[:, :], g[:, 0, :], ALU.mult))
            for k in range(2):
                for c in range(NCH):
                    n = k * NCH + c
                    dve.wait_ge(counted, n + 1)
                    t = slice(c * TC, (c + 1) * TC)
                    v.tensor_tensor(ex[:, t, :], p_n[:, n % 2, 0:TC * E].rearrange("p (a b) -> p a b", b=E),
                                    m[k][:, t, :], ALU.mult).then_inc(count_used, 1)
                dve.wait_ge(count_used, (k + 1) * NCH)
                link(v.tensor_reduce(loc[:, k, :], ex[:, :, :], AX_X, ALU.add))
            link(v.tensor_scalar(valid[:, :, :], loc[:, :, :], float(C), None, ALU.is_lt))
            if split:
                link(v.scalar_tensor_tensor(out=lo[:, :, :], in0=lo_e[:, :, :], scalar=float(C), in1=loc[:, :, :],
                                            op0=ALU.mult, op1=ALU.add))
                link(v.tensor_tensor(lo[:, :, :], lo[:, :, :], valid[:, :, :], ALU.mult))
                link(v.tensor_scalar(rows[:, :, :], valid[:, :, :], -1000.0, 1000.0, ALU.mult, ALU.add))
                link(v.tensor_tensor(lo[:, :, :], lo[:, :, :], rows[:, :, :], ALU.add))
            low, high = (lo, hi_e) if split else (loc, idx)
            for k in range(2):
                link(v.tensor_tensor(A[k][:, :, :], w["iota"][:, 0:LO].unsqueeze(1).broadcast_to([P, NT, LO]),
                                     bcast(low[:, k, :], LO), ALU.is_equal))
                if split:
                    link(v.tensor_tensor(mh[:, :, :], w["iota"][:, 0:HI].unsqueeze(1).broadcast_to([P, NT, HI]),
                                         bcast(high[:, k, :], HI), ALU.is_equal))
                pick = mh if split else m[k]
                v.tensor_scalar(R[k][:, :, 0, :], pick[:, :, :], w["pcol"], None, ALU.mult)
                link(v.tensor_tensor(R[k][:, :, 1, :], pick[:, :, :], bcast(w["iota"][:, 0:NT], HI), ALU.mult))
            v.memset(S[:, :], 0.0).then_inc(onehots, 1)
            link(v.scalar_tensor_tensor(out=rows[:, :, :], in0=idx[:, :, :], scalar=float(C), in1=loc[:, :, :],
                                        op0=ALU.mult, op1=ALU.add))
            link(v.tensor_tensor(rows[:, :, :], rows[:, :, :], valid[:, :, :], ALU.mult))
            if groups > 1:
                for k in range(2):
                    ins = v.tensor_tensor(rows[:, k, :].rearrange("p (a b) -> p a b", b=groups),
                                          rows[:, k, :].rearrange("p (a b) -> p a b", b=groups),
                                          w["group_base"][:, 0:groups].unsqueeze(1).broadcast_to([P, steps, groups]),
                                          ALU.add)
                link(ins)
            link(v.tensor_copy(r.back[:, :, :], rows[:, :, :]))
            if masked_first:
                link(v.tensor_tensor(g[:, :, :], g[:, :, :], valid[:, :, :], ALU.mult))
            link(v.tensor_tensor(den[:, :], g[:, 0, :], g[:, 1, :], ALU.add))
            link(v.tensor_scalar(den[:, :], den[:, :], floor, None, ALU.max))
            link(v.reciprocal(den[:, :], den[:, :]))
            for k in range(2):
                link(v.tensor_tensor(r.wk[:, k, :], g[:, k, :], den[:, :], ALU.mult))
            if not masked_first:
                link(v.tensor_tensor(r.wk[:, :, :], r.wk[:, :, :], valid[:, :, :], ALU.mult))
            dve.wait_ge(table, 1)
            pt = p_t[:, 0:groups * 2 * HI].rearrange("p (h a c) -> p h a c", h=groups, a=2)
            link(v.tensor_scalar(tabf[:, :, :], pt[:, :, 0, :], float(NT), None, ALU.mult))
            link(v.tensor_tensor(tabf[:, :, :], tabf[:, :, :], pt[:, :, 1, :], ALU.add))
            if groups > 1:
                pass
            link(v.tensor_copy(r.tab[:, :, :], tabf[:, :, :]))
            if r.GT is not None:
                link(v.tensor_tensor(ex[:, :, :], m[0][:, :, :], bcast(r.wk[:, 0, :], E), ALU.mult))
                link(v.tensor_tensor(lg[:, :, :], m[1][:, :, :], bcast(r.wk[:, 1, :], E), ALU.mult))
                v.tensor_tensor(ex[:, :, :], ex[:, :, :], lg[:, :, :], ALU.add).then_inc(g_ready, 1)


class Moe0Experts:

    TILES = 2
    UNITS = NT // TILES
    AHEAD = 2

    WORDS = 10752

    def __init__(self, nc, ctx, w, r, arena, xn_dram, W1, y1_dram, r_dram, W2, y2_dram):
        self.nc, self.w, self.r = nc, w, r
        self.xn_rows = xn_dram.rearrange("p t d -> (p t) d")
        self.y1_dram, self.y1_rows = y1_dram, y1_dram.rearrange("h e c n -> (h e c) n")
        self.r_dram, self.r_rows = r_dram, r_dram.rearrange("p t n -> (p t) n")
        self.y2_dram, self.W1, self.W2 = y2_dram, W1, W2
        s = Scope(nc, ctx, "e")

        weights = Arena(arena[:, 0:3 * HID])
        self.w1 = weights.sb("w1", [P, 3, HID])
        self.w2 = self.w1.rearrange("p r (f d) -> p r f d", f=FC)
        first, middle, second = (Arena(arena[:, 3 * HID:]) for _ in range(3))
        self.xg = first.sb("xg", [C0, 4, HG, D])
        self.xgT = first.sb("xgT", [P, 2, HG * C0])
        self.out1 = first.sb("out1", [C0, 2, HG, HID])
        self.yk = middle.sb("yk", [P, 4, 2, HID])
        self.hb = middle.sb("hb", [P, 4, HID])
        self.ro = middle.sb("ro", [P, 6, HID])
        self.rg = second.sb("rg", [C0, 3, HG, HID])
        self.rT = second.sb("rT", [P, 3, FC * C0])
        self.out2 = second.sb("out2", [C0, 2, HG, D])
        self.stats = s.sb("stats", [P, NT, 6])
        self.mv = s.sb("mv", [P, NT, 2])
        self.rstd = s.sb("rstd", [P, NT])
        self.nm = s.sb("nm", [P, NT])
        self.bank = s.ps("bank", [P, 2, 512])
        self.chain = s.sem("chain")
        self.piece_made = s.sem("piece_made")
        self.piece_read = s.sem("piece_read")
        self.biased = s.sem("biased")
        self.combined = s.sem("combined")
        self.var_ready = s.sem("var_ready")
        self.root_ready = s.sem("root_ready")
        self.scale_ready = s.sem("scale_ready")
        self.centred = s.sem("centred")
        self.p_chain = s.sem("p_chain")
        self.weighted = s.sem("weighted")
        self.r_ready = s.sem("r_ready")
        self.turned2 = s.sem("turned2")
        self.rT_ready = s.sem("rT_ready")
        self.product2 = s.sem("product2")
        self.out2_ready = s.sem("out2_ready")
        self.w1_in = [s.sem(f"w1_in{i}") for i in range(3)]
        self.gathered1 = [s.sem(f"gathered1{i}") for i in range(4)]
        self.stored1 = [s.sem(f"stored1{i}") for i in range(2)]
        self.gathered_y = [s.sem(f"gathered_y{i}") for i in range(4)]
        self.stored_r = [s.sem(f"stored_r{i}") for i in range(3)]
        self.w2_in = [s.sem(f"w2_in{i}") for i in range(3)]
        self.gathered2 = [s.sem(f"gathered2{i}") for i in range(3)]
        self.stored2 = [s.sem(f"stored2{i}") for i in range(2)]

    def sync(self, sp):
        for e in range(E0 + 1):
            if e < E0:
                if e >= 3:
                    sp.wait_ge(self.piece_made, 5 * (e - 2))
                sp.dma_start(self.w1[:, e % 3, :], self.W1[e]).then_inc(self.w1_in[e % 3], 16)
            if e:
                f = e - 1
                sp.wait_ge(self.piece_read, 5 * (f + 1))
                sp.dma_start(self.y1_dram[:, f, :, :].rearrange("h c n -> c h n"),
                             self.out1[:, f % 2, :, :]).then_inc(self.stored1[f % 2], 16)
        sp.wait_ge(self.piece_made, 5 * E0)

        def load_w2(e):
            sp.dma_start(self.w2[:, e % 3, :, :],
                         self.W2[e].rearrange("(f p) d -> p f d", p=P)).then_inc(self.w2_in[e % 3], 16)

        for e in range(3):
            load_w2(e)
        for u in range(self.UNITS):
            t = u * self.TILES
            sp.wait_ge(self.r_ready, u + 1)
            sp.dma_start(self.r_dram[:, t:t + 2, :], self.ro[:, t % 6:t % 6 + 2, :]).then_inc(
                self.stored_r[(t // 2) % 3], 16)
        for e in range(E0):
            if 1 <= e and e + 2 < E0:
                sp.wait_ge(self.product2, HG * e)
                load_w2(e + 2)
            sp.wait_ge(self.out2_ready, e + 1)
            sp.dma_start(self.y2_dram[:, e, :, :].rearrange("h c n -> c h n"),
                         self.out2[:, e % 2, :, :]).then_inc(self.stored2[e % 2], 16)
        for i in range(2):
            sp.wait_ge(self.stored2[i], 16 * (E0 // 2))

    def pool(self, pool):
        nc, r = self.nc, self.r

        def gather_x(e):
            if e >= E0:
                return
            if e >= 4:
                pool.wait_ge(self.piece_made, 5 * (e - 4) + 1)
            for h in range(HG):
                nc.gpsimd.indirect_dma_start(
                    out=self.xg[:, e % 4, h, :], out_offset=None, in_=self.xn_rows,
                    in_offset=bass.IndirectOffsetOnAxis(ap=r.tab[:, h, e:e + 1], axis=0),
                ).then_inc(self.gathered1[e % 4], 16)

        def gather_y(u):
            for t in range(2 * u, min(2 * u + 2, NT)):
                if t >= 4:
                    pool.wait_ge(self.combined, t - 3)
                for k in range(2):
                    nc.gpsimd.indirect_dma_start(
                        out=self.yk[:, t % 4, k, :], out_offset=None, in_=self.y1_rows,
                        in_offset=bass.IndirectOffsetOnAxis(ap=r.back[:, k, t:t + 1], axis=0),
                    ).then_inc(self.gathered_y[t % 4], 16)

        def weigh(u):
            pool.wait_ge(self.centred, 2 * u + 2)
            t = 2 * u
            ro = self.ro[:, t % 6:t % 6 + 2, :]
            g = slice(t % HG, t % HG + 2)
            nc.gpsimd.tensor_tensor(ro, ro, self.w["ln_w"][:, g, :], ALU.mult).then_inc(self.p_chain, 1)
            pool.wait_ge(self.p_chain, u + 1)
            nc.gpsimd.tensor_tensor(ro, ro, self.w["ln_b"][:, g, :], ALU.add).then_inc(self.weighted, 1)

        def gather_r(e):
            if e >= E0:
                return
            if e >= 3:
                pool.wait_ge(self.turned2, HG * (e - 2))
            for h in range(HG):
                nc.gpsimd.indirect_dma_start(
                    out=self.rg[:, e % 3, h, :], out_offset=None, in_=self.r_rows,
                    in_offset=bass.IndirectOffsetOnAxis(ap=r.tab[:, h, e:e + 1], axis=0),
                ).then_inc(self.gathered2[e % 3], 16)

        for e in range(self.AHEAD):
            gather_x(e)
        for e in range(E0):
            gather_x(e + self.AHEAD)
            yield
        for i in range(2):
            pool.wait_ge(self.stored1[i], 16 * (E0 // 2))
        gather_y(0)
        yield
        for u in range(self.UNITS + 4):
            gather_y(u + 1)
            if 3 <= u < self.UNITS + 3:
                weigh(u - 3)
            yield
        for i in range(3):
            pool.wait_ge(self.stored_r[i], 16 * len(range(i, self.UNITS, 3)))
        for e in range(self.AHEAD):
            gather_r(e)
        yield
        for e in range(E0):
            gather_r(e + self.AHEAD)
            yield

    def tensor(self, pe):
        nc, w, bank = self.nc, self.w, self.bank

        def turn(e):
            k = 5 * e
            if e:
                pe.wait_ge(self.piece_read, k - 1)
            pe.wait_ge(self.gathered1[e % 4], 16 * HG * (e // 4 + 1))
            for g in range(HG):
                ins = nc.tensor.transpose(bank[:, k % 2, g * C0:(g + 1) * C0], self.xg[:, e % 4, g, :],
                                          w["ident"][0:C0, 0:C0])
            ins.then_inc(self.piece_made, 1)

        turn(0)
        for e in range(E0):
            for h in range(HG):
                k = 5 * e + 1 + h
                if h == 0:
                    pe.wait_ge(self.piece_read, 5 * e + 1)
                    pe.wait_ge(self.w1_in[e % 3], 16 * (e // 3 + 1))
                elif k >= 2:
                    pe.wait_ge(self.piece_read, k - 1)
                nc.tensor.matmul(bank[0:C0, k % 2, :], self.xgT[:, e % 2, h * C0:(h + 1) * C0],
                                 self.w1[:, e % 3, :], start=True, stop=True).then_inc(self.piece_made, 1)
                if h == 3 and e + 1 < E0:
                    turn(e + 1)
                yield
        yield from [None] * PE_SLOTS
        for u in range(self.UNITS + 4):
            for j in range(PE_SLOTS):
                t = 2 * u + j
                if j < 2 and t < NT:
                    if t < 2:
                        pe.wait_ge(self.piece_read, 5 * E0 - 1 + t)
                    else:
                        pe.wait_ge(self.combined, t - 1)
                    nc.tensor.matmul(bank[:, t % 2, :], gate_rows(self.r.GT, t), expert_biases(w["b1_experts"], t), start=True,
                                     stop=True).then_inc(self.biased, 1)
                yield
        yield from [None] * PE_SLOTS

        def product(n):
            e, h = divmod(n, HG)
            pe.wait_ge(self.rT_ready, n + 1)
            if h == 0:
                pe.wait_ge(self.w2_in[e % 3], 16 * (e // 3 + 1))
                if e:
                    pe.wait_ge(self.out2_ready, e)
            for f in range(FC):
                ins = nc.tensor.matmul(bank[0:C0, 1, h * D:(h + 1) * D], self.rT[:, n % 3, f * C0:(f + 1) * C0],
                                       self.w2[:, e % 3, f, :], start=(f == 0), stop=(f == FC - 1))
            ins.then_inc(self.product2, 1)

        for n in range(E0 * HG):
            e, h = divmod(n, HG)
            if h == 0:
                pe.wait_ge(self.gathered2[e % 3], 16 * HG * (e // 3 + 1))
            if n:
                pe.wait_ge(self.rT_ready, n)
            else:
                pe.wait_ge(self.combined, NT)
            for f in range(FC):
                ins = nc.tensor.transpose(bank[:, 0, f * C0:(f + 1) * C0], self.rg[:, e % 3, h, f * P:(f + 1) * P],
                                          w["ident"][0:C0, 0:C0])
            ins.then_inc(self.turned2, 1)
            if n:
                product(n - 1)
            yield
        product(E0 * HG - 1)

    def scalar(self, act):
        nc, bank, ro = self.nc, self.bank, self.ro

        def copy_turned(e):
            act.wait_ge(self.piece_made, 5 * e + 1)
            nc.scalar.activation(self.xgT[:, e % 2, :], bank[:, 5 * e % 2, 0:HG * C0], ACT.Copy).then_inc(
                self.piece_read, 1)

        copy_turned(0)
        for e in range(E0):
            if e >= 2:
                act.wait_ge(self.stored1[e % 2], 16 * (e // 2))
            for h in range(HG):
                k = 5 * e + 1 + h
                act.wait_ge(self.piece_made, k + 1)
                nc.scalar.activation(self.out1[:, e % 2, h, :], bank[0:C0, k % 2, :], ACT.Copy).then_inc(
                    self.piece_read, 1)
                if h == 1:
                    yield
            if e + 1 < E0:
                copy_turned(e + 1)
            yield
        yield from [None] * ACT_SLOTS
        for u in range(self.UNITS + 4):
            if 1 <= u <= self.UNITS:
                act.wait_ge(self.var_ready, 2 * u)
                t = slice(2 * u - 2, 2 * u)
                nc.scalar.activation(self.rstd[:, t], self.nm[:, t], ACT.Sqrt).then_inc(self.root_ready, 1)
            if 4 <= u:
                n = u - 4
                act.wait_ge(self.weighted, n + 1)
                rows = ro[:, 2 * n % 6:2 * n % 6 + 2, :]
                nc.scalar.activation(rows, rows, ACT.Relu).then_inc(self.r_ready, 1)
            yield
            if 2 <= u < self.UNITS + 2:
                n = u - 2
                act.wait_ge(self.scale_ready, n + 1)
                if n >= 3:
                    act.wait_ge(self.stored_r[n % 3], 16 * (n // 3))
                for t in range(2 * n, 2 * n + 2):
                    nc.scalar.activation(ro[:, t % 6, :], self.hb[:, t % 4, :], ACT.Identity,
                                         scale=self.rstd[:, t:t + 1], bias=self.nm[:, t:t + 1]).then_inc(
                                             self.centred, 1)
            yield
        yield from [None] * ACT_SLOTS

        def copy_out(e):
            act.wait_ge(self.product2, HG * (e + 1))
            if e >= 2:
                act.wait_ge(self.stored2[e % 2], 16 * (e // 2))
            nc.scalar.activation(self.out2[:, e % 2, :, :].rearrange("p a b -> p (a b)"), bank[0:C0, 1, :],
                                 ACT.Copy).then_inc(self.out2_ready, 1)

        for e in range(E0):
            for h in range(HG):
                n = HG * e + h
                act.wait_ge(self.turned2, n + 1)
                if n >= 3:
                    act.wait_ge(self.product2, n - 2)
                nc.scalar.activation(self.rT[:, n % 3, :], bank[:, 0, 0:FC * C0], ACT.Copy).then_inc(self.rT_ready, 1)
                if h == 0 and e:
                    copy_out(e - 1)
                if h % 2:
                    yield
        copy_out(E0 - 1)

    def vector(self, dve):
        nc, r, v = self.nc, self.r, self.nc.vector
        link = Chain(dve, self.chain)
        for _ in range(E0 + 1):
            yield
        for u in range(self.UNITS + 4):
            if u < self.UNITS:
                for t in range(2 * u, 2 * u + 2):
                    hb = self.hb[:, t % 4, :]
                    dve.wait_ge(self.gathered_y[t % 4], 32 * (t // 4 + 1))
                    dve.wait_ge(self.biased, t + 1)
                    if t >= 4:
                        dve.wait_ge(self.centred, t - 3)
                    link(v.scalar_tensor_tensor(out=hb, in0=self.yk[:, t % 4, 0, :], scalar=r.wk[:, 0, t:t + 1],
                                                in1=self.bank[:, t % 2, :], op0=ALU.mult, op1=ALU.add))
                    v.scalar_tensor_tensor(out=hb, in0=self.yk[:, t % 4, 1, :], scalar=r.wk[:, 1, t:t + 1],
                                           in1=hb, op0=ALU.mult, op1=ALU.add).then_inc(self.combined, 1)
                    dve.wait_ge(self.combined, t + 1)
                    link(v.bn_stats(self.stats[:, t, :], hb))
                    link(v.bn_aggr(self.mv[:, t, :], self.stats[:, t, :]))
                    v.tensor_scalar(self.nm[:, t:t + 1], self.mv[:, t, 1:2], 1e-6, None, ALU.add).then_inc(
                        self.var_ready, 1)
            if 1 <= u <= self.UNITS:
                dve.wait_ge(self.root_ready, u)
                t = slice(2 * u - 2, 2 * u)
                link(v.reciprocal(self.rstd[:, t], self.rstd[:, t]))
                v.scalar_tensor_tensor(out=self.nm[:, t], in0=self.mv[:, t, 0], scalar=-1.0, in1=self.rstd[:, t],
                                       op0=ALU.mult, op1=ALU.mult).then_inc(self.scale_ready, 1)
            yield


def moe0_output_stage(nc, w, r, y2_rows, xn_rows, s_rows, x_dram, x_rows):
    RING = 4
    with ExitStack() as ctx:
        s = Scope(nc, ctx, "e4")
        yk = s.sb("yk", [P, RING, 2, D])
        o = s.sb("o", [P, NT, D])
        sq = s.sb("sq", [P, 8, D])
        acc = s.sb("acc", [P, NT])
        var = s.sb("var", [P, NT])
        p_b = s.ps("p_b", [P, 4, D * TB])
        gathered = [s.sem(f"gathered{i}") for i in range(RING)]
        chain = s.sem("chain")
        x_in = s.sem("x_in")
        biased = s.sem("biased")
        combined = s.sem("combined")
        var_ready = s.sem("var_ready")
        root_ready = s.sem("root_ready")
        o_ready = s.sem("o_ready")
        g_ready = s.sem("g_ready")
        block = ctx.enter_context(nc.Block())

        @block.sync
        def _(sp):
            sp.dma_start(x_rows[:, :, :], x_dram).then_inc(x_in, 16)
            sp.wait_ge(x_in, 16)

        @block.gpsimd
        def _(pool):
            for t in range(NT):
                if t >= RING:
                    pool.wait_ge(combined, t - RING + 1)
                for k in range(2):
                    nc.gpsimd.indirect_dma_start(
                        out=yk[:, t % RING, k, :], out_offset=None, in_=y2_rows,
                        in_offset=bass.IndirectOffsetOnAxis(ap=r.back[:, k, t:t + 1], axis=0),
                    ).then_inc(gathered[t % RING], 16)

        @block.tensor
        def _(pe):
            for b in range(B):
                if b >= 4:
                    pe.wait_ge(combined, TB * (b - 3))
                for j in range(TB):
                    t = b * TB + j
                    ins = nc.tensor.matmul(p_b[:, b % 4, j * D:(j + 1) * D], gate_rows(r.GT, t),
                                           expert_biases(w["b2_experts"], t), start=True, stop=True)
                ins.then_inc(biased, 1)

        @block.vector
        def _(dve):
            link = Chain(dve, chain)
            v = nc.vector
            for t in range(NT):
                b, j = divmod(t, TB)
                dve.wait_ge(gathered[t % RING], 32 * (t // RING + 1))
                dve.wait_ge(biased, b + 1)
                link(v.scalar_tensor_tensor(out=o[:, t, :], in0=yk[:, t % RING, 0, :], scalar=r.wk[:, 0, t:t + 1],
                                            in1=p_b[:, b % 4, j * D:(j + 1) * D], op0=ALU.mult, op1=ALU.add))
                v.scalar_tensor_tensor(out=o[:, t, :], in0=yk[:, t % RING, 1, :], scalar=r.wk[:, 1, t:t + 1],
                                       in1=o[:, t, :], op0=ALU.mult, op1=ALU.add).then_inc(combined, 1)
            dve.wait_ge(combined, NT)
            row_norm(nc, dve, link, o, xn_rows, sq, acc, var, 1e-6, var_ready, root_ready)
            for c in range(4):
                t = slice(c * 8, (c + 1) * 8)
                link(v.tensor_tensor(o[:, t, :], o[:, t, :], w["ln_out_w"][:, :].unsqueeze(1).broadcast_to([P, 8, D]),
                                     ALU.mult))
                v.tensor_tensor(o[:, t, :], o[:, t, :], w["ln_out_b"][:, :].unsqueeze(1).broadcast_to([P, 8, D]),
                                ALU.add).then_inc(o_ready, 1)
            dve.wait_ge(x_in, 16)
            for c in range(4):
                t = slice(c * 8, (c + 1) * 8)
                dve.wait_ge(g_ready, c + 1)
                link(v.tensor_tensor(o[:, t, :], o[:, t, :], s_rows[:, t, :], ALU.mult))
                link(v.tensor_tensor(x_rows[:, t, :], x_rows[:, t, :], o[:, t, :], ALU.add))

        @block.scalar
        def _(act):
            act.wait_ge(var_ready, 1)
            nc.scalar.activation(var[:, :], var[:, :], ACT.Sqrt).then_inc(root_ready, 1)
            for c in range(4):
                act.wait_ge(o_ready, c + 1)
                nc.scalar.activation(o[:, c * 8:(c + 1) * 8, :], o[:, c * 8:(c + 1) * 8, :], ACT.Silu).then_inc(g_ready, 1)


def row_norm(nc, dve, link, o, add, sq, acc, var, eps, var_ready, root_ready):
    v = nc.vector
    for c in range(4):
        t = slice(c * 8, (c + 1) * 8)
        link(v.tensor_tensor(o[:, t, :], o[:, t, :], add[:, t, :], ALU.add))
        link(v.tensor_reduce(acc[:, t], o[:, t, :], AX_X, ALU.add))
        link(v.tensor_scalar(acc[:, t], acc[:, t], -1.0 / D, None, ALU.mult))
        link(v.tensor_tensor(o[:, t, :], o[:, t, :], bcast(acc[:, t], D), ALU.add))
        link(v.tensor_tensor(sq[:, :, :], o[:, t, :], o[:, t, :], ALU.mult))
        link(v.tensor_reduce(var[:, t], sq[:, :, :], AX_X, ALU.add))
    v.tensor_scalar(var[:, :], var[:, :], 1.0 / D, eps, ALU.mult, ALU.add).then_inc(var_ready, 1)
    dve.wait_ge(root_ready, 1)
    link(v.reciprocal(var[:, :], var[:, :]))
    for c in range(4):
        t = slice(c * 8, (c + 1) * 8)
        link(v.tensor_tensor(o[:, t, :], o[:, t, :], bcast(var[:, t], D), ALU.mult))


NH = 8
SCALE = float(D) ** -0.5
SIM_AT = [(1, 384), (2, 0), (1, 0), (0, 0)]
PT_AT = [(0, 0), (1, 0), (2, 0), (1, 384)]


def attention_fold_stage(nc, w, xn_rows, xaT, M, N):
    with ExitStack() as ctx:
        s = Scope(nc, ctx, "af")
        sq = s.sb("sq", [P, 8, D])
        l2 = s.sb("l2", [P, NT])
        xa = s.sb("xa", [P, NT, D])
        qkv = s.sb("qkv", [P, 3 * NH, D])
        wo = s.sb("wo", [P, NH, D])
        p_w = s.ps("p_w", [P, 4, 512])
        p_x = s.ps("p_x", [P, 4, 512])
        w_in = s.sem("w_in")
        chain = s.sem("chain")
        summed = s.sem("summed")
        root_ready = s.sem("root_ready")
        xa_ready = s.sem("xa_ready")
        folded = s.sem("folded")
        fold_copied = s.sem("fold_copied")
        turned = s.sem("turned")
        xaT_ready = s.sem("xaT_ready")
        block = ctx.enter_context(nc.Block())

        @block.sync
        def _(sp):
            sp.dma_start(qkv[:, :, :], w["qkv_dram"]).then_inc(w_in, 16)
            sp.dma_start(wo[:, :, :], w["wo_dram"]).then_inc(w_in, 16)
            sp.wait_ge(w_in, 32)

        @block.tensor
        def _(pe):
            pe.wait_ge(w_in, 32)
            for n in range(4):
                for j in range(4):
                    h = (n % 2) * 4 + j
                    if n < 2:
                        ins = nc.tensor.matmul(p_w[:, n, j * D:(j + 1) * D], qkv[:, h, :], qkv[:, NH + h, :],
                                               start=True, stop=True)
                    else:
                        ins = nc.tensor.matmul(p_w[:, n, j * D:(j + 1) * D], qkv[:, 2 * NH + h, :], wo[:, h, :],
                                               start=True, stop=True)
                ins.then_inc(folded, 1)
            for b in range(B):
                pe.wait_ge(xa_ready, b // 2 + 1)
                if b >= 4:
                    pe.wait_ge(xaT_ready, b - 3)
                for j in range(TB):
                    ins = nc.tensor.transpose(p_x[:, b % 4, j * P:(j + 1) * P], xa[:, b * TB + j, :], w["ident"])
                ins.then_inc(turned, 1)

        @block.scalar
        def _(act):
            act.wait_ge(summed, 1)
            nc.scalar.activation(l2[:, :], l2[:, :], ACT.Sqrt).then_inc(root_ready, 1)
            for n in range(4):
                act.wait_ge(folded, n + 1)
                dst = (M if n < 2 else N)[:, (n % 2) * 512:(n % 2 + 1) * 512]
                nc.scalar.activation(dst, p_w[:, n, :], ACT.Copy, scale=SCALE if n < 2 else 1.0).then_inc(fold_copied, 1)
            for b in range(B):
                act.wait_ge(turned, b + 1)
                nc.scalar.activation(xaT[:, b, :], p_x[:, b % 4, :], ACT.Copy, scale=w["gamma"]).then_inc(xaT_ready, 1)

        @block.vector
        def _(dve):
            link = Chain(dve, chain)
            v = nc.vector
            for c in range(4):
                t = slice(c * 8, (c + 1) * 8)
                link(v.tensor_tensor(sq[:, :, :], xn_rows[:, t, :], xn_rows[:, t, :], ALU.mult))
                link(v.tensor_reduce(l2[:, t], sq[:, :, :], AX_X, ALU.add))
            v.memset(sq[:, 0, 0:1], 0.0).then_inc(summed, 1)
            dve.wait_ge(root_ready, 1)
            link(v.tensor_scalar(l2[:, :], l2[:, :], 1e-12, None, ALU.max))
            link(v.reciprocal(l2[:, :], l2[:, :]))
            link(v.tensor_scalar(l2[:, :], l2[:, :], float(D) ** 0.5, None, ALU.mult))
            for c in range(4):
                t = slice(c * 8, (c + 1) * 8)
                v.tensor_tensor(xa[:, t, :], xn_rows[:, t, :], bcast(l2[:, t], D), ALU.mult).then_inc(xa_ready, 1)


def attention_stage(nc, w, xaT, M, N, s_rows):
    NI = B * NH
    BANKS = [(3,), (2, 0), (1,)]
    with ExitStack() as ctx:
        s = Scope(nc, ctx, "at")
        qT = s.sb("qT", [P, 3, L])
        V = s.sb("V", [P, 2, TB, NH * D])
        pr = s.sb("pr", [P, 2, 3, 512])
        pT = s.sb("pT", [P, 2, 3, 512])
        mx = s.sb("mx", [P, 2, 4])
        nmx = s.sb("nmx", [P, 2, 4])
        sums = s.sb("sums", [P, 3, 4])
        p_s = s.ps("p_s", [P, 3, 512])
        p_t = s.ps("p_t", [P, 3, 512])
        p_o = s.ps("p_o", [P, 4, D])
        p_q = s.ps("p_q", [P, 512])
        chain = s.sem("chain")
        q_product = s.sem("q_product")
        q_copied = s.sem("q_copied")
        v_product = s.sem("v_product")
        v_copied = s.sem("v_copied")
        scores = s.sem("scores")
        maxed = s.sem("maxed")
        exped = s.sem("exped")
        turned = s.sem("turned")
        pT_ready = s.sem("pT_ready")
        out_ready = s.sem("out_ready")
        out_used = s.sem("out_used")
        block = ctx.enter_context(nc.Block())


        @block.tensor
        def _(pe):
            def query(n):
                b, h = divmod(n, NH)
                pe.wait_ge(v_copied, min(NH * B, NH + max(n - 2, 0)))
                if n:
                    pe.wait_ge(q_copied, n)
                nc.tensor.matmul(p_q[:, :], M[:, h * D:(h + 1) * D], xaT[:, b, :], start=True,
                                 stop=True).then_inc(q_product, 1)

            def value(k):
                b, i = divmod(k, NH)
                t, half = divmod(i, 2)
                if k:
                    pe.wait_ge(v_copied, k)
                if k >= NH:
                    pe.wait_ge(q_copied, min(NI, k - NH + 3))
                nc.tensor.matmul(p_q[:, :], xaT[:, b, t * P:(t + 1) * P], N[:, half * 512:(half + 1) * 512],
                                 start=True, stop=True).then_inc(v_product, 1)

            def score(n):
                b, h = divmod(n, NH)
                pe.wait_ge(q_copied, n + 1)
                for k, tiles in enumerate(BANKS):
                    if n:
                        pe.wait_ge(exped, 3 * (n - 1) + k + 1)
                    for i in tiles:
                        bank, c = SIM_AT[i]
                        K = (i + 1) * P
                        nc.tensor.matmul(p_s[:, bank, c:c + K], qT[:, n % 3, i * P:(i + 1) * P], xaT[:, b, 0:K],
                                         start=True, stop=False)
                        ins = nc.tensor.matmul(p_s[:, bank, c + i * P:c + K], w["ident_bf"], w["mask_bf"],
                                               start=False, stop=True)
                    ins.then_inc(scores, 1)

            def turn(n):
                pe.wait_ge(exped, 3 * (n + 1))
                for bank, keys in enumerate(((0,), (1, 3), (2,))):
                    if n:
                        pe.wait_ge(pT_ready, 3 * (n - 1) + bank + 1)
                    for j in keys:
                        c = PT_AT[j][1]
                        for i in range(j, TB):
                            sbank, sc = SIM_AT[i]
                            ins = nc.tensor.transpose(p_t[:, bank, c + (i - j) * P:c + (i - j + 1) * P],
                                                      pr[:, n % 2, sbank, sc + j * P:sc + (j + 1) * P], w["ident"])
                    ins.then_inc(turned, 1)

            def weigh(n):
                b, h = divmod(n, NH)
                pe.wait_ge(v_copied, NH * (b + 1))
                if n:
                    pe.wait_ge(out_used, n)
                pe.wait_ge(pT_ready, 3 * (n + 1))
                for i in range(TB):
                    for j in range(i + 1):
                        bank, c = PT_AT[j]
                        ins = nc.tensor.matmul(p_o[:, i, :], pT[:, n % 2, bank, c + (i - j) * P:c + (i - j + 1) * P],
                                               V[:, b % 2, j, h * D:(h + 1) * D], start=(j == 0), stop=(j == i))
                ins.then_inc(out_ready, 1)

            for k in range(NH):
                value(k)
            query(0)
            query(1)
            score(0)
            for n in range(NI):
                turn(n)
                if n + 2 < NI:
                    query(n + 2)
                if n + 1 < NI:
                    score(n + 1)
                if n + NH < NI:
                    value(n + NH)
                weigh(n)

        @block.scalar
        def _(act):
            def copy_query(n):
                act.wait_ge(q_product, n + 1)
                if n >= 3:
                    act.wait_ge(scores, 3 * (n - 2))
                nc.scalar.activation(qT[:, n % 3, :], p_q[:, :], ACT.Copy).then_inc(q_copied, 1)

            def copy_value(k):
                b, i = divmod(k, NH)
                t, half = divmod(i, 2)
                act.wait_ge(v_product, k + 1)
                if b >= 2:
                    act.wait_ge(out_ready, NH * (b - 1))
                nc.scalar.activation(V[:, b % 2, t, half * 512:(half + 1) * 512], p_q[:, :],
                                     ACT.Copy).then_inc(v_copied, 1)

            def exps(n):
                if n >= 2:
                    act.wait_ge(turned, 3 * (n - 1))
                if n >= 3:
                    act.wait_ge(out_used, n - 2)
                for k, tiles in enumerate(BANKS):
                    act.wait_ge(maxed, 3 * n + k + 1)
                    for i in tiles:
                        bank, c = SIM_AT[i]
                        K = (i + 1) * P
                        ins = nc.scalar.activation(pr[:, n % 2, bank, c:c + K], p_s[:, bank, c:c + K], ACT.Exp,
                                                   bias=nmx[:, n % 2, i:i + 1], accum_out=sums[:, n % 3, i:i + 1])
                    ins.then_inc(exped, 1)

            for k in range(NH):
                copy_value(k)
            copy_query(0)
            copy_query(1)
            for n in range(NI):
                exps(n)
                if n and n - 1 + NH < NI:
                    copy_value(n - 1 + NH)
                if n + 2 < NI:
                    copy_query(n + 2)

        @block.vector
        def _(dve):
            link = Chain(dve, chain)
            v = nc.vector

            def maxima(n):
                for k, tiles in enumerate(BANKS):
                    dve.wait_ge(scores, 3 * n + k + 1)
                    for i in tiles:
                        bank, c = SIM_AT[i]
                        link(v.tensor_reduce(mx[:, n % 2, i:i + 1], p_s[:, bank, c:c + (i + 1) * P], AX_X, ALU.max))
                        ins = v.tensor_scalar(nmx[:, n % 2, i:i + 1], mx[:, n % 2, i:i + 1], -1.0, None, ALU.mult)
                    ins.then_inc(maxed, 1)

            def add_head(n):
                b, h = divmod(n, NH)
                link(v.reciprocal(sums[:, n % 3, :], sums[:, n % 3, :]))
                dve.wait_ge(out_ready, n + 1)
                for i in range(TB):
                    o = s_rows[:, b * TB + i, :]
                    if h == 0:
                        ins = v.tensor_scalar(o, p_o[:, i, :], sums[:, n % 3, i:i + 1], None, ALU.mult)
                    else:
                        ins = v.scalar_tensor_tensor(out=o, in0=p_o[:, i, :], scalar=sums[:, n % 3, i:i + 1], in1=o,
                                                     op0=ALU.mult, op1=ALU.add)
                ins.then_inc(out_used, 1)

            maxima(0)
            for n in range(NI):
                for bank in range(3):
                    dve.wait_ge(turned, 3 * n + bank + 1)
                    cols = 512 if bank < 2 else 256
                    v.tensor_copy(pT[:, n % 2, bank, 0:cols], p_t[:, bank, 0:cols]).then_inc(pT_ready, 1)
                if n > 1:
                    dve.wait_ge(out_used, n - 1)
                if n:
                    add_head(n - 1)
                if n + 1 < NI:
                    maxima(n + 1)
            dve.wait_ge(out_used, NI - 1)
            add_head(NI - 1)


def moe1_expert_stage(nc, w, r, xn_dram, we_dram, y_dram):
    EG = 4
    NG = E1 // EG
    WG = 4
    RING = 4
    with ExitStack() as ctx:
        s = Scope(nc, ctx, "f1")
        we = s.sb("we", [P, 3, WG * EG, D])
        xg = s.sb("xg", [P, RING, D])
        xgT = s.sb("xgT", [P, 3, P])
        out = s.sb("out", [C1, RING, EG, D])
        p_x = s.ps("p_x", [P, 4, 512])
        p_o = s.ps("p_o", [C1, 4, EG * D])
        w_in = [s.sem(f"w_in{i}") for i in range(3)]
        gathered = [s.sem(f"gathered{i}") for i in range(RING)]
        stored = [s.sem(f"stored{i}") for i in range(RING)]
        turned = s.sem("turned")
        xT_ready = s.sem("xT_ready")
        product = s.sem("product")
        copied = s.sem("copied")
        block = ctx.enter_context(nc.Block())

        @block.sync
        def _(sp):
            def load(c):
                if c >= 3:
                    sp.wait_ge(product, WG * (c - 2))
                sp.dma_start(we[:, c % 3, :, :],
                             we_dram[c * WG * EG:(c + 1) * WG * EG].rearrange("e d f -> d e f")).then_inc(w_in[c % 3], 16)

            for g in range(NG):
                if g % WG == 0:
                    if g == 0:
                        load(0)
                        load(1)
                    if g // WG + 2 < NG // WG:
                        load(g // WG + 2)
                sp.wait_ge(copied, g + 1)
                sp.dma_start(y_dram[g * EG:(g + 1) * EG].rearrange("e c f -> c e f"),
                             out[:, g % RING, :, :]).then_inc(stored[g % RING], 16)
            for i in range(RING):
                sp.wait_ge(stored[i], 16 * (NG // RING))

        @block.gpsimd
        def _(pool):
            for g in range(NG):
                if g >= RING:
                    pool.wait_ge(turned, g - RING + 1)
                nc.gpsimd.indirect_dma_start(
                    out=xg[:, g % RING, :], out_offset=None, in_=xn_dram,
                    in_offset=bass.IndirectOffsetOnAxis(ap=r.tab[:, 0, g:g + 1], axis=0),
                ).then_inc(gathered[g % RING], 16)

        @block.tensor
        def _(pe):
            def turn(g):
                pe.wait_ge(gathered[g % RING], 16 * (g // RING + 1))
                if g >= 4:
                    pe.wait_ge(xT_ready, g - 3)
                nc.tensor.transpose(p_x[:, g % 4, 0:P], xg[:, g % RING, :], w["ident"]).then_inc(turned, 1)

            turn(0)
            turn(1)
            for g in range(NG):
                if g + 2 < NG:
                    turn(g + 2)
                pe.wait_ge(xT_ready, g + 1)
                pe.wait_ge(w_in[(g // WG) % 3], 16 * (g // WG // 3 + 1))
                if g >= 4:
                    pe.wait_ge(copied, g - 3)
                for j in range(EG):
                    ins = nc.tensor.matmul(p_o[:, g % 4, j * D:(j + 1) * D], xgT[:, g % 3, j * C1:(j + 1) * C1],
                                           we[:, (g // WG) % 3, (g % WG) * EG + j, :], start=True, stop=True)
                ins.then_inc(product, 1)

        @block.scalar
        def _(act):
            for g in range(NG):
                act.wait_ge(turned, g + 1)
                if g >= 3:
                    act.wait_ge(product, g - 2)
                nc.scalar.activation(xgT[:, g % 3, :], p_x[:, g % 4, 0:P], ACT.Copy).then_inc(xT_ready, 1)

        @block.vector
        def _(dve):
            for g in range(NG):
                dve.wait_ge(product, g + 1)
                if g >= RING:
                    dve.wait_ge(stored[g % RING], 16 * (g // RING))
                nc.vector.tensor_copy(out[:, g % RING, :, :].rearrange("p a b -> p (a b)"),
                                      p_o[:, g % 4, :]).then_inc(copied, 1)


def moe1_output_stage(nc, w, r, y_rows, s_rows, x_rows, out_dram, stored):
    RING = 4
    with ExitStack() as ctx:
        s = Scope(nc, ctx, "f2")
        yk = s.sb("yk", [P, RING, 2, D])
        o = s.sb("o", [P, NT, D])
        gathered = [s.sem(f"gathered{i}") for i in range(RING)]
        chain = s.sem("chain")
        scaled = s.sem("scaled")
        combined = s.sem("combined")
        g_ready = s.sem("g_ready")
        x_ready = s.sem("x_ready")
        block = ctx.enter_context(nc.Block())

        @block.gpsimd
        def _(pool):
            for t in range(NT):
                if t >= RING:
                    pool.wait_ge(combined, t - RING + 1)
                for k in range(2):
                    nc.gpsimd.indirect_dma_start(
                        out=yk[:, t % RING, k, :], out_offset=None, in_=y_rows,
                        in_offset=bass.IndirectOffsetOnAxis(ap=r.back[:, k, t:t + 1], axis=0),
                    ).then_inc(gathered[t % RING], 16)

        @block.vector
        def _(dve):
            link = Chain(dve, chain)
            v = nc.vector

            def update(c):
                t = slice(c * 8, (c + 1) * 8)
                dve.wait_ge(g_ready, c + 1)
                link(v.tensor_tensor(o[:, t, :], o[:, t, :], s_rows[:, t, :], ALU.mult))
                v.tensor_tensor(x_rows[:, t, :], x_rows[:, t, :], o[:, t, :], ALU.add).then_inc(x_ready, 1)

            for t in range(NT):
                dve.wait_ge(scaled, t + 1)
                v.scalar_tensor_tensor(out=o[:, t, :], in0=yk[:, t % RING, 1, :], scalar=r.wk[:, 1, t:t + 1],
                                       in1=o[:, t, :], op0=ALU.mult, op1=ALU.add).then_inc(combined, 1)
                if t % 8 == 4 and t > 8:
                    update(t // 8 - 1)
            update(3)

        @block.scalar
        def _(act):
            def gate(c):
                act.wait_ge(combined, 8 * (c + 1))
                nc.scalar.activation(o[:, c * 8:(c + 1) * 8, :], o[:, c * 8:(c + 1) * 8, :], ACT.Silu).then_inc(g_ready, 1)

            for t in range(NT):
                act.wait_ge(gathered[t % RING], 32 * (t // RING + 1))
                nc.scalar.activation(o[:, t, :], yk[:, t % RING, 0, :], ACT.Copy,
                                     scale=r.wk[:, 0, t:t + 1]).then_inc(scaled, 1)
                if t % 8 == 1 and t > 8:
                    gate(t // 8 - 1)
            gate(3)

        @block.sync
        def _(sp):
            for c in range(4):
                sp.wait_ge(x_ready, c + 1)
                sp.dma_start(out_dram[:, c * 8:(c + 1) * 8, :], x_rows[:, c * 8:(c + 1) * 8, :]).then_inc(stored, 16)
            sp.wait_ge(stored, 64)


def load_stage(nc, tag, pairs):
    with ExitStack() as ctx:
        s = Scope(nc, ctx, tag)
        loaded = s.sem("loaded")
        block = ctx.enter_context(nc.Block())

        @block.sync
        def _(sp):
            for dst, src in pairs:
                sp.dma_start(dst, src).then_inc(loaded, 16)
            sp.wait_ge(loaded, 16 * len(pairs))


def clear_semaphores(nc):
    released = sorted(int(n) for n in nc.released_uncleared_semaphores)
    with nc.Block() as block:
        @block.gpsimd
        def _(pool):
            first = released[0]
            for n, following in zip(released, released[1:] + [None]):
                if following != n + 1:
                    pool.sem_clear(range(first, n + 1))
                    first = following


def program(nc, a, out):
    with ExitStack() as top:
        G = Scope(nc, top, "g")

        def dram(name, shape):
            return nc.dram_tensor(name, shape, F32, kind="Internal").ap()

        xn_dram = dram("xn_scratch", [P, NT, D])
        y1_dram = dram("y1_scratch", [HG, E0, C0, HID])
        r_dram = dram("r_scratch", [P, NT, HID])
        y2_dram = dram("y2_scratch", [HG, E0, C0, D])
        xn1_dram = dram("xn1_scratch", [P, NT, D])
        y3_dram = dram("y3_scratch", [E1, C1, D])

        outputs_stored = G.sem("outputs_stored")
        w = {}

        def resident(scope, names):
            pairs = []
            for n in names:
                src = a[n]
                shape = list(src.shape)
                buf = scope.sb(n, [P] + shape[1:] if shape[0] == 1 else shape, src.dtype)
                whole = buf[tuple(slice(None) for _ in shape)]
                w[n] = whole
                flat = whole
                if shape[0] == 1:
                    if len(shape) == 3:
                        flat = whole.rearrange("p a b -> p (a b)")
                        src = src.rearrange("o a b -> o (a b)")
                    src = src.broadcast_to([P, src.shape[1]])
                pairs.append((flat, src))
            return pairs

        consts = resident(G, ["ident", "tri", "ones", "iota", "pcol", "group_base"])

        state = G.sb("state", [P, 3 * NT * D])
        rows, xn_rows, s_rows = (state[:, k * NT * D:(k + 1) * NT * D].rearrange("p (t d) -> p t d", d=D)
                                 for k in range(3))

        with ExitStack() as moe:
            F = Scope(nc, moe, "moe")
            r = Routing()
            r.tab = F.sb("tab", [C0, HG, E0], U32)
            r.back = F.sb("back", [P, 2, NT], U32)
            r.wk = F.sb("wk", [P, 2, NT])
            r.GT = F.sb("GT", [64 + E0, GT_BATCHES * L])
            fw = resident(F, ["wg0", "b1_experts", "ln_w", "ln_b"])
            H = Scope(nc, moe, "mamba")
            mw = resident(H, ["xproj_T", "dt_T", "dt_b", "A_log", "D", "sel"])
            zT = H.sb("zT", [P, 2, N_TOK])
            with ExitStack() as scan:
                xT = Scope(nc, scan, "scan").sb("xT", [P, 2, N_TOK])
                with ExitStack() as inp:
                    I = Scope(nc, inp, "inp")
                    iw = resident(I, ["in_T", "conv_rows", "conv_b"])
                    xnT = I.sb("xnT", [P, B, PAD])
                    layernorm_stage(nc, a["x"], xn_dram, rows, xn_rows, xnT, w["ident"], "ln0",
                                    consts + iw + mw + fw)
                    mamba_input_stage(nc, w, xnT, xT, zT)
                    routing_stage(nc, w, r, xnT, w["wg0"],
                                  dict(E=E0, C=C0, groups=HG, LO=C0, HI=E0, masked=True, floor=1e-9), "r0",
                                  Arena(state[:, :]))
                experts = Moe0Experts(nc, scan, w, r, state[:, 0:Moe0Experts.WORDS], xn_dram,
                                      a["W1"], y1_dram, r_dram, a["W2"], y2_dram)
                scan_stage(nc, w, xT, zT, Arena(state[:, Moe0Experts.WORDS:]), experts)
            ow = resident(F, ["out_T", "w1_T", "b1", "w2_T", "b2", "norm1", "b2_experts", "ln_out_w", "ln_out_b"])
            load_stage(nc, "lx", [(xn_rows[:, :, :], xn_dram)] + ow)
            mamba_output_stage(nc, w, zT, xn_rows, s_rows)
            moe0_output_stage(nc, w, r, y2_dram.rearrange("h e c n -> (h e c) n"), xn_rows, s_rows, a["x"], rows)

        clear_semaphores(nc)
        with ExitStack() as l1:
            H = Scope(nc, l1, "l1")
            r = Routing()
            r.tab = H.sb("tab", [P, 1, E1 // 4], U32)
            r.back = H.sb("back", [P, 2, NT], U32)
            r.wk = H.sb("wk", [P, 2, NT])
            r.GT = None
            l1w = resident(H, ["wg1", "gamma", "ident_bf", "mask_bf"])
            with ExitStack() as rt:
                xnT = Scope(nc, rt, "rt1").sb("xnT", [P, B, PAD])
                layernorm_stage(nc, None, xn1_dram, rows, xn_rows, xnT, w["ident"], "ln1", l1w)
                routing_stage(nc, w, r, xnT, w["wg1"],
                              dict(E=E1, C=C1, groups=1, LO=P, HI=E1 // 4, masked=False,
                                   floor=float(np.finfo(np.float32).eps)), "r1",
                              Scope(nc, rt, "r1s"))
            w["qkv_dram"], w["wo_dram"] = a["qkv"], a["wo"]
            with ExitStack() as att:
                A_ = Scope(nc, att, "att")
                xaT = A_.sb("xaT", [P, B, L])
                M = A_.sb("M", [P, NH * D])
                N = A_.sb("N", [P, NH * D])
                attention_fold_stage(nc, w, xn_rows, xaT, M, N)
                attention_stage(nc, w, xaT, M, N, s_rows)
            moe1_expert_stage(nc, w, r, xn1_dram.rearrange("p t d -> (p t) d"), a["we"], y3_dram)
            moe1_output_stage(nc, w, r, y3_dram.rearrange("e c n -> (e c) n"), s_rows, rows, out, outputs_stored)


def laid_out(i):

    c = np.ascontiguousarray
    bf16 = np.dtype("bfloat16")

    def striped(b):
        rows = np.zeros((64 + E0, b.shape[1]), b.dtype)
        for k in range(3):
            rows[32 * k:32 * k + E0] = b
        return rows

    xp = i["L0_attn_x_proj_w"].T.reshape(HALF, P, DTR + 2 * DS).transpose(1, 0, 2)
    sel = np.zeros((96, 2 * DS, P), bf16)
    for row in range(96):
        sel[row, row % (2 * DS)] = 1
    qkv = i["L1_attn_w_qkv"].reshape(3 * NH, D, D).transpose(1, 0, 2)
    return {
        "x": c(i["L0_attn_Z"].reshape(NT, P, D).transpose(1, 0, 2)),
        "in_T": c(i["L0_attn_in_proj_w"].T),
        "conv_rows": c(i["L0_attn_conv_w"].T[None]),
        "conv_b": c(i["L0_attn_conv_b"].reshape(HALF, P).T),
        "xproj_T": c(np.concatenate([xp[:, :, DTR:]] * 3 + [xp[:, :, :DTR]], axis=2)),
        "dt_T": c(i["L0_attn_dt_proj_w"].T),
        "dt_b": c(i["L0_attn_dt_proj_b"].reshape(HALF, P).T),
        "A_log": c(i["L0_attn_A_log"].reshape(HALF, P, DS).transpose(1, 0, 2)),
        "D": c(i["L0_attn_D"].reshape(HALF, P).T),
        "out_T": c(i["L0_attn_out_proj_w"].T.reshape(HALF, P, D).transpose(1, 0, 2)),
        "w1_T": c(i["L0_attn_mlp_w1"].T),
        "b1": c(i["L0_attn_mlp_b1"].reshape(FC, P).T),
        "w2_T": c(i["L0_attn_mlp_w2"].T.reshape(FC, P, D).transpose(1, 0, 2)),
        "b2": c(i["L0_attn_mlp_b2"][None]),
        "norm1": c(i["L0_attn_norm1_w"][None]),
        "wg0": c(i["L0_ffn_Wg"]),
        "W1": c(i["L0_ffn_W1"]),
        "W2": c(i["L0_ffn_W2"]),
        "b1_experts": striped(i["L0_ffn_b1"]),
        "b2_experts": striped(i["L0_ffn_b2"]),
        "ln_w": c(i["L0_ffn_ln_hid_w"][None]),
        "ln_b": c(i["L0_ffn_ln_hid_b"][None]),
        "ln_out_w": c(i["L0_ffn_ln_out_w"][None]),
        "ln_out_b": c(i["L0_ffn_ln_out_b"][None]),
        "gamma": c(i["L1_attn_gamma"][:, None]),
        "qkv": c(qkv),
        "wo": c(i["L1_attn_w_out"].T.reshape(NH, D, D).transpose(1, 0, 2)),
        "wg1": c(i["L1_ffn_wg"]),
        "we": c(i["L1_ffn_we"]),
        "ident": np.eye(P, dtype=np.float32),
        "ident_bf": np.eye(P, dtype=np.float32).astype(bf16),
        "mask_bf": (np.triu(np.ones((P, P), np.float32), 1) * np.float32(-1e30)).astype(bf16),
        "tri": np.triu(np.ones((P, P), np.float32), 1).astype(bf16),
        "ones": np.ones((P, P), bf16),
        "iota": np.tile(np.arange(P, dtype=np.float32), (P, 1)),
        "pcol": np.arange(P, dtype=np.float32)[:, None].copy(),
        "group_base": np.tile(np.arange(HG, dtype=np.float32) * (E0 * C0), (P, 1)),
        "sel": c(sel.reshape(96, 2 * DS * P)),
    }


def kernel(**inputs):
    import concourse.bacc as bacc
    from concourse.bass_utils import run_bass_kernel_spmd

    nc = bacc.Bacc("TRN2", target_bir_lowering=False, num_devices=1)
    arrays = laid_out({n: np.asarray(v) for n, v in inputs.items()})
    a = {n: nc.dram_tensor(n, v.shape, mybir.dt.from_np(v.dtype), kind="ExternalInput").ap() for n, v in arrays.items()}
    out = nc.dram_tensor("out", (P, NT, D), F32, kind="ExternalOutput").ap()
    program(nc, a, out)
    r = run_bass_kernel_spmd(nc, [arrays], core_ids=[0])
    got = r.results[0]["out"]
    return np.ascontiguousarray(got.transpose(1, 0, 2)).reshape(B, L, D)
```

```python
from contextlib import ExitStack

import numpy as np
import concourse.bass as bass
from concourse import mybir

F32 = mybir.dt.float32
BF16 = mybir.dt.bfloat16
U32 = mybir.dt.uint32
ALU = mybir.AluOpType
ACT = mybir.ActivationFunctionType
AX_X = mybir.AxisListType.X

P = 128
B, L, D = 8, 512, 128
N_TOK = B * L
NT = N_TOK // P
TB = L // P
DI, DS, DTR, KC = 256, 16, 8, 4
HALF = DI // P
DFF = 512
FC = DFF // P
PAD = L + KC - 1

HG, E0, C0, HID = 4, 24, 86, 512
E1, C1 = 128, 32


class Chain:

    def __init__(self, eng, sem):
        self.eng, self.sem, self.n = eng, sem, 0

    def __call__(self, ins):
        self.n += 1
        ins.then_inc(self.sem, 1)
        self.eng.wait_ge(self.sem, self.n)
        return ins


class Scope:

    def __init__(self, nc, ctx, tag):
        self.nc, self.ctx, self.tag = nc, ctx, tag

    def sb(self, name, shape, dt=F32):
        return self.ctx.enter_context(self.nc.sbuf_tensor(f"{self.tag}_{name}", shape, dt))

    def ps(self, name, shape, dt=F32):
        return self.ctx.enter_context(self.nc.psum_tensor(f"{self.tag}_{name}", shape, dt))

    def sem(self, name):
        return self.ctx.enter_context(self.nc.semaphore(f"{self.tag}_{name}"))


class Arena:

    def __init__(self, buf):
        self.buf, self.used = buf, 0

    def sb(self, name, shape, dt=F32):
        per_row = int(np.prod(shape[1:]))
        words = -(-per_row * mybir.dt.size(dt) // 4)
        part = self.buf[0:shape[0], self.used:self.used + words]
        self.used += words
        assert self.used <= self.buf.shape[1], name
        if dt is not F32:
            part = part.bitcast(dt)[:, 0:per_row]
        dims = "abcd"[:len(shape) - 1]
        return part.rearrange(f"p ({' '.join(dims)}) -> p {' '.join(dims)}", **dict(zip(dims, shape[1:])))


def bcast(ap, n):
    return ap.unsqueeze(2).broadcast_to([ap.shape[0], ap.shape[1], n])


def layernorm_stage(nc, src_dram, xn_dram, x_rows, xn_rows, xnT, ident, tag, loads):
    G = 4
    steps = NT // G
    with ExitStack() as ctx:
        s = Scope(nc, ctx, tag)
        stats = s.sb("stats", [P, NT, 6])
        mv = s.sb("mv", [P, NT, 2])
        nm = s.sb("nm", [P, NT])
        rstd = s.sb("rstd", [P, NT])
        pt = s.ps("pt", [P, 4, L])
        x_in = [s.sem(f"x_in{i}") for i in range(4)]
        consts_in = s.sem("consts_in")
        chain = s.sem("chain")
        var_ready = s.sem("var_ready")
        root_ready = s.sem("root_ready")
        scale_ready = s.sem("scale_ready")
        normed = s.sem("normed")
        turned = s.sem("turned")
        evacuated = s.sem("evacuated")
        stored = s.sem("stored")
        block = ctx.enter_context(nc.Block())

        @block.sync
        def _(sp):
            if src_dram is not None:
                for h in range(4):
                    sp.dma_start(x_rows[:, h * 8:(h + 1) * 8, :],
                                 src_dram[:, h * 8:(h + 1) * 8, :]).then_inc(x_in[h], 16)
            for dst, src in loads:
                sp.dma_start(dst, src).then_inc(consts_in, 16)
            for g in range(steps):
                sp.wait_ge(normed, g + 1)
                sp.dma_start(xn_dram[:, g * G:(g + 1) * G, :], xn_rows[:, g * G:(g + 1) * G, :]).then_inc(stored, 16)
            sp.wait_ge(stored, 16 * steps)
            if loads:
                sp.wait_ge(consts_in, 16 * len(loads))

        @block.vector
        def _(dve):
            link = Chain(dve, chain)
            v = nc.vector
            link(v.memset(xnT[:, :, 0:KC - 1], 0.0))
            for g in range(steps + 1):
                if g < steps:
                    t = slice(g * G, (g + 1) * G)
                    if src_dram is not None and g % 2 == 0:
                        dve.wait_ge(x_in[g // 2], 16)
                    for n in range(g * G, (g + 1) * G):
                        ins = v.bn_stats(stats[:, n, :], x_rows[:, n, :])
                    link(ins)
                    for n in range(g * G, (g + 1) * G):
                        ins = v.bn_aggr(mv[:, n, :], stats[:, n, :])
                    link(ins)
                    v.tensor_scalar(rstd[:, t], mv[:, t, 1], 1e-5, None, ALU.add).then_inc(var_ready, 1)
                if g:
                    t = slice((g - 1) * G, g * G)
                    dve.wait_ge(root_ready, g)
                    link(v.reciprocal(rstd[:, t], rstd[:, t]))
                    v.scalar_tensor_tensor(out=nm[:, t], in0=mv[:, t, 0], scalar=-1.0, in1=rstd[:, t],
                                           op0=ALU.mult, op1=ALU.mult).then_inc(scale_ready, 1)

        @block.tensor
        def _(pe):
            if loads:
                pe.wait_ge(consts_in, 16 * len(loads))
            for g in range(steps):
                pe.wait_ge(normed, g + 1)
                if g >= 4:
                    pe.wait_ge(evacuated, g - 3)
                for j in range(G):
                    last = nc.tensor.transpose(pt[:, g % 4, j * P:(j + 1) * P], xn_rows[:, g * G + j, :], ident)
                last.then_inc(turned, 1)

        @block.scalar
        def _(act):
            for g in range(steps + 2):
                if g < steps:
                    t = slice(g * G, (g + 1) * G)
                    act.wait_ge(var_ready, g + 1)
                    nc.scalar.activation(rstd[:, t], rstd[:, t], ACT.Sqrt).then_inc(root_ready, 1)
                if 1 <= g <= steps:
                    act.wait_ge(scale_ready, g)
                    for n in range((g - 1) * G, g * G):
                        ins = nc.scalar.activation(xn_rows[:, n, :], x_rows[:, n, :], ACT.Identity,
                                                   scale=rstd[:, n:n + 1], bias=nm[:, n:n + 1])
                    ins.then_inc(normed, 1)
                if g >= 2:
                    act.wait_ge(turned, g - 1)
                    nc.scalar.activation(xnT[:, g - 2, KC - 1:PAD], pt[:, (g - 2) % 4, :],
                                         ACT.Copy).then_inc(evacuated, 1)


def mamba_input_stage(nc, w, xnT, xT, zT, beside):
    with ExitStack() as ctx:
        s = Scope(nc, ctx, "mi")
        taps = s.sb("taps", [P, KC, DI])
        pj = s.ps("pj", [P, 3, L])
        chain = s.sem("chain")
        folded = s.sem("folded")
        product = s.sem("product")
        activated = s.sem("activated")
        block = ctx.enter_context(nc.Block())

        @block.vector
        def _(dve):
            for k in range(KC):
                nc.vector.tensor_tensor(taps[:, k, :], w["in_T"][:, 0:DI], w["conv_rows"][:, k, :],
                                        ALU.mult).then_inc(folded, 1)
            for _ in beside.vector(dve):
                pass
        def tensor_steps(pe):
            yield
            pe.wait_ge(folded, KC)
            for n in range(B * 4):
                b, e = divmod(n, 4)
                if n >= 3:
                    pe.wait_ge(activated, n - 2)
                if e < HALF:
                    for k in range(KC):
                        last = nc.tensor.matmul(pj[:, n % 3, :], taps[:, k, e * P:(e + 1) * P],
                                                xnT[:, b, k:k + L], start=(k == 0), stop=(k == KC - 1))
                else:
                    last = nc.tensor.matmul(pj[:, n % 3, :], w["in_T"][:, e * P:(e + 1) * P],
                                            xnT[:, b, KC - 1:PAD], start=True, stop=True)
                last.then_inc(product, 1)
                yield

        def scalar_steps(act):
            yield
            for n in range(B * 4):
                b, e = divmod(n, 4)
                act.wait_ge(product, n + 1)
                if e < HALF:
                    nc.scalar.activation(xT[:, e, b * L:(b + 1) * L], pj[:, n % 3, :], ACT.Silu,
                                         bias=w["conv_b"][:, e:e + 1]).then_inc(activated, 1)
                else:
                    nc.scalar.activation(zT[:, e - HALF, b * L:(b + 1) * L], pj[:, n % 3, :],
                                         ACT.Silu).then_inc(activated, 1)
                yield

        @block.tensor
        def _(pe):
            side_by_side(tensor_steps(pe), beside.tensor(pe))

        @block.scalar
        def _(act):
            side_by_side(scalar_steps(act), beside.scalar(act))


def side_by_side(main, beside):
    for _ in main:
        next(beside, None)
    for _ in beside:
        pass


PE_SLOTS, ACT_SLOTS, DVE_SLOTS = 4, 2, 2


def scan_stage(nc, w, xT, zT, spare, beside):
    PAIRS = DS // 2
    STEPS = B * PAIRS
    RS = 4
    with ExitStack() as ctx:
        s = Scope(nc, ctx, "sc")
        negA = spare.sb("negA", [P, 2, DS])
        bc3 = s.sb("bc3", [96, 2, L], BF16)
        rest = spare.sb("rest", [96, L])
        mid = spare.sb("mid", [96, L], BF16)
        dtr = s.sb("dtr", [DTR, L])
        dt = s.sb("dt", [P, 2, 2, L])
        u = s.sb("u", [P, 2, 2, L])
        lost = spare.sb("lost", [P, L])
        logs = s.sb("logs", [P, 2, L])
        dA = s.sb("dA", [P, 4, 2, L])
        st = s.sb("st", [P, RS, 2, L])
        p_b = s.ps("p_b", [P, L])
        p_c = s.ps("p_c", [P, 2, L])
        p_y = s.ps("p_y", [P, 2, L])
        p_x = s.ps("p_x", [P, L])
        chain = s.sem("chain")
        a_chain = s.sem("a_chain")
        exp_A = s.sem("exp_A")
        neg_A = s.sem("neg_A")
        cleared = s.sem("cleared")
        xp_ready = s.sem("xp_ready")
        dr_copied = s.sem("dr_copied")
        bc_read = s.sem("bc_read")
        bc_done = s.sem("bc_done")
        dt_product = s.sem("dt_product")
        mag_read = s.sem("mag_read")
        relu_read = s.sem("relu_read")
        ln_ready = s.sem("ln_ready")
        dt_done = s.sem("dt_done")
        b_ready = s.sem("b_ready")
        b_used = s.sem("b_used")
        c_ready = s.sem("c_ready")
        hc_ready = s.sem("hc_ready")
        pair_added = s.sem("pair_added")
        hc_used = s.sem("hc_used")
        decay_ready = s.sem("decay_ready")
        scanned = s.sem("scanned")
        y_used = s.sem("y_used")
        gated = s.sem("gated")
        block = ctx.enter_context(nc.Block())

        def pairs_added(i):
            return sum(not beside.pool_busy(n + 1) for n in range(i))

        def scalar_steps(act):
            link = Chain(act, a_chain)

            def copy_dt_rank(b):
                act.wait_ge(xp_ready, b + 1)
                if b:
                    act.wait_ge(dt_product, 2 * b)
                nc.scalar.activation(dtr[:, :], p_x[96:96 + DTR, :], ACT.Copy).then_inc(dr_copied, 1)

            def softplus_logs(b, h):
                n = 2 * b + h
                act.wait_ge(dt_product, n + 1)
                if n:
                    act.wait_ge(dt_done, n)
                if h == 0 and b >= 2:
                    act.wait_ge(gated, b - 1)
                nc.scalar.activation(lost[:, :], p_x[:, :], ACT.Abs, bias=w["dt_b"][:, h:h + 1]).then_inc(mag_read, 1)
                act.wait_ge(mag_read, n + 1)
                link(nc.scalar.activation(logs[:, 0, :], lost[:, :], ACT.Exp, scale=-1.0))
                nc.scalar.activation(logs[:, 1, :], logs[:, 0, :], ACT.Ln, bias=1.0).then_inc(ln_ready, 1)

            nc.scalar.activation(negA[:, :, :], w["A_log"][:, :, :], ACT.Exp).then_inc(exp_A, 1)
            copy_dt_rank(0)
            softplus_logs(0, 0)
            softplus_logs(0, 1)
            act.wait_ge(cleared, 1)
            act.wait_ge(neg_A, 1)

            def decays(i, h):
                b, q = divmod(i, PAIRS)
                m = 2 * i + h
                if q == 0:
                    act.wait_ge(dt_done, 2 * b + h + 1)
                if m >= 4:
                    act.wait_ge(scanned, m - 3)
                for j in range(2):
                    ins = nc.scalar.activation(dA[:, m % 4, j, 1:L], dt[:, b % 2, h, 1:L], ACT.Exp,
                                               scale=negA[:, h, 2 * q + j:2 * q + j + 1])
                ins.then_inc(decay_ready, 1)

            decays(0, 0)
            decays(0, 1)
            copy_dt_rank(1)
            for i in range(STEPS):
                b, q = divmod(i, PAIRS)
                if i + 1 < STEPS:
                    decays(i + 1, 0)
                yield
                if i + 1 < STEPS:
                    decays(i + 1, 1)
                yield
                if b + 1 < B:
                    if q == 1:
                        softplus_logs(b + 1, 0)
                    if q == 4:
                        softplus_logs(b + 1, 1)
                if b + 2 < B and q == 7:
                    copy_dt_rank(b + 2)

        def tensor_steps(pe):
            def x_project(b):
                if b:
                    pe.wait_ge(relu_read, 2 * b)
                for h in range(HALF):
                    ins = nc.tensor.matmul(p_x[0:96 + DTR, :], w["xproj_T"][:, h, :], xT[:, h, b * L:(b + 1) * L],
                                           start=(h == 0), stop=(h == 1))
                ins.then_inc(xp_ready, 1)

            def dt_project(b, h):
                n = 2 * b + h
                pe.wait_ge(dr_copied, b + 1)
                if h == 0:
                    pe.wait_ge(bc_read, b + 1)
                else:
                    pe.wait_ge(relu_read, n)
                nc.tensor.matmul(p_x[:, :], w["dt_T"][:, h * P:(h + 1) * P], dtr[:, :],
                                 start=True, stop=True).then_inc(dt_product, 1)

            def broadcast_b(i, j):
                b, q = divmod(i, PAIRS)
                if q == 0 and j == 0:
                    pe.wait_ge(bc_done, b + 1)
                if i or j:
                    pe.wait_ge(b_used, 2 * i + j)
                n = 2 * q + j
                nc.tensor.matmul(p_b[:, :], w["sel"][:, n * P:(n + 1) * P], bc3[:, b % 2, :], start=True,
                                 stop=True).then_inc(b_ready, 1)

            def broadcast_c(i):
                b, q = divmod(i, PAIRS)
                if i:
                    pe.wait_ge(hc_ready, 2 * i)
                for j in range(2):
                    n = DS + 2 * q + j
                    ins = nc.tensor.matmul(p_c[:, j, :], w["sel"][:, n * P:(n + 1) * P], bc3[:, b % 2, :],
                                           start=True, stop=True)
                ins.then_inc(c_ready, 1)

            def sum_states(i, h):
                b, q = divmod(i, PAIRS)
                if q == 0 and b and h == 0:
                    pe.wait_ge(y_used, b)
                if beside.pool_busy(i + 1):
                    pe.wait_ge(hc_ready, 2 * i + h + 1)
                    nc.tensor.matmul(p_y[:, h, :], w["ident"], st[:, (2 * i + h) % RS, 1, :], start=(q == 0),
                                     stop=False)
                else:
                    pe.wait_ge(pair_added, 2 * pairs_added(i) + h + 1)
                nc.tensor.matmul(p_y[:, h, :], w["ident"], st[:, (2 * i + h) % RS, 0, :],
                                 start=(q == 0 and not beside.pool_busy(i + 1)),
                                 stop=(q == PAIRS - 1)).then_inc(hc_used, 1)

            x_project(0)
            dt_project(0, 0)
            dt_project(0, 1)
            x_project(1)
            broadcast_b(0, 0)
            for i in range(STEPS):
                b, q = divmod(i, PAIRS)
                broadcast_b(i, 1)
                if b + 1 < B:
                    if q == 1:
                        dt_project(b + 1, 0)
                    if q == 3:
                        dt_project(b + 1, 1)
                if b + 2 < B and q == 7:
                    x_project(b + 2)
                yield
                if i + 1 < STEPS:
                    broadcast_b(i + 1, 0)
                if i:
                    sum_states(i - 1, 0)
                broadcast_c(i)
                yield
                if i:
                    sum_states(i - 1, 1)
                yield
                yield
            sum_states(STEPS - 1, 0)
            sum_states(STEPS - 1, 1)

        def pool_steps(pool):
            def add_pair(i):
                if beside.pool_busy(i + 1):
                    return
                for h in range(HALF):
                    m = 2 * i + h
                    pool.wait_ge(hc_ready, m + 1)
                    nc.gpsimd.tensor_tensor(st[:, m % RS, 0, :], st[:, m % RS, 0, :], st[:, m % RS, 1, :],
                                            ALU.add).then_inc(pair_added, 1)

            for i in range(STEPS):
                if i:
                    add_pair(i - 1)
                yield
            add_pair(STEPS - 1)

        def vector_steps(dve):
            link = Chain(dve, chain)
            dve.wait_ge(exp_A, 1)
            nc.vector.tensor_scalar(negA[:, :, :], negA[:, :, :], -1.0, None, ALU.mult).then_inc(neg_A, 1)
            nc.vector.memset(dA[:, :, :, 0:1], 0.0).then_inc(cleared, 1)

            def split_bc(b):
                dve.wait_ge(dr_copied, b + 1)
                hi = bc3[:, b % 2, :]
                link(nc.vector.tensor_copy(hi, p_x[0:96, :]))
                nc.vector.tensor_tensor(rest[:, :], p_x[0:96, :], hi, ALU.subtract).then_inc(bc_read, 1)
                dve.wait_ge(bc_read, b + 1)
                link(nc.vector.tensor_copy(mid[:, :], rest[:, :]))
                nc.vector.tensor_copy(bc3[32:64, b % 2, :], mid[32:64, :])
                nc.vector.tensor_tensor(bc3[64:96, b % 2, :], rest[64:96, :], mid[64:96, :],
                                        ALU.subtract).then_inc(bc_done, 1)
                dve.wait_ge(bc_done, b + 1)

            def relu(b, h):
                n = 2 * b + h
                dve.wait_ge(mag_read, n + 1)
                nc.vector.tensor_scalar(dt[:, b % 2, h, :], p_x[:, :], w["dt_b"][:, h:h + 1], 0.0,
                                        ALU.add, ALU.max).then_inc(relu_read, 1)

            def softplus(b, h):
                n = 2 * b + h
                em = logs[:, 0, :]
                dve.wait_ge(relu_read, n + 1)
                dve.wait_ge(ln_ready, n + 1)
                link(nc.vector.tensor_scalar(lost[:, :], em, 1.0, 1.0, ALU.add, ALU.subtract))
                link(nc.vector.tensor_tensor(lost[:, :], em, lost[:, :], ALU.subtract))
                link(nc.vector.tensor_tensor(lost[:, :], lost[:, :], logs[:, 1, :], ALU.add))
                nc.vector.tensor_tensor(dt[:, b % 2, h, :], dt[:, b % 2, h, :], lost[:, :], ALU.add).then_inc(dt_done, 1)
                dve.wait_ge(dt_done, n + 1)
                link(nc.vector.tensor_tensor(u[:, b % 2, h, :], dt[:, b % 2, h, :], xT[:, h, b * L:(b + 1) * L],
                                             ALU.mult))

            def gate(b):
                cols = slice(b * L, (b + 1) * L)
                dve.wait_ge(hc_used, 2 * PAIRS * (b + 1))
                for h in range(HALF):
                    ins = nc.vector.scalar_tensor_tensor(out=logs[:, h, :], in0=xT[:, h, cols],
                                                         scalar=w["D"][:, h:h + 1], in1=p_y[:, h, :],
                                                         op0=ALU.mult, op1=ALU.add)
                ins.then_inc(y_used, 1)
                dve.wait_ge(y_used, b + 1)
                for h in range(HALF):
                    ins = nc.vector.tensor_tensor(zT[:, h, cols], logs[:, h, :], zT[:, h, cols], ALU.mult)
                ins.then_inc(gated, 1)

            def times_b(i, j):
                b, q = divmod(i, PAIRS)
                dve.wait_ge(b_ready, 2 * i + j + 1)
                for h in range(HALF):
                    m = 2 * i + h
                    if m >= RS and j == 0:
                        dve.wait_ge(hc_used, m - RS + 1)
                    ins = nc.vector.tensor_tensor(st[:, m % RS, j, :], p_b[:, :], u[:, b % 2, h, :], ALU.mult)
                ins.then_inc(b_used, 1)

            def times_c(i, h):
                m = 2 * i + h
                dve.wait_ge(c_ready, i + 1)
                dve.wait_ge(scanned, m + 1)
                nc.vector.tensor_tensor(st[:, m % RS, :, :], st[:, m % RS, :, :], p_c[:, :, :],
                                        ALU.mult).then_inc(hc_ready, 1)

            split_bc(0)
            for h in range(HALF):
                relu(0, h)
                softplus(0, h)
            for i in range(STEPS):
                b, q = divmod(i, PAIRS)
                times_b(i, 0)
                if i:
                    times_c(i - 1, 0)
                if q == 1 and b:
                    gate(b - 1)
                times_b(i, 1)
                if i:
                    times_c(i - 1, 1)
                yield
                dve.wait_ge(b_used, 2 * i + 2)
                for h in range(HALF):
                    m = 2 * i + h
                    dve.wait_ge(decay_ready, m + 1)
                    nc.vector.tensor_tensor_scan(st[:, m % RS, :, :].rearrange("p a b -> p (a b)"),
                                                 dA[:, m % 4, :, :].rearrange("p a b -> p (a b)"),
                                                 st[:, m % RS, :, :].rearrange("p a b -> p (a b)"),
                                                 0.0, ALU.mult, ALU.add).then_inc(scanned, 1)
                if b + 1 < B:
                    if q == 0:
                        split_bc(b + 1)
                    if q in (2, 5):
                        relu(b + 1, (q - 2) // 3)
                    if q in (3, 6):
                        softplus(b + 1, (q - 3) // 3)
                yield
            times_c(STEPS - 1, 0)
            times_c(STEPS - 1, 1)
            gate(B - 1)

        @block.scalar
        def _(act):
            side_by_side(scalar_steps(act), beside.scalar(act))

        @block.tensor
        def _(pe):
            side_by_side(tensor_steps(pe), beside.tensor(pe))

        @block.gpsimd
        def _(pool):
            side_by_side(pool_steps(pool), beside.pool(pool))

        @block.vector
        def _(dve):
            side_by_side(vector_steps(dve), beside.vector(dve))

        @block.sync
        def _(sp):
            beside.sync(sp)


def mamba_output_stage(nc, w, yT, xn_rows, s_rows, beside):
    with ExitStack() as ctx:
        s = Scope(nc, ctx, "mo")
        z = s.sb("z", [P, NT, D])
        zT = s.sb("zT", [P, 2, L])
        hT = s.sb("hT", [P, 2, FC, L])
        sq = s.sb("sq", [P, TB, D])
        acc = s.sb("acc", [P, NT])
        eps = s.sb("eps", [P, 1])
        root = s.sb("root", [P, NT])
        p_o = s.ps("p_o", [P, L])
        p_t = s.ps("p_t", [P, 2, L])
        p_h = s.ps("p_h", [P, 3, L])
        p_m = s.ps("p_m", [P, L])
        chain = s.sem("chain")
        projected = s.sem("projected")
        o_used = s.sem("o_used")
        a_chain = s.sem("a_chain")
        eps_set = s.sem("eps_set")
        root_ready = s.sem("root_ready")
        z_ready = s.sem("z_ready")
        z_turned = s.sem("z_turned")
        zT_ready = s.sem("zT_ready")
        h_product = s.sem("h_product")
        h_ready = s.sem("h_ready")
        m_product = s.sem("m_product")
        m_used = s.sem("m_used")
        s_ready = s.sem("s_ready")
        beside.s_ready = s_ready
        block = ctx.enter_context(nc.Block())

        def tensor_steps(pe):
            pe.wait_ge(beside.weights_in, 16 * len(beside.weights))
            for b in range(B):
                if b:
                    pe.wait_ge(o_used, b)
                for j in range(TB):
                    for h in range(HALF):
                        ins = nc.tensor.matmul(p_o[:, j * D:(j + 1) * D], yT[:, h, b * L + j * P:b * L + (j + 1) * P],
                                               w["out_T"][:, h, :], start=(h == 0), stop=(h == 1))
                ins.then_inc(projected, 1)
                yield
            yield

            def hidden(b):
                pe.wait_ge(z_ready, b + 1)
                if b >= 2:
                    pe.wait_ge(zT_ready, b - 1)
                for j in range(TB):
                    ins = nc.tensor.transpose(p_t[:, b % 2, j * P:(j + 1) * P], z[:, b * TB + j, :], w["ident"])
                ins.then_inc(z_turned, 1)
                pe.wait_ge(zT_ready, b + 1)
                for f in range(FC):
                    n = FC * b + f
                    if n >= 3:
                        pe.wait_ge(h_ready, n - 2)
                    nc.tensor.matmul(p_h[:, n % 3, :], w["w1_T"][:, f * P:(f + 1) * P], zT[:, b % 2, :],
                                     start=True, stop=True).then_inc(h_product, 1)

            hidden(0)
            for b in range(B):
                if b + 1 < B:
                    hidden(b + 1)
                pe.wait_ge(h_ready, FC * (b + 1))
                if b:
                    pe.wait_ge(m_used, b)
                for j in range(TB):
                    for f in range(FC):
                        ins = nc.tensor.matmul(p_m[:, j * D:(j + 1) * D], hT[:, b % 2, f, j * P:(j + 1) * P],
                                               w["w2_T"][:, f, :], start=(f == 0), stop=(f == FC - 1))
                ins.then_inc(m_product, 1)
                yield

        def scalar_steps(act):
            act.wait_ge(beside.weights_in, 16 * len(beside.weights))
            link = Chain(act, a_chain)
            act.wait_ge(eps_set, 1)

            def squares(v, b):
                for t in range(b * TB, (b + 1) * TB):
                    ins = nc.scalar.activation(sq[:, t % TB, :], v[:, t, :], ACT.Square, accum_out=acc[:, t:t + 1])
                link(ins)

            def roots(t):
                nc.scalar.activation(root[:, t], acc[:, t], ACT.Sqrt, scale=1.0 / D,
                                     bias=eps[:, 0:1]).then_inc(root_ready, 1)

            for b in range(B):
                act.wait_ge(o_used, b + 1)
                squares(z, b)
                roots(slice(b * TB, (b + 1) * TB))
                yield
            yield
            for b in range(B):
                act.wait_ge(z_turned, b + 1)
                if b >= 2:
                    act.wait_ge(h_product, FC * (b - 1))
                nc.scalar.activation(zT[:, b % 2, :], p_t[:, b % 2, :], ACT.Copy).then_inc(zT_ready, 1)
                for f in range(FC):
                    n = FC * b + f
                    act.wait_ge(h_product, n + 1)
                    if b >= 2 and f == 0:
                        act.wait_ge(m_product, b - 1)
                    nc.scalar.activation(hT[:, b % 2, f, :], p_h[:, n % 3, :], ACT.Gelu,
                                         bias=w["b1"][:, f:f + 1]).then_inc(h_ready, 1)
                if b >= 2:
                    act.wait_ge(m_used, b - 1)
                    squares(s_rows, b - 2)
                yield
            for b in (B - 2, B - 1):
                act.wait_ge(m_used, b + 1)
                squares(s_rows, b)
            roots(slice(0, NT))

        def vector_steps(dve):
            link = Chain(dve, chain)
            nc.vector.memset(eps[:, :], 1e-6).then_inc(eps_set, 1)
            dve.wait_ge(beside.weights_in, 16 * len(beside.weights))

            def rows(p):
                return p[:, :].rearrange("p (a d) -> p a d", d=D)

            def scale(v, t, signal):
                n = t.stop - t.start
                link(nc.vector.reciprocal(root[:, t], root[:, t]))
                for k in range(n):
                    ins = nc.vector.scalar_tensor_tensor(out=v[:, k, :], in0=v[:, k, :],
                                                         scalar=root[:, t.start + k:t.start + k + 1],
                                                         in1=w["norm1"], op0=ALU.mult, op1=ALU.mult)
                if signal is None:
                    link(ins)
                else:
                    ins.then_inc(signal, 1)

            for b in range(B + 1):
                if b < B:
                    t = slice(b * TB, (b + 1) * TB)
                    dve.wait_ge(beside.xn_in[b], 16)
                    dve.wait_ge(projected, b + 1)
                    nc.vector.tensor_tensor(z[:, t, :], rows(p_o), xn_rows[:, t, :], ALU.add).then_inc(o_used, 1)
                if b:
                    dve.wait_ge(root_ready, b)
                    t = slice((b - 1) * TB, b * TB)
                    scale(z[:, t, :], t, z_ready)
                yield
            dve.wait_ge(z_ready, B)
            for b in range(B):
                t = slice(b * TB, (b + 1) * TB)
                link(nc.vector.tensor_tensor(s_rows[:, t, :], z[:, t, :],
                                             w["b2"][:, :].unsqueeze(1).broadcast_to([P, TB, D]), ALU.add))
                dve.wait_ge(m_product, b + 1)
                nc.vector.tensor_tensor(s_rows[:, t, :], rows(p_m), s_rows[:, t, :], ALU.add).then_inc(m_used, 1)
                yield
            dve.wait_ge(root_ready, B + 1)
            for c in range(4):
                t = slice(c * 8, (c + 1) * 8)
                scale(s_rows[:, t, :], t, s_ready)

        @block.tensor
        def _(pe):
            side_by_side(tensor_steps(pe), beside.tensor(pe))

        @block.scalar
        def _(act):
            side_by_side(scalar_steps(act), beside.scalar(act))

        @block.vector
        def _(dve):
            side_by_side(vector_steps(dve), beside.vector(dve))

        @block.gpsimd
        def _(pool):
            side_by_side((None for _ in range(2 * B + 1)), beside.pool(pool))

        @block.sync
        def _(sp):
            beside.sync(sp)


class Routing:
    pass


GT_BATCHES = 3


def gate_rows(GT, t, n=1):
    stripe, at = divmod(t, GT_BATCHES * TB)
    return GT[32 * stripe:32 * stripe + E0, at * P:(at + n) * P]


def expert_biases(b, t):
    stripe = t // (GT_BATCHES * TB)
    return b[32 * stripe:32 * stripe + E0, :]


class Programs:

    def __init__(self, tensor, scalar, vector):
        self.tensor, self.scalar, self.vector = tensor, scalar, vector


def routing_programs(nc, ctx, w, r, xnT, wg, cfg, tag, scratch):
    E, C, groups, LO, HI, masked_first, floor = (cfg[x] for x in ("E", "C", "groups", "LO", "HI", "masked", "floor"))
    gaps = cfg["gaps"]
    steps = NT // groups
    width = groups * E
    TC = 16 if E < 32 else 4
    NCH = NT // TC
    PL = min(NCH, 4)
    split = HI < E
    s = Scope(nc, ctx, tag)
    lg = scratch.sb("lg", [P, NT, E])
    ex = scratch.sb("ex", [P, NT, E])
    mx = scratch.sb("mx", [P, NT, 8])
    ix = scratch.sb("ix", [P, NT, 8], U32)
    idx = scratch.sb("idx", [P, 2, NT])
    lo_e = scratch.sb("lo_e", [P, 2, NT])
    hi_e = scratch.sb("hi_e", [P, 2, NT])
    bits = scratch.sb("bits", [P, 2, NT], U32)
    m = [scratch.sb(f"m{k}", [P, NT, E], BF16) for k in range(2)]
    acc = [scratch.sb(f"acc{k}", [P, steps + 1, width], BF16) for k in range(2)]
    mh = scratch.sb("mh", [P, NT, HI], BF16)
    loc = scratch.sb("loc", [P, 2, NT])
    valid = scratch.sb("valid", [P, 2, NT])
    lo = scratch.sb("lo", [P, 2, NT])
    A = [scratch.sb(f"A{k}", [P, NT, LO], BF16) for k in range(2)]
    R = [scratch.sb(f"R{k}", [P, NT, 2, HI], BF16) for k in range(2)]
    S = scratch.sb("S", [P, NT])
    d21 = scratch.sb("d21", [P, NT])
    nmx = scratch.sb("nmx", [P, NT])
    g = scratch.sb("g", [P, 2, NT])
    den = scratch.sb("den", [P, NT])
    rows = scratch.sb("rows", [P, 2, NT])
    tabf = scratch.sb("tabf", [LO, groups, HI])
    p_l = s.ps("p_l", [P, PL, 512])
    p_n = s.ps("p_n", [P, 2, 512])
    p_t = s.ps("p_t", [LO, 512])
    chain = s.sem("chain")
    logits = s.sem("logits")
    logits_used = s.sem("logits_used")
    masks = s.sem("masks")
    counted = s.sem("counted")
    count_used = s.sem("count_used")
    shifted = s.sem("shifted")
    exps = s.sem("exps")
    onehots = s.sem("onehots")
    low, high = (lo, hi_e) if split else (loc, idx)
    table = s.sem("table")
    g_ready = s.sem("g_ready")
    g_turned = s.sem("g_turned")
    g_copied = s.sem("g_copied")

    def tensor(pe):
        for t in range(NT):
            c, j = divmod(t, TC)
            b, q = divmod(t, TB)
            if j == 0 and c >= PL:
                pe.wait_ge(logits_used, c - PL + 1)
            ins = nc.tensor.matmul(p_l[:, c % PL, j * E:(j + 1) * E],
                                   xnT[:, b, KC - 1 + q * P:KC - 1 + (q + 1) * P], wg, start=True, stop=True)
            if j == TC - 1:
                ins.then_inc(logits, 1)
        yield from [None] * gaps[0]
        pe.wait_ge(masks, 1)
        for k in range(2):
            for c in range(NCH):
                n = k * NCH + c
                if n >= 2:
                    pe.wait_ge(count_used, n - 1)
                cols = TC * E
                steps_c = TC // groups
                out = p_n[:, n % 2, 0:cols]
                nc.tensor.matmul(out, w["tri"], m[k][:, c * TC:(c + 1) * TC, :].rearrange("p a b -> p (a b)"),
                                 start=True, stop=False)
                last = k == 0
                ins = nc.tensor.matmul(out, w["ones"],
                                       acc[k][:, c * steps_c:(c + 1) * steps_c, :].rearrange("p a b -> p (a b)"),
                                       start=False, stop=last)
                if k:
                    total = acc[0][:, steps:steps + 1, :].broadcast_to([P, steps_c, width])
                    ins = nc.tensor.matmul(out, w["ones"], total, start=False, stop=True)
                ins.then_inc(counted, 1)
        yield from [None] * gaps[1]
        pe.wait_ge(onehots, 1)
        for h in range(groups):
            for i in range(steps):
                t = i * groups + h
                for k in range(2):
                    ins = nc.tensor.matmul(p_t[:, h * 2 * HI:(h + 1) * 2 * HI], A[k][:, t, :],
                                           R[k][:, t, :, :].rearrange("p a b -> p (a b)"),
                                           start=(i == 0 and k == 0), stop=(i == steps - 1 and k == 1))
        ins.then_inc(table, 1)
        if r.GT is not None:
            yield from [None] * gaps[2]
            pe.wait_ge(g_ready, 1)
            for b in range(B):
                if b >= 2:
                    pe.wait_ge(g_copied, b - 1)
                for j in range(TB):
                    ins = nc.tensor.transpose(p_l[0:E, b % 2, j * P:(j + 1) * P], ex[:, b * TB + j, :], w["ident"])
                ins.then_inc(g_turned, 1)

    def scalar(act):
        yield from [None] * gaps[3]
        act.wait_ge(shifted, 1)
        for t in range(NT):
            nc.scalar.activation(ex[:, t, :], lg[:, t, :], ACT.Exp, bias=nmx[:, t:t + 1],
                                 accum_out=S[:, t:t + 1]).then_inc(exps, 1)
        nc.scalar.activation(d21[:, :], d21[:, :], ACT.Exp).then_inc(exps, 1)
        yield from [None] * (sum(gaps[0:3]) - gaps[3])
        if r.GT is not None:
            for b in range(B):
                act.wait_ge(g_turned, b + 1)
                nc.scalar.activation(gate_rows(r.GT, b * TB, TB), p_l[0:E, b % 2, :], ACT.Copy).then_inc(g_copied, 1)

    def vector(dve):
        link = Chain(dve, chain)
        v = nc.vector
        for c in range(NCH):
            dve.wait_ge(logits, c + 1)
            v.tensor_copy(lg[:, c * TC:(c + 1) * TC, :],
                          p_l[:, c % PL, 0:TC * E].rearrange("p (a b) -> p a b", b=E)).then_inc(logits_used, 1)
        dve.wait_ge(logits_used, NCH)
        for t in range(NT):
            ins = v.max(mx[:, t, :], lg[:, t, :])
        link(ins)
        for t in range(NT):
            ins = v.max_index(ix[:, t, :], mx[:, t, :], lg[:, t, :])
        link(ins)
        v.tensor_tensor(d21[:, :], mx[:, :, 1], mx[:, :, 0], ALU.subtract)
        v.tensor_scalar(nmx[:, :], mx[:, :, 0], -1.0, None, ALU.mult).then_inc(shifted, 1)
        for k in range(2):
            link(v.tensor_copy(idx[:, k, :], ix[:, :, k]))
        for k in range(2):
            v.tensor_tensor(m[k][:, :, :], w["iota"][:, 0:E].unsqueeze(1).broadcast_to([P, NT, E]),
                            bcast(idx[:, k, :], E), ALU.is_equal)
            link(v.memset(acc[k][:, 0, :], 0.0))
        for i in range(steps):
            for k in range(2):
                ins = v.tensor_tensor(acc[k][:, i + 1, :], acc[k][:, i, :],
                                      m[k][:, i * groups:(i + 1) * groups, :].rearrange("p a b -> p (a b)"), ALU.add)
            link(ins)
        v.memset(den[:, :], 0.0).then_inc(masks, 1)
        if split:
            for k in range(2):
                link(v.tensor_single_scalar(bits[:, k, :], ix[:, :, k], 2, ALU.logical_shift_right))
                link(v.tensor_copy(hi_e[:, k, :], bits[:, k, :]))
                link(v.tensor_single_scalar(bits[:, k, :], ix[:, :, k], 3, ALU.bitwise_and))
                link(v.tensor_copy(lo_e[:, k, :], bits[:, k, :]))
        dve.wait_ge(exps, NT + 1)
        link(v.reciprocal(g[:, 0, :], S[:, :]))
        link(v.tensor_tensor(g[:, 1, :], d21[:, :], g[:, 0, :], ALU.mult))
        for k in range(2):
            for c in range(NCH):
                n = k * NCH + c
                dve.wait_ge(counted, n + 1)
                t = slice(c * TC, (c + 1) * TC)
                v.tensor_tensor(ex[:, t, :], p_n[:, n % 2, 0:TC * E].rearrange("p (a b) -> p a b", b=E),
                                m[k][:, t, :], ALU.mult).then_inc(count_used, 1)
            dve.wait_ge(count_used, (k + 1) * NCH)
            link(v.tensor_reduce(loc[:, k, :], ex[:, :, :], AX_X, ALU.add))
        link(v.tensor_scalar(valid[:, :, :], loc[:, :, :], float(C), None, ALU.is_lt))
        if split:
            link(v.scalar_tensor_tensor(out=lo[:, :, :], in0=lo_e[:, :, :], scalar=float(C), in1=loc[:, :, :],
                                        op0=ALU.mult, op1=ALU.add))
            link(v.tensor_tensor(lo[:, :, :], lo[:, :, :], valid[:, :, :], ALU.mult))
            link(v.tensor_scalar(rows[:, :, :], valid[:, :, :], -1000.0, 1000.0, ALU.mult, ALU.add))
            link(v.tensor_tensor(lo[:, :, :], lo[:, :, :], rows[:, :, :], ALU.add))
        for k in range(2):
            link(v.tensor_tensor(A[k][:, :, :], w["iota"][:, 0:LO].unsqueeze(1).broadcast_to([P, NT, LO]),
                                 bcast(low[:, k, :], LO), ALU.is_equal))
            if split:
                link(v.tensor_tensor(mh[:, :, :], w["iota"][:, 0:HI].unsqueeze(1).broadcast_to([P, NT, HI]),
                                     bcast(high[:, k, :], HI), ALU.is_equal))
            pick = mh if split else m[k]
            v.tensor_scalar(R[k][:, :, 0, :], pick[:, :, :], w["pcol"], None, ALU.mult)
            link(v.tensor_tensor(R[k][:, :, 1, :], pick[:, :, :], bcast(w["iota"][:, 0:NT], HI), ALU.mult))
        v.memset(S[:, :], 0.0).then_inc(onehots, 1)
        link(v.scalar_tensor_tensor(out=rows[:, :, :], in0=idx[:, :, :], scalar=float(C), in1=loc[:, :, :],
                                    op0=ALU.mult, op1=ALU.add))
        link(v.tensor_tensor(rows[:, :, :], rows[:, :, :], valid[:, :, :], ALU.mult))
        if groups > 1:
            for k in range(2):
                ins = v.tensor_tensor(rows[:, k, :].rearrange("p (a b) -> p a b", b=groups),
                                      rows[:, k, :].rearrange("p (a b) -> p a b", b=groups),
                                      w["group_base"][:, 0:groups].unsqueeze(1).broadcast_to([P, steps, groups]),
                                      ALU.add)
            link(ins)
        link(v.tensor_copy(r.back[:, :, :], rows[:, :, :]))
        if masked_first:
            link(v.tensor_tensor(g[:, :, :], g[:, :, :], valid[:, :, :], ALU.mult))
        link(v.tensor_tensor(den[:, :], g[:, 0, :], g[:, 1, :], ALU.add))
        link(v.tensor_scalar(den[:, :], den[:, :], floor, None, ALU.max))
        link(v.reciprocal(den[:, :], den[:, :]))
        for k in range(2):
            link(v.tensor_tensor(r.wk[:, k, :], g[:, k, :], den[:, :], ALU.mult))
        if not masked_first:
            link(v.tensor_tensor(r.wk[:, :, :], r.wk[:, :, :], valid[:, :, :], ALU.mult))
        dve.wait_ge(table, 1)
        pt = p_t[:, 0:groups * 2 * HI].rearrange("p (h a c) -> p h a c", h=groups, a=2)
        link(v.tensor_scalar(tabf[:, :, :], pt[:, :, 0, :], float(NT), None, ALU.mult))
        link(v.tensor_tensor(tabf[:, :, :], tabf[:, :, :], pt[:, :, 1, :], ALU.add))
        link(v.tensor_copy(r.tab[:, :, :], tabf[:, :, :]))
        if r.GT is not None:
            link(v.tensor_tensor(ex[:, :, :], m[0][:, :, :], bcast(r.wk[:, 0, :], E), ALU.mult))
            link(v.tensor_tensor(lg[:, :, :], m[1][:, :, :], bcast(r.wk[:, 1, :], E), ALU.mult))
            v.tensor_tensor(ex[:, :, :], ex[:, :, :], lg[:, :, :], ALU.add).then_inc(g_ready, 1)
        yield

    return Programs(tensor, scalar, vector)


def run_alone(nc, ctx, programs):
    block = ctx.enter_context(nc.Block())

    @block.tensor
    def _(pe):
        for _ in programs.tensor(pe):
            pass

    @block.scalar
    def _(act):
        for _ in programs.scalar(act):
            pass

    @block.vector
    def _(dve):
        for _ in programs.vector(dve):
            pass


class Moe0Experts:

    TILES = 2
    UNITS = NT // TILES
    AHEAD = 2

    WORDS = 10752

    def __init__(self, nc, ctx, w, r, arena, xn_dram, W1, y1_dram, r_dram, W2, y2_dram):
        self.nc, self.w, self.r = nc, w, r
        self.xn_rows = xn_dram.rearrange("p t d -> (p t) d")
        self.y1_dram, self.y1_rows = y1_dram, y1_dram.rearrange("h e c n -> (h e c) n")
        self.r_dram, self.r_rows = r_dram, r_dram.rearrange("p t n -> (p t) n")
        self.y2_dram, self.W1, self.W2 = y2_dram, W1, W2
        s = Scope(nc, ctx, "e")

        weights = Arena(arena[:, 0:3 * HID])
        self.w1 = weights.sb("w1", [P, 3, HID])
        self.w2 = self.w1.rearrange("p r (f d) -> p r f d", f=FC)
        first, middle, second = (Arena(arena[:, 3 * HID:]) for _ in range(3))
        self.xg = first.sb("xg", [C0, 4, HG, D])
        self.xgT = first.sb("xgT", [P, 2, HG * C0])
        self.out1 = first.sb("out1", [C0, 2, HG, HID])
        self.yk = middle.sb("yk", [P, 4, 2, HID])
        self.hb = middle.sb("hb", [P, 4, HID])
        self.ro = middle.sb("ro", [P, 6, HID])
        self.rg = second.sb("rg", [C0, 3, HG, HID])
        self.rT = second.sb("rT", [P, 3, FC * C0])
        self.out2 = second.sb("out2", [C0, 2, HG, D])
        self.stats = s.sb("stats", [P, NT, 6])
        self.mv = s.sb("mv", [P, NT, 2])
        self.rstd = s.sb("rstd", [P, NT])
        self.nm = s.sb("nm", [P, NT])
        self.diag = s.sb("diag", [P, 2, 2, P])
        self.bank = s.ps("bank", [P, 2, 512])
        self.diag_ready = s.sem("diag_ready")
        self.chain = s.sem("chain")
        self.piece_made = s.sem("piece_made")
        self.piece_read = s.sem("piece_read")
        self.biased = s.sem("biased")
        self.combined = s.sem("combined")
        self.var_ready = s.sem("var_ready")
        self.root_ready = s.sem("root_ready")
        self.scale_ready = s.sem("scale_ready")
        self.centred = s.sem("centred")
        self.p_chain = s.sem("p_chain")
        self.weighted = s.sem("weighted")
        self.r_ready = s.sem("r_ready")
        self.turned2 = s.sem("turned2")
        self.rT_ready = s.sem("rT_ready")
        self.product2 = s.sem("product2")
        self.out2_ready = s.sem("out2_ready")
        self.w1_in = [s.sem(f"w1_in{i}") for i in range(3)]
        self.gathered1 = [s.sem(f"gathered1{i}") for i in range(4)]
        self.stored1 = [s.sem(f"stored1{i}") for i in range(2)]
        self.gathered_y = [s.sem(f"gathered_y{i}") for i in range(4)]
        self.stored_r = [s.sem(f"stored_r{i}") for i in range(3)]
        self.w2_in = [s.sem(f"w2_in{i}") for i in range(3)]
        self.gathered2 = [s.sem(f"gathered2{i}") for i in range(3)]
        self.stored2 = [s.sem(f"stored2{i}") for i in range(2)]

    def pool_busy(self, i):
        return E0 < i <= E0 + self.UNITS + 4

    def sync(self, sp):
        for e in range(E0 + 1):
            if e < E0:
                if e >= 3:
                    sp.wait_ge(self.piece_made, 5 * (e - 2))
                sp.dma_start(self.w1[:, e % 3, :], self.W1[e]).then_inc(self.w1_in[e % 3], 16)
            if e:
                f = e - 1
                sp.wait_ge(self.piece_read, 5 * (f + 1))
                sp.dma_start(self.y1_dram[:, f, :, :].rearrange("h c n -> c h n"),
                             self.out1[:, f % 2, :, :]).then_inc(self.stored1[f % 2], 16)
        sp.wait_ge(self.piece_made, 5 * E0)

        def load_w2(e):
            sp.dma_start(self.w2[:, e % 3, :, :],
                         self.W2[e].rearrange("(f p) d -> p f d", p=P)).then_inc(self.w2_in[e % 3], 16)

        for e in range(3):
            load_w2(e)
        for u in range(self.UNITS):
            t = u * self.TILES
            sp.wait_ge(self.r_ready, u + 1)
            sp.dma_start(self.r_dram[:, t:t + 2, :], self.ro[:, t % 6:t % 6 + 2, :]).then_inc(
                self.stored_r[(t // 2) % 3], 16)
        for e in range(E0):
            if 1 <= e and e + 2 < E0:
                sp.wait_ge(self.product2, HG * e)
                load_w2(e + 2)
            sp.wait_ge(self.out2_ready, e + 1)
            sp.dma_start(self.y2_dram[:, e, :, :].rearrange("h c n -> c h n"),
                         self.out2[:, e % 2, :, :]).then_inc(self.stored2[e % 2], 16)
        for i in range(2):
            sp.wait_ge(self.stored2[i], 16 * (E0 // 2))

    def pool(self, pool):
        nc, r = self.nc, self.r

        def gather_x(e):
            if e >= E0:
                return
            if e >= 4:
                pool.wait_ge(self.piece_made, 5 * (e - 4) + 1)
            for h in range(HG):
                nc.gpsimd.indirect_dma_start(
                    out=self.xg[:, e % 4, h, :], out_offset=None, in_=self.xn_rows,
                    in_offset=bass.IndirectOffsetOnAxis(ap=r.tab[:, h, e:e + 1], axis=0),
                ).then_inc(self.gathered1[e % 4], 16)

        def gather_y(u):
            for t in range(2 * u, min(2 * u + 2, NT)):
                if t >= 4:
                    pool.wait_ge(self.biased, t - 3)
                for k in range(2):
                    nc.gpsimd.indirect_dma_start(
                        out=self.yk[:, t % 4, k, :], out_offset=None, in_=self.y1_rows,
                        in_offset=bass.IndirectOffsetOnAxis(ap=r.back[:, k, t:t + 1], axis=0),
                    ).then_inc(self.gathered_y[t % 4], 16)

        def weigh(u):
            pool.wait_ge(self.centred, 2 * u + 2)
            t = 2 * u
            ro = self.ro[:, t % 6:t % 6 + 2, :]
            g = slice(t % HG, t % HG + 2)
            nc.gpsimd.tensor_tensor(ro, ro, self.w["ln_w"][:, g, :], ALU.mult).then_inc(self.p_chain, 1)
            pool.wait_ge(self.p_chain, u + 1)
            nc.gpsimd.tensor_tensor(ro, ro, self.w["ln_b"][:, g, :], ALU.add).then_inc(self.weighted, 1)

        def gather_r(e):
            if e >= E0:
                return
            if e >= 3:
                pool.wait_ge(self.turned2, HG * (e - 2))
            for h in range(HG):
                nc.gpsimd.indirect_dma_start(
                    out=self.rg[:, e % 3, h, :], out_offset=None, in_=self.r_rows,
                    in_offset=bass.IndirectOffsetOnAxis(ap=r.tab[:, h, e:e + 1], axis=0),
                ).then_inc(self.gathered2[e % 3], 16)

        for e in range(self.AHEAD):
            gather_x(e)
        for e in range(E0):
            gather_x(e + self.AHEAD)
            yield
        for i in range(2):
            pool.wait_ge(self.stored1[i], 16 * (E0 // 2))
        gather_y(0)
        yield
        for u in range(self.UNITS + 4):
            gather_y(u + 1)
            if 3 <= u < self.UNITS + 3:
                weigh(u - 3)
            yield
        for i in range(3):
            pool.wait_ge(self.stored_r[i], 16 * len(range(i, self.UNITS, 3)))
        for e in range(self.AHEAD):
            gather_r(e)
        yield
        for e in range(E0):
            gather_r(e + self.AHEAD)
            yield

    def tensor(self, pe):
        nc, w, bank = self.nc, self.w, self.bank

        def turn(e):
            k = 5 * e
            if e:
                pe.wait_ge(self.piece_read, k - 1)
            pe.wait_ge(self.gathered1[e % 4], 16 * HG * (e // 4 + 1))
            for g in range(HG):
                ins = nc.tensor.transpose(bank[:, k % 2, g * C0:(g + 1) * C0], self.xg[:, e % 4, g, :],
                                          w["ident"][0:C0, 0:C0])
            ins.then_inc(self.piece_made, 1)

        turn(0)
        for e in range(E0):
            for h in range(HG):
                k = 5 * e + 1 + h
                if h == 0:
                    pe.wait_ge(self.piece_read, 5 * e + 1)
                    pe.wait_ge(self.w1_in[e % 3], 16 * (e // 3 + 1))
                elif k >= 2:
                    pe.wait_ge(self.piece_read, k - 1)
                nc.tensor.matmul(bank[0:C0, k % 2, :], self.xgT[:, e % 2, h * C0:(h + 1) * C0],
                                 self.w1[:, e % 3, :], start=True, stop=True).then_inc(self.piece_made, 1)
                if h == 3 and e + 1 < E0:
                    turn(e + 1)
                yield
        yield from [None] * PE_SLOTS
        for u in range(self.UNITS + 4):
            for slot in range(PE_SLOTS):
                t = 2 * u + slot
                if slot < 2 and t < NT:
                    if t < 2:
                        pe.wait_ge(self.piece_read, 5 * E0 - 1 + t)
                    else:
                        pe.wait_ge(self.combined, t - 1)
                    nc.tensor.matmul(bank[:, t % 2, :], gate_rows(self.r.GT, t), expert_biases(w["b1_experts"], t),
                                     start=True, stop=False)
                    pe.wait_ge(self.gathered_y[t % 4], 32 * (t // 4 + 1))
                    pe.wait_ge(self.diag_ready, t + 1)
                    for k in range(2):
                        ins = nc.tensor.matmul(bank[:, t % 2, :], self.diag[:, t % 2, k, :], self.yk[:, t % 4, k, :],
                                               start=False, stop=(k == 1))
                    ins.then_inc(self.biased, 1)
                yield
        yield from [None] * PE_SLOTS

        def product(n):
            e, h = divmod(n, HG)
            pe.wait_ge(self.rT_ready, n + 1)
            if h == 0:
                pe.wait_ge(self.w2_in[e % 3], 16 * (e // 3 + 1))
                if e:
                    pe.wait_ge(self.out2_ready, e)
            for f in range(FC):
                ins = nc.tensor.matmul(bank[0:C0, 1, h * D:(h + 1) * D], self.rT[:, n % 3, f * C0:(f + 1) * C0],
                                       self.w2[:, e % 3, f, :], start=(f == 0), stop=(f == FC - 1))
            ins.then_inc(self.product2, 1)

        for n in range(E0 * HG):
            e, h = divmod(n, HG)
            if h == 0:
                pe.wait_ge(self.gathered2[e % 3], 16 * HG * (e // 3 + 1))
            if n:
                pe.wait_ge(self.rT_ready, n)
            else:
                pe.wait_ge(self.combined, NT)
            for f in range(FC):
                ins = nc.tensor.transpose(bank[:, 0, f * C0:(f + 1) * C0], self.rg[:, e % 3, h, f * P:(f + 1) * P],
                                          w["ident"][0:C0, 0:C0])
            ins.then_inc(self.turned2, 1)
            if n:
                product(n - 1)
            yield
        product(E0 * HG - 1)

    def scalar(self, act):
        nc, bank, ro = self.nc, self.bank, self.ro

        def copy_turned(e):
            act.wait_ge(self.piece_made, 5 * e + 1)
            nc.scalar.activation(self.xgT[:, e % 2, :], bank[:, 5 * e % 2, 0:HG * C0], ACT.Copy).then_inc(
                self.piece_read, 1)

        copy_turned(0)
        for e in range(E0):
            if e >= 2:
                act.wait_ge(self.stored1[e % 2], 16 * (e // 2))
            for h in range(HG):
                k = 5 * e + 1 + h
                act.wait_ge(self.piece_made, k + 1)
                nc.scalar.activation(self.out1[:, e % 2, h, :], bank[0:C0, k % 2, :], ACT.Copy).then_inc(
                    self.piece_read, 1)
                if h == 1:
                    yield
            if e + 1 < E0:
                copy_turned(e + 1)
            yield

        def diagonals(t):
            if t < NT:
                if t >= 2:
                    act.wait_ge(self.biased, t - 1)
                for k in range(2):
                    ins = nc.scalar.activation(self.diag[:, t % 2, k, :], self.w["ident"], ACT.Copy,
                                               scale=self.r.wk[:, k, t:t + 1])
                ins.then_inc(self.diag_ready, 1)

        diagonals(0)
        diagonals(1)
        yield from [None] * ACT_SLOTS
        for u in range(self.UNITS + 4):
            if 4 <= u:
                n = u - 4
                act.wait_ge(self.weighted, n + 1)
                rows = ro[:, 2 * n % 6:2 * n % 6 + 2, :]
                nc.scalar.activation(rows, rows, ACT.Relu).then_inc(self.r_ready, 1)
            if 2 <= u < self.UNITS + 2:
                n = u - 2
                act.wait_ge(self.scale_ready, n + 1)
                if n >= 3:
                    act.wait_ge(self.stored_r[n % 3], 16 * (n // 3))
                for t in range(2 * n, 2 * n + 2):
                    nc.scalar.activation(ro[:, t % 6, :], self.hb[:, t % 4, :], ACT.Identity,
                                         scale=self.rstd[:, t:t + 1], bias=self.nm[:, t:t + 1]).then_inc(
                                             self.centred, 1)
            yield
            if 1 <= u <= self.UNITS:
                act.wait_ge(self.var_ready, 2 * u)
                t = slice(2 * u - 2, 2 * u)
                nc.scalar.activation(self.rstd[:, t], self.nm[:, t], ACT.Sqrt).then_inc(self.root_ready, 1)
            if u < self.UNITS:
                for t in range(2 * u, 2 * u + 2):
                    act.wait_ge(self.biased, t + 1)
                    if t >= 4:
                        act.wait_ge(self.centred, t - 3)
                        act.wait_ge(self.var_ready, t - 3)
                    nc.scalar.activation(self.hb[:, t % 4, :], bank[:, t % 2, :], ACT.Copy).then_inc(
                        self.combined, 1)
                    diagonals(t + 2)
            yield
        yield from [None] * ACT_SLOTS

        def copy_out(e):
            act.wait_ge(self.product2, HG * (e + 1))
            if e >= 2:
                act.wait_ge(self.stored2[e % 2], 16 * (e // 2))
            nc.scalar.activation(self.out2[:, e % 2, :, :].rearrange("p a b -> p (a b)"), bank[0:C0, 1, :],
                                 ACT.Copy).then_inc(self.out2_ready, 1)

        for e in range(E0):
            for h in range(HG):
                n = HG * e + h
                act.wait_ge(self.turned2, n + 1)
                if n >= 3:
                    act.wait_ge(self.product2, n - 2)
                nc.scalar.activation(self.rT[:, n % 3, :], bank[:, 0, 0:FC * C0], ACT.Copy).then_inc(self.rT_ready, 1)
                if h == 0 and e:
                    copy_out(e - 1)
                if h % 2:
                    yield
        copy_out(E0 - 1)

    def vector(self, dve):
        nc, r, v = self.nc, self.r, self.nc.vector
        link = Chain(dve, self.chain)
        yield from [None] * (DVE_SLOTS * (E0 + 1))
        for u in range(self.UNITS + 4):
            if 1 <= u <= self.UNITS:
                for t in range(2 * u - 2, 2 * u):
                    dve.wait_ge(self.combined, t + 1)
                    link(v.bn_stats(self.stats[:, t, :], self.hb[:, t % 4, :]))
                    link(v.bn_aggr(self.mv[:, t, :], self.stats[:, t, :]))
                    v.tensor_scalar(self.nm[:, t:t + 1], self.mv[:, t, 1:2], 1e-6, None, ALU.add).then_inc(
                        self.var_ready, 1)
            yield
            if 1 <= u <= self.UNITS:
                dve.wait_ge(self.root_ready, u)
                t = slice(2 * u - 2, 2 * u)
                link(v.reciprocal(self.rstd[:, t], self.rstd[:, t]))
                v.scalar_tensor_tensor(out=self.nm[:, t], in0=self.mv[:, t, 0], scalar=-1.0, in1=self.rstd[:, t],
                                       op0=ALU.mult, op1=ALU.mult).then_inc(self.scale_ready, 1)
            yield


class Moe0Output:

    HALF_TILES = NT // 2

    def __init__(self, nc, ctx, w, r, y2_dram, xn_dram, xn_rows, s_rows, x_dram, x_rows, weights):
        self.nc, self.w, self.r = nc, w, r
        self.y2_rows = y2_dram.rearrange("h e c n -> (h e c) n")
        self.xn_rows, self.s_rows, self.x_dram, self.x_rows = xn_rows, s_rows, x_dram, x_rows
        self.xn_dram, self.weights = xn_dram, weights
        s = Scope(nc, ctx, "e4")
        self.yk = s.sb("yk", [P, 4, 2, D])
        self.o = s.sb("o", [P, NT, D])
        self.stats = s.sb("stats", [P, NT, 6])
        self.mv = s.sb("mv", [P, NT, 2])
        self.rstd = s.sb("rstd", [P, NT])
        self.nm = s.sb("nm", [P, NT])
        self.bank = s.ps("bank", [P, TB * D])
        self.gathered = [s.sem(f"gathered{i}") for i in range(4)]
        self.chain = s.sem("chain")
        self.p_chain = s.sem("p_chain")
        self.x_in = s.sem("x_in")
        self.weights_in = s.sem("weights_in")
        self.xn_in = [s.sem(f"xn_in{i}") for i in range(B)]
        self.biased = s.sem("biased")
        self.combined = s.sem("combined")
        self.var_ready = s.sem("var_ready")
        self.root_ready = s.sem("root_ready")
        self.scale_ready = s.sem("scale_ready")
        self.centred = s.sem("centred")
        self.weighted = s.sem("weighted")
        self.g_ready = s.sem("g_ready")
        self.s_ready = None

    def sync(self, sp):
        for dst, src in self.weights:
            sp.dma_start(dst, src).then_inc(self.weights_in, 16)
        for b in range(B):
            t = slice(b * TB, (b + 1) * TB)
            sp.dma_start(self.xn_rows[:, t, :], self.xn_dram[:, t, :]).then_inc(self.xn_in[b], 16)
        sp.dma_start(self.x_rows[:, :, :], self.x_dram).then_inc(self.x_in, 16)
        sp.wait_ge(self.x_in, 16)

    def pool(self, pool):
        nc, r, w = self.nc, self.r, self.w

        def gather(u):
            for t in range(2 * u, min(2 * u + 2, NT)):
                if t >= 4:
                    pool.wait_ge(self.combined, t - 3)
                for k in range(2):
                    nc.gpsimd.indirect_dma_start(
                        out=self.yk[:, t % 4, k, :], out_offset=None, in_=self.y2_rows,
                        in_offset=bass.IndirectOffsetOnAxis(ap=r.back[:, k, t:t + 1], axis=0),
                    ).then_inc(self.gathered[t % 4], 16)

        gather(0)
        pool.wait_ge(self.weights_in, 16 * len(self.weights))
        for u in range(2 * B + 1):
            gather(u + 1)
            if u >= B + 2:
                n = u - B - 2
                if n % 2 == 0 and n // 2 < 3:
                    self.weigh_on_pool(pool, n // 2)
            yield
        self.weigh_on_pool(pool, 3)

    def weigh_on_pool(self, pool, q):
        nc, w = self.nc, self.w
        o = self.o[:, 4 * q:4 * q + 4, :]
        pool.wait_ge(self.centred, 4 * q + 4)
        nc.gpsimd.tensor_tensor(o, o, w["ln_out_w"][:, :].unsqueeze(1).broadcast_to([P, 4, D]),
                                ALU.mult).then_inc(self.p_chain, 1)
        pool.wait_ge(self.p_chain, q + 1)
        nc.gpsimd.tensor_tensor(o, o, w["ln_out_b"][:, :].unsqueeze(1).broadcast_to([P, 4, D]),
                                ALU.add).then_inc(self.weighted, 1)

    def tensor(self, pe):
        for b in range(B):
            if b:
                pe.wait_ge(self.combined, TB * b)
            for j in range(TB):
                t = b * TB + j
                ins = self.nc.tensor.matmul(self.bank[:, j * D:(j + 1) * D], gate_rows(self.r.GT, t),
                                            expert_biases(self.w["b2_experts"], t), start=True, stop=True)
            ins.then_inc(self.biased, 1)
            yield
            yield

    def scalar(self, act):
        nc = self.nc

        def roots(h):
            t = slice(h * self.HALF_TILES, (h + 1) * self.HALF_TILES)
            act.wait_ge(self.var_ready, h + 1)
            nc.scalar.activation(self.rstd[:, t], self.nm[:, t], ACT.Sqrt).then_inc(self.root_ready, 1)

        def centre(t):
            nc.scalar.activation(self.o[:, t, :], self.o[:, t, :], ACT.Identity, scale=self.rstd[:, t:t + 1],
                                 bias=self.nm[:, t:t + 1]).then_inc(self.centred, 1)

        yield from [None] * B
        roots(0)
        yield
        for u in range(B):
            act.wait_ge(self.scale_ready, 1)
            centre(2 * u)
            centre(2 * u + 1)
            yield
        roots(1)
        act.wait_ge(self.scale_ready, 2)
        for t in range(self.HALF_TILES, NT):
            centre(t)
        for c in range(4):
            act.wait_ge(self.weighted, 4 + max(c - 1, 0))
            rows = self.o[:, 8 * c:8 * c + 8, :]
            nc.scalar.activation(rows, rows, ACT.Silu).then_inc(self.g_ready, 1)

    def vector(self, dve):
        r, v, w = self.r, self.nc.vector, self.w
        link = Chain(dve, self.chain)

        def scales(h):
            t = slice(h * self.HALF_TILES, (h + 1) * self.HALF_TILES)
            dve.wait_ge(self.root_ready, h + 1)
            link(v.reciprocal(self.rstd[:, t], self.rstd[:, t]))
            v.scalar_tensor_tensor(out=self.nm[:, t], in0=self.mv[:, t, 0], scalar=-1.0, in1=self.rstd[:, t],
                                   op0=ALU.mult, op1=ALU.mult).then_inc(self.scale_ready, 1)

        for u in range(2 * B):
            for t in range(2 * u, 2 * u + 2):
                b, j = divmod(t, TB)
                dve.wait_ge(self.gathered[t % 4], 32 * (t // 4 + 1))
                dve.wait_ge(self.biased, b + 1)
                link(v.scalar_tensor_tensor(out=self.o[:, t, :], in0=self.yk[:, t % 4, 0, :],
                                            scalar=r.wk[:, 0, t:t + 1], in1=self.bank[:, j * D:(j + 1) * D],
                                            op0=ALU.mult, op1=ALU.add))
                v.scalar_tensor_tensor(out=self.o[:, t, :], in0=self.yk[:, t % 4, 1, :], scalar=r.wk[:, 1, t:t + 1],
                                       in1=self.o[:, t, :], op0=ALU.mult, op1=ALU.add).then_inc(self.combined, 1)
            pair = slice(2 * u, 2 * u + 2)
            dve.wait_ge(self.combined, 2 * u + 2)
            link(v.tensor_tensor(self.o[:, pair, :], self.o[:, pair, :], self.xn_rows[:, pair, :], ALU.add))
            for t in range(2 * u, 2 * u + 2):
                ins = v.bn_stats(self.stats[:, t, :], self.o[:, t, :])
            link(ins)
            for t in range(2 * u, 2 * u + 2):
                ins = v.bn_aggr(self.mv[:, t, :], self.stats[:, t, :])
            link(ins)
            ins = v.tensor_scalar(self.nm[:, pair], self.mv[:, pair, 1], 1e-6, None, ALU.add)
            if u % B == B - 1:
                ins.then_inc(self.var_ready, 1)
            else:
                link(ins)
            if u == B:
                scales(0)
            yield
        yield
        scales(1)
        for c in (2, 3):
            o = self.o[:, 8 * c:8 * c + 8, :]
            dve.wait_ge(self.centred, 8 * c + 8)
            link(v.tensor_tensor(o, o, w["ln_out_w"][:, :].unsqueeze(1).broadcast_to([P, 8, D]), ALU.mult))
            dve.wait_ge(self.weighted, 4 + c - 2)
            v.tensor_tensor(o, o, w["ln_out_b"][:, :].unsqueeze(1).broadcast_to([P, 8, D]),
                            ALU.add).then_inc(self.weighted, 1)
        dve.wait_ge(self.x_in, 16)
        for c in range(4):
            t = slice(c * 8, (c + 1) * 8)
            dve.wait_ge(self.g_ready, c + 1)
            dve.wait_ge(self.s_ready, c + 1)
            link(v.tensor_tensor(self.o[:, t, :], self.o[:, t, :], self.s_rows[:, t, :], ALU.mult))
            link(v.tensor_tensor(self.x_rows[:, t, :], self.x_rows[:, t, :], self.o[:, t, :], ALU.add))


NH = 8
SCALE = float(D) ** -0.5
SIM_AT = [(1, 384), (2, 0), (1, 0), (0, 0)]
PT_AT = [(0, 0), (1, 0), (2, 0), (1, 384)]
PT_BANK = (0, 1, 0)


def attention_fold_stage(nc, w, xn_rows, xaT, M, N):
    with ExitStack() as ctx:
        s = Scope(nc, ctx, "af")
        sq = s.sb("sq", [P, 8, D])
        l2 = s.sb("l2", [P, NT])
        xa = s.sb("xa", [P, NT, D])
        qkv = s.sb("qkv", [P, 3 * NH, D])
        wo = s.sb("wo", [P, NH, D])
        p_w = s.ps("p_w", [P, 4, 512])
        p_x = s.ps("p_x", [P, 4, 512])
        w_in = s.sem("w_in")
        chain = s.sem("chain")
        summed = s.sem("summed")
        root_ready = s.sem("root_ready")
        xa_ready = s.sem("xa_ready")
        folded = s.sem("folded")
        fold_copied = s.sem("fold_copied")
        turned = s.sem("turned")
        xaT_ready = s.sem("xaT_ready")
        block = ctx.enter_context(nc.Block())

        @block.sync
        def _(sp):
            sp.dma_start(qkv[:, :, :], w["qkv_dram"]).then_inc(w_in, 16)
            sp.dma_start(wo[:, :, :], w["wo_dram"]).then_inc(w_in, 16)
            sp.wait_ge(w_in, 32)

        @block.tensor
        def _(pe):
            pe.wait_ge(w_in, 32)
            for n in range(4):
                for j in range(4):
                    h = (n % 2) * 4 + j
                    if n < 2:
                        ins = nc.tensor.matmul(p_w[:, n, j * D:(j + 1) * D], qkv[:, h, :], qkv[:, NH + h, :],
                                               start=True, stop=True)
                    else:
                        ins = nc.tensor.matmul(p_w[:, n, j * D:(j + 1) * D], qkv[:, 2 * NH + h, :], wo[:, h, :],
                                               start=True, stop=True)
                ins.then_inc(folded, 1)
            for b in range(B):
                pe.wait_ge(xa_ready, b // 2 + 1)
                if b >= 4:
                    pe.wait_ge(xaT_ready, b - 3)
                for j in range(TB):
                    ins = nc.tensor.transpose(p_x[:, b % 4, j * P:(j + 1) * P], xa[:, b * TB + j, :], w["ident"])
                ins.then_inc(turned, 1)

        @block.scalar
        def _(act):
            act.wait_ge(summed, 1)
            nc.scalar.activation(l2[:, :], l2[:, :], ACT.Sqrt).then_inc(root_ready, 1)
            for n in range(4):
                act.wait_ge(folded, n + 1)
                dst = (M if n < 2 else N)[:, (n % 2) * 512:(n % 2 + 1) * 512]
                nc.scalar.activation(dst, p_w[:, n, :], ACT.Copy, scale=SCALE if n < 2 else 1.0).then_inc(fold_copied, 1)
            for b in range(B):
                act.wait_ge(turned, b + 1)
                nc.scalar.activation(xaT[:, b, :], p_x[:, b % 4, :], ACT.Copy, scale=w["gamma"]).then_inc(xaT_ready, 1)

        @block.vector
        def _(dve):
            link = Chain(dve, chain)
            v = nc.vector
            for c in range(4):
                t = slice(c * 8, (c + 1) * 8)
                link(v.tensor_tensor(sq[:, :, :], xn_rows[:, t, :], xn_rows[:, t, :], ALU.mult))
                link(v.tensor_reduce(l2[:, t], sq[:, :, :], AX_X, ALU.add))
            v.memset(sq[:, 0, 0:1], 0.0).then_inc(summed, 1)
            dve.wait_ge(root_ready, 1)
            link(v.tensor_scalar(l2[:, :], l2[:, :], 1e-12, None, ALU.max))
            link(v.reciprocal(l2[:, :], l2[:, :]))
            link(v.tensor_scalar(l2[:, :], l2[:, :], float(D) ** 0.5, None, ALU.mult))
            for c in range(4):
                t = slice(c * 8, (c + 1) * 8)
                v.tensor_tensor(xa[:, t, :], xn_rows[:, t, :], bcast(l2[:, t], D), ALU.mult).then_inc(xa_ready, 1)


def attention_stage(nc, w, xaT, M, N, s_rows, beside):
    NI = B * NH
    BANKS = [(3,), (2, 0), (1,)]
    with ExitStack() as ctx:
        s = Scope(nc, ctx, "at")
        qT = s.sb("qT", [P, 3, L])
        V = s.sb("V", [P, 2, TB, NH * D])
        pr = s.sb("pr", [P, 2, 3, 512])
        pT = s.sb("pT", [P, 2, 3, 512])
        mx = s.sb("mx", [P, 2, 4])
        nmx = s.sb("nmx", [P, 2, 4])
        sums = s.sb("sums", [P, 3, 4])
        p_s = s.ps("p_s", [P, 3, 512])
        p_t = s.ps("p_t", [P, 2, 512])
        p_o = s.ps("p_o", [P, 4, D])
        p_q = s.ps("p_q", [P, 512])
        chain = s.sem("chain")
        q_product = s.sem("q_product")
        q_copied = s.sem("q_copied")
        v_product = s.sem("v_product")
        v_copied = s.sem("v_copied")
        scores = s.sem("scores")
        maxed = s.sem("maxed")
        exped = s.sem("exped")
        turned = s.sem("turned")
        pT_ready = s.sem("pT_ready")
        out_ready = s.sem("out_ready")
        out_used = s.sem("out_used")
        beside.s_rows_added = out_used
        block = ctx.enter_context(nc.Block())


        def tensor_steps(pe):
            def query(n):
                b, h = divmod(n, NH)
                pe.wait_ge(v_copied, min(NH * B, NH + max(n - 2, 0)))
                if n:
                    pe.wait_ge(q_copied, n)
                nc.tensor.matmul(p_q[:, :], M[:, h * D:(h + 1) * D], xaT[:, b, :], start=True,
                                 stop=True).then_inc(q_product, 1)

            def value(k):
                b, i = divmod(k, NH)
                t, half = divmod(i, 2)
                if k:
                    pe.wait_ge(v_copied, k)
                if k >= NH:
                    pe.wait_ge(q_copied, min(NI, k - NH + 3))
                nc.tensor.matmul(p_q[:, :], xaT[:, b, t * P:(t + 1) * P], N[:, half * 512:(half + 1) * 512],
                                 start=True, stop=True).then_inc(v_product, 1)

            def score(n):
                b, h = divmod(n, NH)
                pe.wait_ge(q_copied, n + 1)
                for k, tiles in enumerate(BANKS):
                    if n:
                        pe.wait_ge(exped, 3 * (n - 1) + k + 1)
                    for i in tiles:
                        bank, c = SIM_AT[i]
                        K = (i + 1) * P
                        nc.tensor.matmul(p_s[:, bank, c:c + K], qT[:, n % 3, i * P:(i + 1) * P], xaT[:, b, 0:K],
                                         start=True, stop=False)
                        ins = nc.tensor.matmul(p_s[:, bank, c + i * P:c + K], w["ident_bf"], w["mask_bf"],
                                               start=False, stop=True)
                    ins.then_inc(scores, 1)

            def turn(n):
                pe.wait_ge(exped, 3 * (n + 1))
                for part, keys in enumerate(((0,), (1, 3), (2,))):
                    bank = PT_BANK[part]
                    if part == 2:
                        if n + 2 < NI:
                            query(n + 2)
                        pe.wait_ge(pT_ready, 3 * n + 1)
                    elif n:
                        pe.wait_ge(pT_ready, 3 * n - part)
                    for j in keys:
                        c = PT_AT[j][1]
                        for i in range(j, TB):
                            sbank, sc = SIM_AT[i]
                            ins = nc.tensor.transpose(p_t[:, bank, c + (i - j) * P:c + (i - j + 1) * P],
                                                      pr[:, n % 2, sbank, sc + j * P:sc + (j + 1) * P], w["ident"])
                    ins.then_inc(turned, 1)

            def weigh(n):
                b, h = divmod(n, NH)
                pe.wait_ge(v_copied, NH * (b + 1))
                if n:
                    pe.wait_ge(out_used, n)
                pe.wait_ge(pT_ready, 3 * (n + 1))
                for i in range(TB):
                    for j in range(i + 1):
                        bank, c = PT_AT[j]
                        ins = nc.tensor.matmul(p_o[:, i, :], pT[:, n % 2, bank, c + (i - j) * P:c + (i - j + 1) * P],
                                               V[:, b % 2, j, h * D:(h + 1) * D], start=(j == 0), stop=(j == i))
                ins.then_inc(out_ready, 1)

            for k in range(NH):
                value(k)
            query(0)
            query(1)
            score(0)
            for n in range(NI):
                turn(n)
                yield
                if n + 1 < NI:
                    score(n + 1)
                yield
                if n + NH < NI:
                    value(n + NH)
                weigh(n)

        def scalar_steps(act):
            def copy_query(n):
                act.wait_ge(q_product, n + 1)
                if n >= 3:
                    act.wait_ge(scores, 3 * (n - 2))
                nc.scalar.activation(qT[:, n % 3, :], p_q[:, :], ACT.Copy).then_inc(q_copied, 1)

            def copy_value(k):
                b, i = divmod(k, NH)
                t, half = divmod(i, 2)
                act.wait_ge(v_product, k + 1)
                if b >= 2:
                    act.wait_ge(out_ready, NH * (b - 1))
                nc.scalar.activation(V[:, b % 2, t, half * 512:(half + 1) * 512], p_q[:, :],
                                     ACT.Copy).then_inc(v_copied, 1)

            def exps(n):
                if n >= 2:
                    act.wait_ge(turned, 3 * (n - 1))
                if n >= 3:
                    act.wait_ge(out_used, n - 2)
                for k, tiles in enumerate(BANKS):
                    act.wait_ge(maxed, 3 * n + k + 1)
                    for i in tiles:
                        bank, c = SIM_AT[i]
                        K = (i + 1) * P
                        ins = nc.scalar.activation(pr[:, n % 2, bank, c:c + K], p_s[:, bank, c:c + K], ACT.Exp,
                                                   bias=nmx[:, n % 2, i:i + 1], accum_out=sums[:, n % 3, i:i + 1])
                    ins.then_inc(exped, 1)

            for k in range(NH):
                copy_value(k)
            copy_query(0)
            copy_query(1)
            for n in range(NI):
                exps(n)
                if n and n - 1 + NH < NI:
                    copy_value(n - 1 + NH)
                yield
                if n + 2 < NI:
                    copy_query(n + 2)
                yield

        def vector_steps(dve):
            link = Chain(dve, chain)
            v = nc.vector

            def maxima(n):
                for k, tiles in enumerate(BANKS):
                    dve.wait_ge(scores, 3 * n + k + 1)
                    for i in tiles:
                        bank, c = SIM_AT[i]
                        link(v.tensor_reduce(mx[:, n % 2, i:i + 1], p_s[:, bank, c:c + (i + 1) * P], AX_X, ALU.max))
                        ins = v.tensor_scalar(nmx[:, n % 2, i:i + 1], mx[:, n % 2, i:i + 1], -1.0, None, ALU.mult)
                    ins.then_inc(maxed, 1)

            def add_head(n):
                b, h = divmod(n, NH)
                link(v.reciprocal(sums[:, n % 3, :], sums[:, n % 3, :]))
                dve.wait_ge(out_ready, n + 1)
                for i in range(TB):
                    o = s_rows[:, b * TB + i, :]
                    if h == 0:
                        ins = v.tensor_scalar(o, p_o[:, i, :], sums[:, n % 3, i:i + 1], None, ALU.mult)
                    else:
                        ins = v.scalar_tensor_tensor(out=o, in0=p_o[:, i, :], scalar=sums[:, n % 3, i:i + 1], in1=o,
                                                     op0=ALU.mult, op1=ALU.add)
                ins.then_inc(out_used, 1)

            maxima(0)
            for n in range(NI):
                for part in range(3):
                    dve.wait_ge(turned, 3 * n + part + 1)
                    cols = 512 if part < 2 else 256
                    v.tensor_copy(pT[:, n % 2, part, 0:cols], p_t[:, PT_BANK[part], 0:cols]).then_inc(pT_ready, 1)
                if n > 1:
                    dve.wait_ge(out_used, n - 1)
                if n:
                    add_head(n - 1)
                if n + 1 < NI:
                    maxima(n + 1)
                yield
            dve.wait_ge(out_used, NI - 1)
            add_head(NI - 1)

        @block.tensor
        def _(pe):
            side_by_side(tensor_steps(pe), beside.tensor(pe))

        @block.scalar
        def _(act):
            side_by_side(scalar_steps(act), beside.scalar(act))

        @block.vector
        def _(dve):
            side_by_side(vector_steps(dve), beside.vector(dve))

        @block.gpsimd
        def _(pool):
            side_by_side((None for _ in range(NI)), beside.pool(pool))

        @block.sync
        def _(sp):
            beside.sync(sp)


class Moe1Experts:

    EG = 4
    NG = E1 // EG
    WG = 4
    AHEAD = 2
    CU = NT // 2
    IDLE = B * NH - (NG + 1 + CU + 2 + B - 1)

    def __init__(self, nc, ctx, w, r, xn_dram, we_dram, y_dram, o, s_rows, x_rows, out_dram, stored):
        self.nc, self.w, self.r = nc, w, r
        self.xn_rows = xn_dram.rearrange("p t d -> (p t) d")
        self.y_dram, self.y_rows = y_dram, y_dram.rearrange("e c f -> (e c) f")
        self.we_dram, self.out_dram, self.outputs_stored = we_dram, out_dram, stored
        self.o, self.s_rows, self.x_rows = o, s_rows, x_rows
        s = Scope(nc, ctx, "f")
        self.we = s.sb("we", [P, 2, self.WG * self.EG, D])
        self.xg = s.sb("xg", [P, 4, D])
        self.xgT = s.sb("xgT", [P, 2, P])
        self.out = s.sb("out", [C1, 4, self.EG, D])
        self.yk = s.sb("yk", [P, 4, 2, D])
        self.bank = s.ps("bank", [P, 512])
        self.chain = s.sem("chain")
        self.turned = s.sem("turned")
        self.xT_ready = s.sem("xT_ready")
        self.product = s.sem("product")
        self.copied = s.sem("copied")
        self.combined = s.sem("combined")
        self.g_ready = s.sem("g_ready")
        self.scaled = s.sem("scaled")
        self.x_ready = s.sem("x_ready")
        self.w_in = [s.sem(f"w_in{i}") for i in range(2)]
        self.gathered = [s.sem(f"gathered{i}") for i in range(4)]
        self.y_stored = [s.sem(f"y_stored{i}") for i in range(4)]
        self.gathered_y = [s.sem(f"gathered_y{i}") for i in range(4)]
        self.s_rows_added = None

    def sync(self, sp):
        n = self.WG * self.EG

        def load(c):
            if c >= 2:
                sp.wait_ge(self.product, self.WG * (c - 1))
            sp.dma_start(self.we[:, c % 2, :, :],
                         self.we_dram[c * n:(c + 1) * n].rearrange("e d f -> d e f")).then_inc(self.w_in[c % 2], 16)

        load(0)
        load(1)
        for g in range(self.NG):
            if g and g % self.WG == 0 and g // self.WG + 1 < self.NG // self.WG:
                load(g // self.WG + 1)
            sp.wait_ge(self.copied, g + 1)
            sp.dma_start(self.y_dram[g * self.EG:(g + 1) * self.EG].rearrange("e c f -> c e f"),
                         self.out[:, g % 4, :, :]).then_inc(self.y_stored[g % 4], 16)
        for b in range(B):
            t = slice(b * TB, (b + 1) * TB)
            sp.wait_ge(self.x_ready, b + 1)
            sp.dma_start(self.out_dram[:, t, :], self.x_rows[:, t, :]).then_inc(self.outputs_stored, 16)
        sp.wait_ge(self.outputs_stored, 16 * B)

    def pool(self, pool):
        nc, r = self.nc, self.r

        def gather_x(g):
            if g >= self.NG:
                return
            if g >= 4:
                pool.wait_ge(self.turned, g - 3)
            nc.gpsimd.indirect_dma_start(
                out=self.xg[:, g % 4, :], out_offset=None, in_=self.xn_rows,
                in_offset=bass.IndirectOffsetOnAxis(ap=r.tab[:, 0, g:g + 1], axis=0),
            ).then_inc(self.gathered[g % 4], 16)

        def gather_y(u):
            for t in range(2 * u, min(2 * u + 2, NT)):
                if t >= 4:
                    pool.wait_ge(self.combined, t - 3)
                for k in range(2):
                    nc.gpsimd.indirect_dma_start(
                        out=self.yk[:, t % 4, k, :], out_offset=None, in_=self.y_rows,
                        in_offset=bass.IndirectOffsetOnAxis(ap=r.back[:, k, t:t + 1], axis=0),
                    ).then_inc(self.gathered_y[t % 4], 16)

        for g in range(self.AHEAD):
            gather_x(g)
        for g in range(self.NG):
            gather_x(g + self.AHEAD)
            yield
        for i in range(4):
            pool.wait_ge(self.y_stored[i], 16 * (self.NG // 4))
        gather_y(0)
        yield
        for u in range(self.CU):
            gather_y(u + 1)
            yield

    def tensor(self, pe):
        nc = self.nc

        def turn(g):
            pe.wait_ge(self.gathered[g % 4], 16 * (g // 4 + 1))
            if g:
                pe.wait_ge(self.copied, g)
            nc.tensor.transpose(self.bank[:, 0:P], self.xg[:, g % 4, :], self.w["ident"]).then_inc(self.turned, 1)

        turn(0)
        for g in range(self.NG):
            c = g // self.WG
            pe.wait_ge(self.xT_ready, g + 1)
            pe.wait_ge(self.w_in[c % 2], 16 * (c // 2 + 1))
            for j in range(self.EG):
                ins = nc.tensor.matmul(self.bank[0:C1, j * D:(j + 1) * D], self.xgT[:, g % 2, j * C1:(j + 1) * C1],
                                       self.we[:, c % 2, (g % self.WG) * self.EG + j, :], start=True, stop=True)
            ins.then_inc(self.product, 1)
            yield
            if g + 1 < self.NG:
                turn(g + 1)
            yield

    def scalar(self, act):
        nc = self.nc

        def copy_turned(g):
            act.wait_ge(self.turned, g + 1)
            if g >= 2:
                act.wait_ge(self.product, g - 1)
            nc.scalar.activation(self.xgT[:, g % 2, :], self.bank[:, 0:P], ACT.Copy).then_inc(self.xT_ready, 1)

        copy_turned(0)
        for g in range(self.NG):
            act.wait_ge(self.product, g + 1)
            if g >= 4:
                act.wait_ge(self.y_stored[g % 4], 16 * (g // 4))
            nc.scalar.activation(self.out[:, g % 4, :, :].rearrange("p a b -> p (a b)"), self.bank[0:C1, :],
                                 ACT.Copy).then_inc(self.copied, 1)
            yield
            if g + 1 < self.NG:
                copy_turned(g + 1)
            yield
        yield from [None] * (2 * (1 + self.CU + 1))
        act.wait_ge(self.combined, NT)
        for h in range(4):
            rows = self.o[:, h * 8:(h + 1) * 8, :]
            nc.scalar.activation(rows, rows, ACT.Silu).then_inc(self.g_ready, 1)

    def vector(self, dve):
        r, v = self.r, self.nc.vector
        link = Chain(dve, self.chain)
        yield from [None] * (self.NG + 1)
        for u in range(self.CU):
            for t in range(2 * u, 2 * u + 2):
                o = self.o[:, t, :]
                dve.wait_ge(self.gathered_y[t % 4], 32 * (t // 4 + 1))
                link(v.tensor_scalar(o, self.yk[:, t % 4, 0, :], r.wk[:, 0, t:t + 1], None, ALU.mult))
                v.scalar_tensor_tensor(out=o, in0=self.yk[:, t % 4, 1, :], scalar=r.wk[:, 1, t:t + 1], in1=o,
                                       op0=ALU.mult, op1=ALU.add).then_inc(self.combined, 1)
            yield
        yield from [None] * (2 + self.IDLE)

        for b in range(B):
            t = slice(b * TB, (b + 1) * TB)
            dve.wait_ge(self.g_ready, b // 2 + 1)
            dve.wait_ge(self.s_rows_added, NH * (b + 1))
            link(v.tensor_tensor(self.o[:, t, :], self.o[:, t, :], self.s_rows[:, t, :], ALU.mult))
            v.tensor_tensor(self.x_rows[:, t, :], self.x_rows[:, t, :], self.o[:, t, :], ALU.add).then_inc(
                self.x_ready, 1)
            if b < B - 1:
                yield


def clear_semaphores(nc):
    released = sorted(int(n) for n in nc.released_uncleared_semaphores)
    with nc.Block() as block:
        @block.gpsimd
        def _(pool):
            first = released[0]
            for n, following in zip(released, released[1:] + [None]):
                if following != n + 1:
                    pool.sem_clear(range(first, n + 1))
                    first = following


def program(nc, a, out):
    with ExitStack() as top:
        G = Scope(nc, top, "g")

        def dram(name, shape):
            return nc.dram_tensor(name, shape, F32, kind="Internal").ap()

        xn_dram = dram("xn_scratch", [P, NT, D])
        y1_dram = dram("y1_scratch", [HG, E0, C0, HID])
        r_dram = dram("r_scratch", [P, NT, HID])
        y2_dram = dram("y2_scratch", [HG, E0, C0, D])
        xn1_dram = dram("xn1_scratch", [P, NT, D])
        y3_dram = dram("y3_scratch", [E1, C1, D])

        outputs_stored = G.sem("outputs_stored")
        w = {}

        def resident(scope, names):
            pairs = []
            for n in names:
                src = a[n]
                shape = list(src.shape)
                buf = scope.sb(n, [P] + shape[1:] if shape[0] == 1 else shape, src.dtype)
                whole = buf[tuple(slice(None) for _ in shape)]
                w[n] = whole
                flat = whole
                if shape[0] == 1:
                    if len(shape) == 3:
                        flat = whole.rearrange("p a b -> p (a b)")
                        src = src.rearrange("o a b -> o (a b)")
                    src = src.broadcast_to([P, src.shape[1]])
                pairs.append((flat, src))
            return pairs

        consts = resident(G, ["ident", "tri", "ones", "iota", "pcol", "group_base"])

        state = G.sb("state", [P, 3 * NT * D])
        rows, xn_rows, s_rows = (state[:, k * NT * D:(k + 1) * NT * D].rearrange("p (t d) -> p t d", d=D)
                                 for k in range(3))

        with ExitStack() as moe:
            F = Scope(nc, moe, "moe")
            r = Routing()
            r.tab = F.sb("tab", [C0, HG, E0], U32)
            r.back = F.sb("back", [P, 2, NT], U32)
            r.wk = F.sb("wk", [P, 2, NT])
            r.GT = F.sb("GT", [64 + E0, GT_BATCHES * L])
            fw = resident(F, ["wg0", "b1_experts", "ln_w", "ln_b"])
            H = Scope(nc, moe, "mamba")
            mw = resident(H, ["xproj_T", "dt_T", "dt_b", "A_log", "D", "sel"])
            zT = H.sb("zT", [P, 2, N_TOK])
            with ExitStack() as scan:
                xT = Scope(nc, scan, "scan").sb("xT", [P, 2, N_TOK])
                with ExitStack() as inp:
                    I = Scope(nc, inp, "inp")
                    iw = resident(I, ["in_T", "conv_rows", "conv_b"])
                    xnT = I.sb("xnT", [P, B, PAD])
                    layernorm_stage(nc, a["x"], xn_dram, rows, xn_rows, xnT, w["ident"], "ln0",
                                    consts + iw + mw + fw)
                    routing = routing_programs(nc, inp, w, r, xnT, w["wg0"],
                                               dict(E=E0, C=C0, groups=HG, LO=C0, HI=E0, masked=True, floor=1e-9,
                                                    gaps=(6, 6, 6, 3)), "r0", Arena(state[:, :]))
                    mamba_input_stage(nc, w, xnT, xT, zT, routing)
                experts = Moe0Experts(nc, scan, w, r, state[:, 0:Moe0Experts.WORDS], xn_dram,
                                      a["W1"], y1_dram, r_dram, a["W2"], y2_dram)
                scan_stage(nc, w, xT, zT, Arena(state[:, Moe0Experts.WORDS:]), experts)
            ow = resident(F, ["out_T", "w1_T", "b1", "w2_T", "b2", "norm1", "b2_experts", "ln_out_w", "ln_out_b"])
            ending = Moe0Output(nc, moe, w, r, y2_dram, xn_dram, xn_rows, s_rows, a["x"], rows, ow)
            mamba_output_stage(nc, w, zT, xn_rows, s_rows, ending)

        clear_semaphores(nc)
        with ExitStack() as l1:
            H = Scope(nc, l1, "l1")
            r = Routing()
            r.tab = H.sb("tab", [P, 1, E1 // 4], U32)
            r.back = H.sb("back", [P, 2, NT], U32)
            r.wk = H.sb("wk", [P, 2, NT])
            r.GT = None
            l1w = resident(H, ["wg1", "gamma", "ident_bf", "mask_bf"])
            with ExitStack() as rt:
                xnT = Scope(nc, rt, "rt1").sb("xnT", [P, B, PAD])
                layernorm_stage(nc, None, xn1_dram, rows, xn_rows, xnT, w["ident"], "ln1", l1w)
                routing = routing_programs(nc, rt, w, r, xnT, w["wg1"],
                                           dict(E=E1, C=C1, groups=1, LO=P, HI=E1 // 4, masked=False,
                                                floor=float(np.finfo(np.float32).eps), gaps=(0, 0, 0, 0)), "r1",
                                           Scope(nc, rt, "r1s"))
                run_alone(nc, rt, routing)
            w["qkv_dram"], w["wo_dram"] = a["qkv"], a["wo"]
            with ExitStack() as att:
                A_ = Scope(nc, att, "att")
                xaT = A_.sb("xaT", [P, B, L])
                M = A_.sb("M", [P, NH * D])
                N = A_.sb("N", [P, NH * D])
                attention_fold_stage(nc, w, xn_rows, xaT, M, N)
                experts = Moe1Experts(nc, att, w, r, xn1_dram, a["we"], y3_dram, xn_rows, s_rows, rows, out,
                                      outputs_stored)
                attention_stage(nc, w, xaT, M, N, s_rows, experts)


def laid_out(i):

    c = np.ascontiguousarray
    bf16 = np.dtype("bfloat16")

    def striped(b):
        rows = np.zeros((64 + E0, b.shape[1]), b.dtype)
        for k in range(3):
            rows[32 * k:32 * k + E0] = b
        return rows

    xp = i["L0_attn_x_proj_w"].T.reshape(HALF, P, DTR + 2 * DS).transpose(1, 0, 2)
    sel = np.zeros((96, 2 * DS, P), bf16)
    for row in range(96):
        sel[row, row % (2 * DS)] = 1
    qkv = i["L1_attn_w_qkv"].reshape(3 * NH, D, D).transpose(1, 0, 2)
    return {
        "x": c(i["L0_attn_Z"].reshape(NT, P, D).transpose(1, 0, 2)),
        "in_T": c(i["L0_attn_in_proj_w"].T),
        "conv_rows": c(i["L0_attn_conv_w"].T[None]),
        "conv_b": c(i["L0_attn_conv_b"].reshape(HALF, P).T),
        "xproj_T": c(np.concatenate([xp[:, :, DTR:]] * 3 + [xp[:, :, :DTR]], axis=2)),
        "dt_T": c(i["L0_attn_dt_proj_w"].T),
        "dt_b": c(i["L0_attn_dt_proj_b"].reshape(HALF, P).T),
        "A_log": c(i["L0_attn_A_log"].reshape(HALF, P, DS).transpose(1, 0, 2)),
        "D": c(i["L0_attn_D"].reshape(HALF, P).T),
        "out_T": c(i["L0_attn_out_proj_w"].T.reshape(HALF, P, D).transpose(1, 0, 2)),
        "w1_T": c(i["L0_attn_mlp_w1"].T),
        "b1": c(i["L0_attn_mlp_b1"].reshape(FC, P).T),
        "w2_T": c(i["L0_attn_mlp_w2"].T.reshape(FC, P, D).transpose(1, 0, 2)),
        "b2": c(i["L0_attn_mlp_b2"][None]),
        "norm1": c(i["L0_attn_norm1_w"][None]),
        "wg0": c(i["L0_ffn_Wg"]),
        "W1": c(i["L0_ffn_W1"]),
        "W2": c(i["L0_ffn_W2"]),
        "b1_experts": striped(i["L0_ffn_b1"]),
        "b2_experts": striped(i["L0_ffn_b2"]),
        "ln_w": c(i["L0_ffn_ln_hid_w"][None]),
        "ln_b": c(i["L0_ffn_ln_hid_b"][None]),
        "ln_out_w": c(i["L0_ffn_ln_out_w"][None]),
        "ln_out_b": c(i["L0_ffn_ln_out_b"][None]),
        "gamma": c(i["L1_attn_gamma"][:, None]),
        "qkv": c(qkv),
        "wo": c(i["L1_attn_w_out"].T.reshape(NH, D, D).transpose(1, 0, 2)),
        "wg1": c(i["L1_ffn_wg"]),
        "we": c(i["L1_ffn_we"]),
        "ident": np.eye(P, dtype=np.float32),
        "ident_bf": np.eye(P, dtype=np.float32).astype(bf16),
        "mask_bf": (np.triu(np.ones((P, P), np.float32), 1) * np.float32(-1e30)).astype(bf16),
        "tri": np.triu(np.ones((P, P), np.float32), 1).astype(bf16),
        "ones": np.ones((P, P), bf16),
        "iota": np.tile(np.arange(P, dtype=np.float32), (P, 1)),
        "pcol": np.arange(P, dtype=np.float32)[:, None].copy(),
        "group_base": np.tile(np.arange(HG, dtype=np.float32) * (E0 * C0), (P, 1)),
        "sel": c(sel.reshape(96, 2 * DS * P)),
    }


def kernel(**inputs):
    import concourse.bacc as bacc
    from concourse.bass_utils import run_bass_kernel_spmd

    nc = bacc.Bacc("TRN2", target_bir_lowering=False, num_devices=1)
    arrays = laid_out({n: np.asarray(v) for n, v in inputs.items()})
    a = {n: nc.dram_tensor(n, v.shape, mybir.dt.from_np(v.dtype), kind="ExternalInput").ap() for n, v in arrays.items()}
    out = nc.dram_tensor("out", (P, NT, D), F32, kind="ExternalOutput").ap()
    program(nc, a, out)
    r = run_bass_kernel_spmd(nc, [arrays], core_ids=[0])
    got = r.results[0]["out"]
    return np.ascontiguousarray(got.transpose(1, 0, 2)).reshape(B, L, D)
```
